# Optimizing a Trainium2 kernel written in Bass

```python
import numpy as np
import jax
import jax.numpy as jnp

def _softmax(x, axis=-1):
    return jax.nn.softmax(x, axis=axis)

def _gelu(x):
    return jax.nn.gelu(x, approximate=True)

def _silu(x):
    return jax.nn.silu(x)

def _sigmoid(x):
    return jax.nn.sigmoid(x)

def _layernorm(x, axis=-1, eps=1e-05):
    m = jnp.mean(x, axis=axis, keepdims=True)
    v = jnp.var(x, axis=axis, keepdims=True)
    return (x - m) / jnp.sqrt(v + eps)

def _scatter_add(tgt, idx, src, axis=0):
    return tgt.at[idx].add(src)

def _segment_sum(src, seg, n):
    return jax.ops.segment_sum(src, seg, n)
kernel_name = 'mk_xattn_ffn_d2_seqx_r4_87c2b9'

def setup_inputs(seed: int=0):
    np.random.seed(seed)
    _w = jnp.asarray

    def _rec_inputs():
        import jax
        import jax.numpy as jnp
        _rk = jax.random.key(seed)
        x = -0.000125 + 0.9999 * jax.random.normal(jax.random.fold_in(_rk, 1), (16, 128, 256), jnp.float32)
        _lenS = 128 - jax.random.randint(jax.random.fold_in(_rk, 7), (16,), 0, max(1, 128 // 4) + 1, jnp.int32)
        _lenS2 = 128 - jax.random.randint(jax.random.fold_in(_rk, 8), (16,), 0, max(1, 128 // 4) + 1, jnp.int32)
        _ctx_1024P = jax.random.normal(jax.random.fold_in(_rk, 11), (16, 16, 256), jnp.float32)
        _ctx_1024c = jax.random.dirichlet(jax.random.fold_in(_rk, 511), 0.3 * jnp.ones((16,), jnp.float32), (16, 128))
        _ctx_1024t = jnp.einsum('bsk,bkd->bsd', _ctx_1024c, _ctx_1024P)
        _ctx_1024t = _ctx_1024t * jax.lax.rsqrt(jnp.mean(jnp.square(_ctx_1024t)) + 1e-12) * 0.953939
        ctx_1024 = -1.52775e-05 + 0.999936 * (_ctx_1024t + 0.3 * jax.random.normal(jax.random.fold_in(_rk, 611), (16, 128, 256), jnp.float32))
        return (x, ctx_1024)
    x, ctx_1024 = _rec_inputs()

    def _L0_xattn_setup():
        import jax, jax.numpy as jnp
        import numpy as np
        D_MODEL = 256
        HEAD_SIZE = 256
        CONTEXT_SIZE = 128
        key = jax.random.key(seed)
        kq, kk, kv, kwq, kwk, kwv = jax.random.split(key, 6)
        B, S = (64, 128)
        scale = 1.0 / np.sqrt(D_MODEL)
        return {'query': jax.random.normal(kq, (B, S, D_MODEL), dtype=jnp.float32), 'key': jax.random.normal(kk, (B, S, D_MODEL), dtype=jnp.float32), 'value': jax.random.normal(kv, (B, S, D_MODEL), dtype=jnp.float32), 'w_q': jax.random.normal(kwq, (D_MODEL, HEAD_SIZE), dtype=jnp.float32) * scale, 'w_k': jax.random.normal(kwk, (D_MODEL, HEAD_SIZE), dtype=jnp.float32) * scale, 'w_v': jax.random.normal(kwv, (D_MODEL, HEAD_SIZE), dtype=jnp.float32) * scale, 'mask': 1}
    _L0_xattn_all = _L0_xattn_setup()
    _L0_xattn_in = {k: v for k, v in _L0_xattn_all.items() if k in ('w_q', 'w_k', 'w_v')}
    del _L0_xattn_all

    def _L0_ffn_setup():
        import jax, jax.numpy as jnp
        import numpy as np
        TOP_K = 2
        key = jax.random.key(seed)
        k1, k2, k3, k4 = jax.random.split(key, 4)
        B, T, D, H, E = (2, 512, 256, 512, 8)
        x = jax.random.normal(k1, (B, T, D), dtype=jnp.float32)
        w12 = jax.random.normal(k2, (E, 2 * H, D), dtype=jnp.float32) * D ** (-0.5)
        w3 = jax.random.normal(k3, (E, D, H), dtype=jnp.float32) * H ** (-0.5)
        gate_w = jax.random.normal(k4, (E, D), dtype=jnp.float32) * D ** (-0.5)
        return {'x': x, 'w12': w12, 'w3': w3, 'gate_w': gate_w}
    _L0_ffn_all = _L0_ffn_setup()
    _L0_ffn_in = {k: v for k, v in _L0_ffn_all.items() if k in ('w12', 'w3', 'gate_w')}
    del _L0_ffn_all

    def _L1_xattn_setup():
        import jax, jax.numpy as jnp
        import numpy as np
        N_HEADS = 16
        D_EMBED = 256
        D_HEAD = D_EMBED // N_HEADS
        B, S = (2, 512)
        key = jax.random.key(seed)
        ks = jax.random.split(key, 6)
        k = jax.random.normal(ks[0], (B, S, D_EMBED), dtype=jnp.float32)
        q = jax.random.normal(ks[1], (B, S, D_EMBED), dtype=jnp.float32)
        v = jax.random.normal(ks[2], (B, S, D_EMBED), dtype=jnp.float32)
        scale = 1.0 / np.sqrt(D_HEAD)
        Wk = jax.random.normal(ks[3], (D_HEAD, D_HEAD), dtype=jnp.float32) * scale
        Wq = jax.random.normal(ks[4], (D_HEAD, D_HEAD), dtype=jnp.float32) * scale
        Wv = jax.random.normal(ks[5], (D_HEAD, D_HEAD), dtype=jnp.float32) * scale
        return {'k': k, 'q': q, 'v': v, 'Wk': Wk, 'Wq': Wq, 'Wv': Wv}
    _L1_xattn_all = _L1_xattn_setup()
    _L1_xattn_in = {k: v for k, v in _L1_xattn_all.items() if k in ('Wk', 'Wq', 'Wv')}
    del _L1_xattn_all

    def _L1_ffn_setup():
        import jax, jax.numpy as jnp
        import numpy as np
        QMAX = 127.0

        def _ste_round(v):
            return v + jax.lax.stop_gradient(jnp.round(v) - v)

        def _act_fake_quant(x, clip_factor):
            scale = jax.nn.sigmoid(clip_factor) * jnp.max(jnp.abs(x)) / QMAX
            return jnp.clip(_ste_round(x / scale), -QMAX - 1.0, QMAX) * scale

        def _weight_fake_quant(w):
            scale = jnp.max(jnp.abs(w), axis=1, keepdims=True) / QMAX
            return jnp.clip(_ste_round(w / scale), -QMAX - 1.0, QMAX) * scale
        key = jax.random.key(seed)
        k1, k2, k3, k4 = jax.random.split(key, 4)
        B, S, H, I = (8, 2048, 256, 704)
        return {'x': jax.random.normal(k1, (B, S, H), dtype=jnp.float32), 'clip_x': jnp.full((1,), 4.0, dtype=jnp.float32), 'clip_down': jnp.full((1,), 4.0, dtype=jnp.float32), 'w_gate': jax.random.normal(k2, (I, H), dtype=jnp.float32) * 0.02, 'w_up': jax.random.normal(k3, (I, H), dtype=jnp.float32) * 0.02, 'w_down': jax.random.normal(k4, (H, I), dtype=jnp.float32) * 0.02}
    _L1_ffn_all = _L1_ffn_setup()
    _L1_ffn_in = {k: v for k, v in _L1_ffn_all.items() if k in ('clip_x', 'clip_down', 'w_gate', 'w_up', 'w_down')}
    del _L1_ffn_all
    return {'x': x, 'ctx_1024': ctx_1024, 'L0_xattn_w_q': _L0_xattn_in['w_q'], 'L0_xattn_w_k': _L0_xattn_in['w_k'], 'L0_xattn_w_v': _L0_xattn_in['w_v'], 'L0_ffn_w12': _L0_ffn_in['w12'], 'L0_ffn_w3': _L0_ffn_in['w3'], 'L0_ffn_gate_w': _L0_ffn_in['gate_w'], 'L1_xattn_Wk': _L1_xattn_in['Wk'], 'L1_xattn_Wq': _L1_xattn_in['Wq'], 'L1_xattn_Wv': _L1_xattn_in['Wv'], 'L1_ffn_clip_x': _L1_ffn_in['clip_x'], 'L1_ffn_clip_down': _L1_ffn_in['clip_down'], 'L1_ffn_w_gate': _L1_ffn_in['w_gate'], 'L1_ffn_w_up': _L1_ffn_in['w_up'], 'L1_ffn_w_down': _L1_ffn_in['w_down']}

def reference(x, ctx_1024, L0_xattn_w_q, L0_xattn_w_k, L0_xattn_w_v, L0_ffn_w12, L0_ffn_w3, L0_ffn_gate_w, L1_xattn_Wk, L1_xattn_Wq, L1_xattn_Wv, L1_ffn_clip_x, L1_ffn_clip_down, L1_ffn_w_gate, L1_ffn_w_up, L1_ffn_w_down):
    import jax
    import jax.numpy as jnp

    def _L0_xattn_ref(query, key, value, w_q, w_k, w_v, mask):
        import jax, jax.numpy as jnp
        import numpy as np
        D_MODEL = 256
        HEAD_SIZE = 256
        CONTEXT_SIZE = 128
        q = jnp.einsum('bsd,dh->bsh', query, w_q)
        k = jnp.einsum('bsd,dh->bsh', key, w_k)
        v = jnp.einsum('bsd,dh->bsh', value, w_v)
        scale = 1.0 / np.sqrt(query.shape[-1]).astype(np.float32)
        scores = jnp.einsum('bqh,bkh->bqk', q, k) * scale
        if mask:
            S = scores.shape[1]
            causal = jnp.tril(jnp.ones((S, S), dtype=bool))
            scores = jnp.where(causal, scores, -jnp.inf)
        attn = jax.nn.softmax(scores, axis=-1)
        out = jnp.einsum('bqk,bkh->bqh', attn, v)
        return out

    def _L0_ffn_ref(x, w12, w3, gate_w):
        import jax, jax.numpy as jnp
        import numpy as np
        TOP_K = 2
        E = gate_w.shape[0]
        H = w3.shape[-1]
        scores = jnp.einsum('btd,ed->bte', x, gate_w)
        topk_scores, topk_idx = jax.lax.top_k(scores, TOP_K)
        topk_probs = jax.nn.softmax(topk_scores, axis=-1)
        total_probs = jnp.sum(jax.nn.one_hot(topk_idx, E, dtype=topk_probs.dtype) * topk_probs[..., None], axis=-2)
        h12 = jnp.einsum('btd,ehd->bteh', x, w12)
        h1, h2 = (h12[..., :H], h12[..., H:])
        hidden = jax.nn.silu(h1) * h2
        expert_out = jnp.einsum('bteh,edh->bted', hidden, w3)
        y = jnp.sum(total_probs[..., None] * expert_out, axis=-2)
        return y

    def _L1_xattn_ref(k, q, v, Wk, Wq, Wv):
        import jax, jax.numpy as jnp
        import numpy as np
        N_HEADS = 16
        D_EMBED = 256
        D_HEAD = D_EMBED // N_HEADS
        B, S = (2, 512)
        b, s, _ = k.shape
        kh = k.reshape(b, s, N_HEADS, D_HEAD)
        qh = q.reshape(b, s, N_HEADS, D_HEAD)
        vh = v.reshape(b, s, N_HEADS, D_HEAD)
        kh = jnp.einsum('bshd,ed->bshe', kh, Wk)
        qh = jnp.einsum('bshd,ed->bshe', qh, Wq)
        vh = jnp.einsum('bshd,ed->bshe', vh, Wv)
        scores = jnp.einsum('bqhd,bkhd->bhqk', qh, kh) / np.sqrt(D_HEAD).astype(np.float32)
        attn = jax.nn.softmax(scores, axis=-1)
        out = jnp.einsum('bhqk,bkhd->bqhd', attn, vh)
        return out.reshape(b, s, D_EMBED)

    def _L1_ffn_ref(x, clip_x, clip_down, w_gate, w_up, w_down):
        import jax, jax.numpy as jnp
        import numpy as np
        QMAX = 127.0

        def _ste_round(v):
            return v + jax.lax.stop_gradient(jnp.round(v) - v)

        def _act_fake_quant(x, clip_factor):
            scale = jax.nn.sigmoid(clip_factor) * jnp.max(jnp.abs(x)) / QMAX
            return jnp.clip(_ste_round(x / scale), -QMAX - 1.0, QMAX) * scale

        def _weight_fake_quant(w):
            scale = jnp.max(jnp.abs(w), axis=1, keepdims=True) / QMAX
            return jnp.clip(_ste_round(w / scale), -QMAX - 1.0, QMAX) * scale
        xq = _act_fake_quant(x, clip_x[0])
        gate = jnp.einsum('bsh,ih->bsi', xq, _weight_fake_quant(w_gate))
        up = jnp.einsum('bsh,ih->bsi', xq, _weight_fake_quant(w_up))
        h = _act_fake_quant(jax.nn.silu(gate) * up, clip_down[0])
        return jnp.einsum('bsi,hi->bsh', h, _weight_fake_quant(w_down))
    x = x + _L0_xattn_ref(_layernorm(x, axis=-1), ctx_1024, ctx_1024, L0_xattn_w_q, L0_xattn_w_k, L0_xattn_w_v, 1)
    x = x + _L0_ffn_ref(_layernorm(x, axis=-1), L0_ffn_w12, L0_ffn_w3, L0_ffn_gate_w)
    x = x + _L1_xattn_ref(ctx_1024, _layernorm(x, axis=-1), ctx_1024, L1_xattn_Wk, L1_xattn_Wq, L1_xattn_Wv)
    x = x + _L1_ffn_ref(_layernorm(x, axis=-1), L1_ffn_clip_x, L1_ffn_clip_down, L1_ffn_w_gate, L1_ffn_w_up, L1_ffn_w_down)
    return x

_drawn_inputs = setup_inputs


def setup_inputs(seed=0):
    import zlib

    import numpy as np

    out = dict(_drawn_inputs(seed))
    spreads = {}
    factors = {}
    for name, (base, spread) in spreads.items():
        noise = np.random.default_rng([zlib.crc32(name.encode()), seed]).standard_normal(out[name].shape)
        drawn = base * np.exp(spread * noise) if base else spread * noise
        out[name] = jnp.asarray(drawn.astype(out[name].dtype))
    for name, factor in factors.items():
        out[name] = (out[name] * factor).astype(out[name].dtype)
    return out
```

```python
import concourse.bass as bass
from concourse import mybir
from contextlib import ExitStack


class Tile:

    def __init__(self, t, parity, half):
        self.t, self.p, self.half = t, parity, half


def steps(eng, count, stages, peel=2):
    lead = max(a for a, _ in stages)
    end = (count - lead) // 2 * 2

    def straight(first, last):
        for t in range(first, last):
            for ahead, step in stages:
                if 0 <= t + ahead < count:
                    step(Tile(t + ahead, (t + ahead) % 2, (t + ahead) // 2))

    straight(-lead, peel)
    with eng.Fori(peel // 2, end // 2) as i:
        for p in range(2):
            for ahead, step in stages:
                n = p + ahead
                step(Tile(i * 2 + n, n % 2, i + n // 2))
    straight(end, count)


def each(eng, count, body):
    body(0)
    with eng.Fori(1, count) as i:
        body(i)


def at_least(eng, sem, value):
    if not isinstance(value, int) or value > 0:
        eng.wait_ge(sem, value)


def block_program(nc, x, ctx, wq0, wk0, wv0, w12, w3, gate_w, Wk1, Wq1, Wv1,
                  clip_x, clip_down, w_gate, w_up, w_down, out):
    f32, f16, bf16 = mybir.dt.float32, mybir.dt.float16, mybir.dt.bfloat16
    ALU, ACT, AX = mybir.AluOpType, mybir.ActivationFunctionType, mybir.AxisListType

    REDUCE_MAX = bass.bass_isa.ReduceOp.max

    P = 128
    T, S, D = x.shape
    DC = D // P
    E, H2, _ = w12.shape
    H = H2 // 2
    HC = H // P
    DH = Wk1.shape[0]
    NH = D // DH
    I = w_gate.shape[0]
    IC = -(-I // P)
    IROWS = [min(P, I - c * P) for c in range(IC)]
    BLK = 512
    NB = T * S // BLK
    EPS = 1e-5
    NEG = -1e30
    QMAX = 127.0
    MAGIC = 1.5 * 2.0 ** 23
    WS = 64.0
    SCALE0 = float(D) ** -0.5
    SCALE1 = float(DH) ** -0.5

    st = ExitStack()
    with st:
        def sb(name, shape, dt=f32):
            return st.enter_context(nc.sbuf_tensor(name, shape, dt))

        def sem(name):
            return st.enter_context(nc.semaphore(name))

        hs = sb("hs", [P, IC, T * S])
        hs_flat = hs[:, :, :].rearrange("p c n -> p (c n)")

        def within(at, words, dt, pattern, **sizes):
            v = hs_flat[:, at:at + words]
            return (v if dt == f32 else v.bitcast(dt)).rearrange(pattern, **sizes)

        xs = sb("xs", [P, T, D])
        stat = sb("stat", [P, T, 6])
        ln = sb("ln", [P, 8, T])
        mean, var_eps, root, rstd = ln[:, 0, :], ln[:, 1, :], ln[:, 2, :], ln[:, 3, :]
        ln_a, ln_b, ln_c = ln[:, 4, :], ln[:, 5, :], ln[:, 6, :]
        ident = sb("ident", [P, P])
        ident_b = sb("ident_b", [P, P], bf16)
        ones = sb("ones", [P, P])
        causal = sb("causal", [P, P])
        key8 = sb("key8", [P, T, E])
        zero1 = sb("zero1", [P, 1])
        wq = sb("wq", [P, DC, D])
        wk = sb("wk", [P, DC, D])
        wv = sb("wv", [P, DC, D])
        bdk = sb("bdk", [P, P])
        bdv = sb("bdv", [P, P])
        bdq = sb("bdq", [P, P])
        bdq2 = sb("bdq2", [P, 2, P])
        ctx_in = sb("ctx_in", [P, 2, D])
        xn = sb("xn", [P, 2, D])
        xT = sb("xT", [P, 2, 2 * D])
        qk = sb("qk", [P, 2, 2 * D])
        v0 = sb("v0", [P, 2, D])
        sc = sb("sc", [P, 2, P])
        pr = sb("pr", [P, 2, P])
        prT = sb("prT", [P, 2, P])
        nmax = sb("nmax", [P, 2])
        psum_row = sb("psum_row", [P, 2])
        prcp = sb("prcp", [P, 2])
        k1T = sb("k1T", [P, DC, T * S])
        v1 = sb("v1", [P, T, NH, DH + 1])
        gwT = sb("gwT", [P, DC, E])
        xh = within(0, DC * T * S // 2, f16, "p (c n) -> p c n", c=DC)
        xl = within(2048, DC * T * S // 2, f16, "p (c n) -> p c n", c=DC)
        rsc = sb("rsc", [P, T, E])
        rt = sb("rt", [P, 4, T, E])
        rs = sb("rs", [P, 8, T])
        pw = sb("pw", [P, T, E])
        w12r = sb("w12r", [P, H2 // P, D])
        w3r = sb("w3r", [P, DC, H])
        w12h = within(4096, DC * H2 // 2, f16, "p (c n) -> p c n", c=DC)
        w12l = within(5120, DC * H2 // 2, f16, "p (c n) -> p c n", c=DC)
        w3h = within(6144, HC * D // 2, f16, "p (c n) -> p c n", c=HC)
        w3l = within(6656, HC * D // 2, f16, "p (c n) -> p c n", c=HC)
        sil = sb("sil", [P, 2, BLK])
        hid = sb("hid", [P, 2, HC * P])
        hh = sb("hh", [P, 2, HC * P], f16)
        hl = sb("hl", [P, 2, HC * P], f16)
        q1 = sb("q1", [P, 2, 2, DC, P])
        k1s = sb("k1s", [P, 2, DC, P])
        sc1 = sb("sc1", [P, 2, 4 * P])
        pr1 = sb("pr1", [P, 2, 4 * P])
        pT1 = sb("pT1", [P, 2, 4 * P])
        nm1 = sb("nm1", [P, 2, 4])
        rc1 = sb("rc1", [P, NH])
        o1 = sb("o1", [P, NH, DH])
        wraw = within(0, 2 * IC * D, f32, "p (w c n) -> p w c n", w=2, c=IC)
        wdraw = within(2 * IC * D, DC * I, f32, "p (c n) -> p c n", c=DC)
        wqb = within(2 * IC * D + DC * I, IC * D, bf16, "p (w c n) -> p w c n", w=2, c=IC)
        wdqb = within(3 * IC * D + DC * I, DC * I // 2, bf16, "p (c n) -> p c n", c=DC)
        wmax = sb("wmax", [P, 2 * IC + DC])
        wsc = sb("wsc", [P, 2 * IC + DC])
        wrc = sb("wrc", [P, 2 * IC + DC])
        wguT = sb("wguT", [P, 2, DC, IC * P], bf16)
        wdT = sb("wdT", [P, IC, D], bf16)
        diag = sb("diag", [P, DC, P])
        wdrow = sb("wdrow", [P, D])
        cdrow = sb("cdrow", [P, D])
        clips = sb("clips", [P, 2])
        sig = sb("sig", [P, 4, 2])
        zam = sb("zam", [P, T])
        am = sb("am", [P, 8])
        gu = sb("gu", [P, 2, IC])
        zqa = sb("zqa", [P, 2, D])
        zqb = sb("zqb", [P, 2, D], bf16)
        zqT = sb("zqT", [P, DC, T * S], bf16)
        ham = sb("ham", [P, IC, NB])
        hqa = sb("hqa", [P, 2, BLK])
        hq = sb("hq", [P, IC, BLK], bf16)
        oo = xT[:, :, 0:D]

        ps = st.enter_context(nc.psum_tensor("ps", [P, 8, 512], f32))

        def bank(n):
            return ps[:, n, :]

        x_loaded = sem("x_loaded")
        w_loaded = sem("w_loaded")
        bd_loaded = sem("bd_loaded")
        l1w_loaded = sem("l1w_loaded")
        ctx_loaded = [sem("ctx_loaded0"), sem("ctx_loaded1")]
        const_ready = sem("const_ready")
        pool_step = sem("pool_step")
        bd_zero = sem("bd_zero")
        dchain = sem("dchain")
        setup_done = sem("setup_done")
        bdq2_ready = sem("bdq2_ready")
        sig_exp = sem("sig_exp")
        sig_one = sem("sig_one")
        l1q_ready = sem("l1q_ready")
        l1t_done = sem("l1t_done")
        l1t_copied = sem("l1t_copied")
        ln_ve = sem("ln_ve")
        ln_root = sem("ln_root")
        a_xn, a_tr, a_trc, a_qk, a_qkc, a_v, a_vc, a_k1c = [
            sem(n) for n in ("a_xn", "a_tr", "a_trc", "a_qk", "a_qkc", "a_v", "a_vc", "a_k1c")]
        a_s, a_sm, a_e, a_pt, a_ptc, a_o, a_fin, a_lk = [
            sem(n) for n in ("a_s", "a_sm", "a_e", "a_pt", "a_ptc", "a_o", "a_fin", "a_lk")]
        b_xn, b_tr, b_hi, b_f, b_lo, b_r, b_rc = [
            sem(n) for n in ("b_xn", "b_tr", "b_hi", "b_f", "b_lo", "b_r", "b_rc")]
        r_d, r_e = sem("r_d"), sem("r_e")
        w_in, w_tr, w_hi, w_lo = [sem(n) for n in ("w_in", "w_tr", "w_hi", "w_lo")]
        m_u, m_s, m_h, m_hh, m_hl, m_y, m_acc = [
            sem(n) for n in ("m_u", "m_s", "m_h", "m_hh", "m_hl", "m_y", "m_acc")]
        st_done = sem("st_done")
        c_xn, c_tr, c_trc, c_q, c_qc, c_k = [
            sem(n) for n in ("c_xn", "c_tr", "c_trc", "c_q", "c_qc", "c_k")]
        c_s, c_nm, c_sm, c_e, c_t, c_tc, c_v, c_fin, c_lk = [
            sem(n) for n in ("c_s", "c_nm", "c_sm", "c_e", "c_t", "c_tc", "c_v", "c_fin", "c_lk")]
        d_z, d_am, d_amr, d_sc, d_lk, d_q, d_qb, d_tr, d_trc = [
            sem(n) for n in ("d_z", "d_am", "d_amr", "d_sc", "d_lk", "d_q", "d_qb", "d_tr", "d_trc")]
        g_p, g_s, g_h, g_am = [sem(n) for n in ("g_p", "g_s", "g_h", "g_am")]
        e_am, e_amr, e_sc, e_a, e_c, e_q, e_y, e_o, e_lk, e_out0, e_out1 = [
            sem(n) for n in ("e_am", "e_amr", "e_sc", "e_a", "e_c", "e_q", "e_y", "e_o", "e_lk",
                             "e_out0", "e_out1")]
        e_out = [e_out0, e_out1]
        st0, st2, a_f1, a_f2, c_f1, c_f2, c_f3, e_f = [
            sem(n) for n in ("st0", "st2", "a_f1", "a_f2", "c_f1", "c_f2", "c_f3", "e_f")]

        NBD = P // DH
        NW = 2 * IC + DC

        def cols(t):
            return bass.ts(t, P)

        block = st.enter_context(nc.Block())

        @block.sync
        def _(sp):
            x_v = x.rearrange("b s d -> s b d")
            sp.dma_start(xs[:, 0:T // 2, :], x_v[:, 0:T // 2, :]).then_inc(x_loaded, 16)
            sp.dma_start(xs[:, T // 2:T, :], x_v[:, T // 2:T, :]).then_inc(x_loaded, 16)
            for dst, src in ((wq, wq0), (wk, wk0), (wv, wv0)):
                sp.dma_start(dst[:, :, :], src.rearrange("(c p) h -> p c h", p=P)).then_inc(w_loaded, 16)
            for n, src in enumerate((w_gate, w_up)):
                full = I // P
                sp.dma_start(wraw[:, n, 0:full, :],
                             src[0:full * P, :].rearrange("(c p) d -> p c d", p=P)).then_inc(l1w_loaded, 16)
                sp.dma_start(wraw[0:I - full * P, n, full, :], src[full * P:I, :]).then_inc(l1w_loaded, 16)
            sp.dma_start(wdraw[:, :, :], w_down.rearrange("(c p) i -> p c i", p=P)).then_inc(l1w_loaded, 16)

            def load_ctx(k):
                at_least(sp, a_tr, k.t - 1)
                sp.dma_start(ctx_in[:, k.p, :], ctx[k.t, :, :]).then_inc(ctx_loaded[k.p], 16)

            steps(sp, T, [(2, load_ctx)])

            def load_expert(e):
                at_least(sp, w_tr, e * 6)
                sp.dma_start(w12r[:, :, :], w12[e, :, :].rearrange("(c p) d -> p c d", p=P)).then_inc(w_in, 16)
                sp.dma_start(w3r[:, :, :], w3[e, :, :].rearrange("(c p) h -> p c h", p=P)).then_inc(w_in, 16)

            each(sp, E, load_expert)

            def store(k):
                sp.wait_ge(e_o, k.t + 1)
                sp.dma_start(out[k.t, :, :], oo[:, k.p, :]).then_inc(e_out[k.p], 16)

            steps(sp, T, [(0, store)])
            for p in range(2):
                sp.wait_ge(e_out[p], 16 * (T // 2))

        @block.gpsimd
        def _(pool):
            nc.gpsimd.memset(bdk[:, :], 0.0).then_inc(bd_zero, 1)
            nc.gpsimd.memset(bdv[:, :], 0.0).then_inc(bd_zero, 1)
            nc.gpsimd.memset(bdq[:, :], 0.0).then_inc(bd_zero, 1)
            nc.gpsimd.memset(ident[:, :], 0.0).then_inc(pool_step, 1)
            nc.gpsimd.memset(causal[:, :], 0.0).then_inc(pool_step, 1)
            nc.gpsimd.memset(v1[:, :, :, DH:DH + 1], 1.0)
            nc.gpsimd.memset(zero1[:, :], 0.0)
            nc.gpsimd.memset(ones[:, :], 1.0)
            for j in range(E):
                nc.gpsimd.memset(key8[:, :, j:j + 1], float(E - j))
            pool.wait_ge(pool_step, 2)
            nc.gpsimd.affine_select(out=ident[:, :], in_=ident[:, :], compare_op=ALU.not_equal, fill=1.0,
                                    base=0, pattern=[[-1, P]], channel_multiplier=1).then_inc(pool_step, 1)
            nc.gpsimd.affine_select(out=causal[:, :], in_=causal[:, :], compare_op=ALU.is_ge, fill=NEG,
                                    base=0, pattern=[[-1, P]], channel_multiplier=1).then_inc(pool_step, 1)
            pool.wait_ge(pool_step, 4)
            nc.gpsimd.tensor_copy(ident_b[:, :], ident[:, :]).then_inc(const_ready, 1)

            def key_copy(k):
                if not isinstance(k.t, int) or k.t >= 2:
                    pool.wait_ge(c_s, (k.t - 1) * 4)
                if isinstance(k.t, int) and k.t == 0:
                    pool.wait_ge(a_k1c, T)
                nc.gpsimd.tensor_copy(k1s[:, k.p, :, :], k1T[:, :, cols(k.t)]).then_inc(c_k, 1)

            steps(pool, T, [(2, key_copy)])

            pool.wait_ge(d_am, 1)
            nc.gpsimd.partition_all_reduce(am[:, 1:2], am[:, 0:1], P, REDUCE_MAX).then_inc(d_amr, 1)
            pool.wait_ge(e_am, 1)
            nc.gpsimd.partition_all_reduce(am[:, 5:6], am[:, 4:5], P, REDUCE_MAX).then_inc(e_amr, 1)

        @block.tensor
        def _(pe):
            mm = nc.tensor.matmul
            pe.wait_ge(const_ready, 1)
            n = 0
            for w in range(2):
                for dk in range(DC):
                    if n == 0:
                        pe.wait_ge(l1q_ready, 1)
                    if n >= 2:
                        pe.wait_ge(l1t_copied, n - 1)
                    bk = bank(n % 2).bitcast(bf16)
                    for c in range(IC):
                        last = nc.tensor.transpose(bk[:, c * P:c * P + IROWS[c]],
                                                   wqb[0:IROWS[c], w, c, dk * P:(dk + 1) * P],
                                                   ident_b[0:IROWS[c], 0:IROWS[c]])
                    last.then_inc(l1t_done, 1)
                    n += 1
            for half in range(2):
                pe.wait_ge(l1t_copied, n - 1)
                bk = bank(n % 2).bitcast(bf16)
                for c in range(half * IC // 2, (half + 1) * IC // 2):
                    for dk in range(DC):
                        o = (c - half * IC // 2) * D + dk * P
                        last = nc.tensor.transpose(bk[0:IROWS[c], o:o + P],
                                                   wdqb[:, dk, c * P:c * P + IROWS[c]], ident_b[:, :])
                last.then_inc(l1t_done, 1)
                n += 1
            pe.wait_ge(l1t_copied, n)
            for dk in range(DC):
                last = mm(bank(0)[:, dk * P:(dk + 1) * P], ones[:, :], diag[:, dk, :], start=True, stop=True)
            last.then_inc(l1t_done, 1)
            pe.wait_ge(l1t_copied, n + 1)
            pe.wait_ge(w_loaded, 48)
            pe.wait_ge(bdq2_ready, 1)

            def transposes(k):
                pe.wait_ge(a_xn, k.t + 1)
                pe.wait_ge(ctx_loaded[k.p], (k.half + 1) * 16)
                for c in range(DC):
                    nc.tensor.transpose(bank(k.p)[:, c * P:(c + 1) * P],
                                        xn[:, k.p, c * P:(c + 1) * P], ident[:, :])
                for c in range(DC):
                    last = nc.tensor.transpose(bank(k.p)[:, D + c * P:D + (c + 1) * P],
                                               ctx_in[:, k.p, c * P:(c + 1) * P], ident[:, :])
                last.then_inc(a_tr, 1)

            def projections(k):
                pe.wait_ge(a_trc, k.t + 1)
                at_least(pe, a_k1c, k.t - 1)
                at_least(pe, a_fin, k.t - 1)
                for src, w, o in ((0, wq, 0), (D, wk, D)):
                    for m in range(DC):
                        for c in range(DC):
                            last = mm(bank(2 + k.p)[:, o + m * P:o + (m + 1) * P],
                                      w[:, c, m * P:(m + 1) * P],
                                      xT[:, k.p, src + c * P:src + (c + 1) * P],
                                      start=(c == 0), stop=(c == DC - 1))
                last.then_inc(a_qk, 1)
                for c in range(DC):
                    mm(bank(4 + k.p)[:, 0:D], xT[:, k.p, D + c * P:D + (c + 1) * P], wv[:, c, :],
                       start=(c == 0), stop=(c == DC - 1))
                for c in range(DC):
                    mm(bank(4 + k.p)[:, D + c * P:D + (c + 1) * P],
                       xT[:, k.p, D + c * P:D + (c + 1) * P], bdv[:, :], start=True, stop=True)
                mm(bank(6 + k.p)[:, 0:D], bdk[:, :], xT[:, k.p, D:2 * D],
                   start=True, stop=True).then_inc(a_v, 1)

            def scores(k):
                pe.wait_ge(a_qkc, k.t + 1)
                pe.wait_ge(a_k1c, k.t + 1)
                for c in range(DC):
                    last = mm(bank(6 + k.p)[:, D:D + P], qk[:, k.p, c * P:(c + 1) * P],
                              qk[:, k.p, D + c * P:D + (c + 1) * P], start=(c == 0), stop=(c == DC - 1))
                last.then_inc(a_s, 1)

            def prob_transpose(k):
                pe.wait_ge(a_e, k.t + 1)
                nc.tensor.transpose(bank(6 + k.p)[:, D + P:D + 2 * P], pr[:, k.p, :],
                                    ident[:, :]).then_inc(a_pt, 1)

            def attend(k):
                pe.wait_ge(a_ptc, k.t + 1)
                pe.wait_ge(a_vc, k.t + 1)
                mm(bank(4 + k.p)[:, 0:D], prT[:, k.p, :], v0[:, k.p, :], start=True,
                   stop=True).then_inc(a_o, 1)

            steps(pe, T, [(0, scores), (1, projections), (0, prob_transpose), (2, transposes), (0, attend)])

            pe.wait_ge(a_fin, T)

            def b_transposes(k):
                pe.wait_ge(b_xn, k.t + 1)
                at_least(pe, b_lo, k.t - 1)
                for c in range(DC):
                    last = nc.tensor.transpose(bank(k.p)[:, c * P:(c + 1) * P],
                                               xn[:, k.p, c * P:(c + 1) * P], ident[:, :])
                last.then_inc(b_tr, 1)

            def router(k):
                pe.wait_ge(b_f, k.t + 1)
                at_least(pe, b_rc, k.t - 1)
                for c in range(DC):
                    last = mm(bank(2 + k.p)[:, 0:E], xT[:, k.p, c * P:(c + 1) * P], gwT[:, c, :],
                              start=(c == 0), stop=(c == DC - 1))
                last.then_inc(b_r, 1)

            steps(pe, T, [(1, b_transposes), (0, router)])

            with pe.Fori(0, E) as e:
                pe.wait_ge(w_in, (e + 1) * 32)
                for g in range(6):
                    if g >= 2:
                        pe.wait_ge(w_lo, e * 6 + (g - 1))
                    for j in range(4):
                        if g < 4:
                            dk, hc = g // 2, 4 * (g % 2) + j
                            src = w12r[:, hc, dk * P:(dk + 1) * P]
                        else:
                            hc, dk = 2 * (g - 4) + j // 2, j % 2
                            src = w3r[:, dk, hc * P:(hc + 1) * P]
                        last = nc.tensor.transpose(bank(6 + g % 2)[:, j * P:(j + 1) * P], src, ident[:, :])
                    last.then_inc(w_tr, 1)
                pe.wait_ge(w_lo, e * 6 + 6)

                def up(k):
                    for n in range(2 * HC):
                        dst = bank(2 * k.p + n // HC)[:, (n % HC) * P:(n % HC + 1) * P]
                        terms = [(w, v, c) for c in range(DC) for w, v in ((w12h, xh), (w12h, xl), (w12l, xh))]
                        for m, (w, v, c) in enumerate(terms):
                            last = mm(dst, w[:, c, n * P:(n + 1) * P], v[:, c, cols(k.t)],
                                      start=(m == 0), stop=(m == len(terms) - 1))
                    last.then_inc(m_u, 1)

                def down(k):
                    pe.wait_ge(m_hl, e * T + k.t + 1)
                    terms = [(a, w, c) for c in range(HC) for a, w in ((hh, w3h), (hh, w3l), (hl, w3h))]
                    for m, (a, w, c) in enumerate(terms):
                        last = mm(bank(4 + k.p)[:, 0:D], a[:, k.p, c * P:(c + 1) * P], w[:, c, :],
                                  start=(m == 0), stop=(m == len(terms) - 1))
                    last.then_inc(m_y, 1)

                steps(pe, T, [(1, up), (0, down)])

            def c_transposes(k):
                pe.wait_ge(c_xn, k.t + 1)
                for c in range(DC):
                    last = nc.tensor.transpose(bank(1)[:, c * P:(c + 1) * P],
                                               xn[:, 0, c * P:(c + 1) * P], ident[:, :])
                last.then_inc(c_tr, 1)

            def c_project(k):
                pe.wait_ge(c_trc, k.t + 1)
                for par in range(2):
                    last = mm(bank(1)[:, par * D:(par + 1) * D], bdq2[:, par, :], xT[:, 0, 0:D],
                              start=True, stop=True)
                last.then_inc(c_q, 1)

            def c_scores(s):
                def step(k):
                    if s == 0:
                        pe.wait_ge(c_qc, k.t + 1)
                        pe.wait_ge(c_k, k.t + 1)
                    for c in range(DC):
                        for par in range(2):
                            last = mm(bank(4 + s)[:, (2 * c + par) * P:(2 * c + par + 1) * P],
                                      q1[32 * s:32 * s + 32, k.p, par, c, :],
                                      k1s[32 * s:32 * s + 32, k.p, c, :], start=True, stop=True)
                    last.then_inc(c_s, 1)
                return step

            def c_ptrans(s):
                def step(k):
                    pe.wait_ge(c_e, k.t * 4 + (s + 1))
                    for j in range(4):
                        last = nc.tensor.transpose(bank(2 + s % 2)[:, j * P:(j + 1) * P],
                                                   pr1[:, s % 2, j * P:(j + 1) * P], ident[:, :])
                    last.then_inc(c_t, 1)
                return step

            def c_values(s):
                def step(k):
                    pe.wait_ge(c_tc, k.t * 4 + (s + 1))
                    if s == 0:
                        at_least(pe, c_fin, k.t)
                    for c in range(DC):
                        for par in range(2):
                            h = c * NBD + 2 * s + par
                            last = mm(bank(0)[:, h * (DH + 1):(h + 1) * (DH + 1)],
                                      pT1[:, s % 2, (2 * c + par) * P:(2 * c + par + 1) * P],
                                      v1[:, k.t, h, :], start=True, stop=True)
                    last.then_inc(c_v, 1)
                return step

            pe.wait_ge(st_done, 1)
            stages = []
            for s in range(4):
                stages.append(((s + 1) // 4, c_ptrans((s + 1) % 4)))
                stages.append(((s + 3) // 4, c_scores((s + 3) % 4)))
                if s == 1:
                    stages.append((2, c_transposes))
                if s == 2:
                    stages.append((2, c_project))
                stages.append((0, c_values(s)))
            steps(pe, T, stages)

            def d_transposes(k):
                pe.wait_ge(d_qb, k.t + 1)
                at_least(pe, d_trc, k.t - 1)
                bk = bank(k.p).bitcast(bf16)
                for c in range(DC):
                    last = nc.tensor.transpose(bk[:, c * P:(c + 1) * P], zqb[:, k.p, c * P:(c + 1) * P],
                                               ident_b[:, :])
                last.then_inc(d_tr, 1)

            pe.wait_ge(c_fin, T)
            steps(pe, T, [(0, d_transposes)])
            pe.wait_ge(d_trc, T)
            def gate_up(b):
                for c in range(IC):
                    r = IROWS[c]
                    if c < IC - 1:
                        back = c - 1 if c == IC - 2 else c - 2
                        at_least(pe, g_h, b * IC + back if back > 0 else b * IC)
                    for w in range(2):
                        for dk in range(DC):
                            last = mm(ps[0:r, 2 * (c % 3) + w, :], wguT[:, w, dk, c * P:c * P + r],
                                      zqT[:, dk, bass.ts(b, BLK)], start=(dk == 0), stop=(dk == DC - 1))
                    last.then_inc(g_p, 1)
            each(pe, NB, gate_up)
            pe.wait_ge(g_am, NB * IC)

            def last_down(b):
                pe.wait_ge(e_q, (b + 1) * IC)
                for j in range(BLK // P):
                    at_least(pe, e_f, b * 4 + (j - 1))
                    for c in range(IC):
                        r = IROWS[c]
                        last = mm(bank(6 + j % 2)[:, 0:D], hq[0:r, c, j * P:(j + 1) * P], wdT[0:r, c, :],
                                  start=(c == 0), stop=(c == IC - 1))
                    last.then_inc(e_y, 1)

            each(pe, NB, last_down)

        @block.scalar
        def _(act):
            def wt(w):
                return w.rearrange("e d -> d e")
            with nc.allow_non_contiguous_dma(reason="small transposed weights"):
                act.wait_ge(bd_zero, 3)
                for g in range(NBD):
                    for dst, src in ((bdk, Wk1), (bdv, Wv1), (bdq, Wq1)):
                        act.dma_start(dst[g * DH:(g + 1) * DH, g * DH:(g + 1) * DH],
                                      wt(src)).then_inc(bd_loaded, 16)
                for c in range(DC):
                    act.dma_start(gwT[:, c, :], wt(gate_w[:, c * P:(c + 1) * P])).then_inc(bd_loaded, 16)
                for n, src in enumerate((clip_x, clip_down)):
                    act.dma_start(clips[:, n:n + 1], src.rearrange("(a n) -> a n", a=1).to_broadcast([P, 1])
                                  ).then_inc(bd_loaded, 16)
            act.wait_ge(bd_loaded, 16 * (3 * NBD + DC + 2))
            act.activation(sig[:, 0, :], clips[:, :], ACT.Exp, scale=-1.0).then_inc(sig_exp, 1)
            n = 0
            for w in range(2):
                for dk in range(DC):
                    act.wait_ge(l1t_done, n + 1)
                    act.copy(wguT[:, w, dk, 0:(IC - 1) * P],
                             bank(n % 2).bitcast(bf16)[:, 0:(IC - 1) * P])
                    act.copy(wguT[:, w, dk, (IC - 1) * P:I],
                             bank(n % 2).bitcast(bf16)[:, (IC - 1) * P:I]).then_inc(l1t_copied, 1)
                    n += 1
            for half in range(2):
                act.wait_ge(l1t_done, n + 1)
                bk = bank(n % 2).bitcast(bf16)
                for c in range(half * IC // 2, (half + 1) * IC // 2):
                    o = (c - half * IC // 2) * D
                    last = act.copy(wdT[0:IROWS[c], c, :], bk[0:IROWS[c], o:o + D])
                last.then_inc(l1t_copied, 1)
                n += 1
            act.wait_ge(l1t_done, n + 1)
            act.copy(wdrow[:, :], bank(0)[:, 0:D]).then_inc(l1t_copied, 1)

            def roots(n):
                act.wait_ge(ln_ve, n + 1)
                act.activation(root, var_eps, ACT.Sqrt).then_inc(ln_root, 1)

            roots(0)

            def transposed(k):
                act.wait_ge(a_tr, k.t + 1)
                at_least(act, a_v, k.t - 1)
                act.copy(xT[:, k.p, :], bank(k.p)).then_inc(a_trc, 1)

            def qk_copy(k):
                act.wait_ge(a_qk, k.t + 1)
                act.copy(qk[:, k.p, :], bank(2 + k.p)).then_inc(a_qkc, 1)

            def v_copy(k):
                act.wait_ge(a_v, k.t + 1)
                act.copy(v0[:, k.p, :], bank(4 + k.p)[:, 0:D])
                act.copy(v1[:, k.t, :, 0:DH],
                         bank(4 + k.p)[:, D:2 * D].rearrange("p (h e) -> p h e", e=DH)).then_inc(a_vc, 1)

            def exps(k):
                act.wait_ge(a_sm, k.t + 1)
                act.activation(pr[:, k.p, :], sc[:, k.p, :], ACT.Exp, bias=nmax[:, k.p:k.p + 1],
                               accum_out=psum_row[:, k.p:k.p + 1]).then_inc(a_e, 1)

            def pt_copy(k):
                act.wait_ge(a_pt, k.t + 1)
                act.copy(prT[:, k.p, :], bank(6 + k.p)[:, D + P:D + 2 * P]).then_inc(a_ptc, 1)

            act.wait_ge(const_ready, 1)
            nc.scalar.preload_act_table(ACT.Exp)
            steps(act, T, [(0, exps), (1, qk_copy), (0, pt_copy), (2, transposed), (1, v_copy)])

            roots(1)

            nc.scalar.preload_act_table(ACT.Exp)

            def b_high(k):
                act.wait_ge(b_tr, k.t + 1)
                act.copy(xh[:, :, cols(k.t)],
                         bank(k.p)[:, 0:D].rearrange("p (c s) -> p c s", c=DC)).then_inc(b_hi, 1)
                at_least(act, b_r, k.t - 1)
                act.copy(xT[:, k.p, 0:D], bank(k.p)[:, 0:D]).then_inc(b_f, 1)

            steps(act, T, [(0, b_high)])
            act.wait_ge(r_d, 1)
            act.activation(rs[:, 2, :], rs[:, 3, :], ACT.Exp).then_inc(r_e, 1)

            nc.scalar.preload_act_table(ACT.Silu)
            with act.Fori(0, E) as e:
                for g in range(6):
                    act.wait_ge(w_tr, e * 6 + (g + 1))
                    if g < 4:
                        dst = w12h[:, g // 2, (g % 2) * 512:(g % 2 + 1) * 512]
                    else:
                        dst = w3h[:, 2 * (g - 4):2 * (g - 4) + 2, :]
                    act.mul(dst, bank(6 + g % 2) if g < 4 else bank(6 + g % 2).rearrange(
                        "p (c d) -> p c d", d=D), WS).then_inc(w_hi, 1)

                def silu(k):
                    act.wait_ge(m_u, e * T + k.t + 1)
                    act.activation(sil[:, k.p, :], bank(2 * k.p), ACT.Silu, scale=1.0 / WS).then_inc(m_s, 1)

                def high(k):
                    act.wait_ge(m_h, e * T + k.t + 1)
                    act.copy(hh[:, k.p, :], hid[:, k.p, :]).then_inc(m_hh, 1)

                steps(act, T, [(0, silu), (0, high)])

            roots(2)

            nc.scalar.preload_act_table(ACT.Exp)

            def c_xcopy(k):
                act.wait_ge(c_tr, k.t + 1)
                act.copy(xT[:, 0, 0:D], bank(1)[:, 0:D]).then_inc(c_trc, 1)

            def c_qcopy(k):
                act.wait_ge(c_q, k.t + 1)
                act.copy(q1[:, k.p, :, :, :].rearrange("p a c s -> p (a c s)"), bank(1)).then_inc(c_qc, 1)

            def c_exp(s):
                def step(k):
                    act.wait_ge(c_sm, k.t * 4 + (s + 1))
                    at_least(act, c_t, k.t * 4 + (s - 1))
                    act.activation(pr1[:, s % 2, :], sc1[:, s % 2, :], ACT.Exp).then_inc(c_e, 1)
                return step

            def c_ptcopy(s):
                def step(k):
                    act.wait_ge(c_t, k.t * 4 + (s + 1))
                    act.copy(pT1[:, s % 2, :], bank(2 + s % 2)).then_inc(c_tc, 1)
                return step

            stages = []
            for s in range(4):
                stages.append(((s + 1) // 4, c_ptcopy((s + 1) % 4)))
                stages.append(((s + 2) // 4, c_exp((s + 2) % 4)))
                if s == 1:
                    stages.append((2, c_xcopy))
                if s == 2:
                    stages.append((2, c_qcopy))
            steps(act, T, stages)

            roots(3)

            nc.scalar.preload_act_table(ACT.Silu)

            def z_int(k):
                act.wait_ge(d_q, k.t + 1)
                at_least(act, d_tr, k.t - 1)
                act.activation(zqb[:, k.p, :], zqa[:, k.p, :], ACT.Copy, bias=-MAGIC).then_inc(d_qb, 1)

            def z_tcopy(k):
                act.wait_ge(d_tr, k.t + 1)
                act.copy(zqT[:, :, cols(k.t)],
                         bank(k.p).bitcast(bf16)[:, 0:D].rearrange("p (c s) -> p c s", c=DC)).then_inc(d_trc, 1)

            steps(act, T, [(1, z_int), (0, z_tcopy)])
            def gate_silu(b):
                for c in range(IC):
                    r = IROWS[c]
                    act.wait_ge(g_p, b * IC + (c + 1))
                    at_least(act, g_h, b * IC + (c - 1))
                    act.activation(sil[0:r, c % 2, :], ps[0:r, 2 * (c % 3), :], ACT.Silu,
                                   scale=gu[0:r, 0, c:c + 1]).then_inc(g_s, 1)
            each(act, NB, gate_silu)
            act.wait_ge(e_sc, 1)

            def hidden_scale(b):
                for c in range(IC):
                    r = IROWS[c]
                    at_least(act, e_q, b * IC + (c - 1))
                    act.activation(hqa[0:r, c % 2, :], hs[0:r, c, bass.ts(b, BLK)], ACT.Copy,
                                   bias=MAGIC, scale=am[0:r, 7:8]).then_inc(e_a, 1)

            each(act, NB, hidden_scale)

        @block.vector
        def _(dve):
            chain = [0]

            def link(ins):
                chain[0] += 1
                ins.then_inc(dchain, 1)
                dve.wait_ge(dchain, chain[0])

            ts, tt, stt = nc.vector.tensor_scalar, nc.vector.tensor_tensor, nc.vector.scalar_tensor_tensor

            dve.wait_ge(l1w_loaded, 16 * 5)
            dve.wait_ge(const_ready, 1)
            parts = []
            for w in range(2):
                for c in range(IC):
                    parts.append((wraw[0:IROWS[c], w, c, :], wqb[0:IROWS[c], w, c, :], IROWS[c], w * IC + c))
            for c in range(DC):
                parts.append((wdraw[:, c, :], wdqb[:, c, :], P, 2 * IC + c))
            link(nc.vector.memset(wmax[:, :], 1.0))
            for src, _, r, n in parts:
                last = nc.vector.tensor_reduce(wmax[0:r, n:n + 1], src, axis=AX.X, op=ALU.max,
                                               apply_absolute_value=True)
            link(last)
            link(ts(wsc[:, :], wmax[:, :], 1.0 / QMAX, None, ALU.mult))
            link(nc.vector.reciprocal(wrc[:, :], wsc[:, :]))
            for src, _, r, n in parts:
                last = ts(src, src, wrc[0:r, n:n + 1], MAGIC, ALU.mult, ALU.add)
            link(last)
            for src, _, r, n in parts:
                last = ts(src, src, MAGIC + QMAX, MAGIC - QMAX - 1.0, ALU.min, ALU.max)
            link(last)
            for src, dst, r, n in parts:
                nc.vector.tensor_scalar(dst, src, -MAGIC, None, ALU.add)
            for c in range(DC):
                last = ts(diag[:, c, :], ident[:, :], wsc[:, 2 * IC + c:2 * IC + c + 1], None, ALU.mult)
            last.then_inc(l1q_ready, 1)
            dve.wait_ge(bd_loaded, 16 * (3 * NBD + DC + 2))
            link(nc.vector.memset(bdq2[:, :, :], 0.0))
            for par in range(2):
                v = bdq2[:, par, :].rearrange("p (g a e) -> p g a e", a=2, e=DH)[:, :, par, :]
                u = bdq[:, :].rearrange("p (g a e) -> p g a e", a=2, e=DH)[:, :, par, :]
                last = ts(v, u, SCALE1, None, ALU.mult)
            last.then_inc(bdq2_ready, 1)
            dve.wait_ge(sig_exp, 1)
            link(ts(sig[:, 1, :], sig[:, 0, :], 1.0, None, ALU.add))
            link(nc.vector.reciprocal(sig[:, 2, :], sig[:, 1, :]))

            def statistics(sem_name):
                with dve.Fori(0, T) as t:
                    last = nc.vector.bn_stats(stat[:, t, :], xs[:, t, :])
                    last.then_inc(sem_name, 1)

            def rstds(n, sem_name, count):
                dve.wait_ge(sem_name, count)
                me, mo, ve, vo = stat[:, :, 1], stat[:, :, 4], stat[:, :, 2], stat[:, :, 5]
                link(tt(ln_a, me, mo, ALU.add))
                link(ts(mean, ln_a, 0.5, None, ALU.mult))
                link(tt(ln_b, me, mo, ALU.subtract))
                link(tt(ln_c, ln_b, ln_b, ALU.mult))
                link(tt(ln_a, ve, vo, ALU.add))
                link(ts(ln_b, ln_a, 1.0 / D, EPS, ALU.mult, ALU.add))
                stt(var_eps, ln_c, 0.25, ln_b, ALU.mult, ALU.add).then_inc(ln_ve, 1)
                dve.wait_ge(ln_root, n + 1)
                link(nc.vector.reciprocal(rstd, root))
                link(tt(ln_a, rstd, rstd, ALU.mult))
                link(tt(ln_b, ln_a, var_eps, ALU.mult))
                link(ts(ln_c, ln_b, -0.5, 1.5, ALU.mult, ALU.add))
                link(tt(rstd, rstd, ln_c, ALU.mult))

            def normalise(dst, k):
                return ts(dst, xs[:, k.t, :], mean[:, cols1(k.t)], rstd[:, cols1(k.t)],
                          ALU.subtract, ALU.mult)

            def cols1(t):
                return bass.ts(t, 1)

            dve.wait_ge(x_loaded, 32)
            statistics(st0)
            rstds(0, st0, T)

            def a_norm(k):
                at_least(dve, a_tr, k.t - 1)
                normalise(xn[:, k.p, :], k).then_inc(a_xn, 1)

            def a_mask(k):
                dve.wait_ge(a_s, k.t + 1)
                stt(sc[:, k.p, :], bank(6 + k.p)[:, D:D + P], SCALE0, causal[:, :], ALU.mult,
                    ALU.add).then_inc(a_lk, 1)
                dve.wait_ge(a_lk, k.t + 1)
                nc.vector.tensor_reduce(nmax[:, k.p:k.p + 1], sc[:, k.p, :], axis=AX.X, op=ALU.max,
                                        negate=True).then_inc(a_sm, 1)

            def a_keys(k):
                dve.wait_ge(a_v, k.t + 1)
                nc.vector.tensor_copy(k1T[:, :, cols(k.t)],
                                      bank(6 + k.p)[:, 0:D].rearrange("p (c s) -> p c s", c=DC)
                                      ).then_inc(a_k1c, 1)

            def a_finish(k):
                dve.wait_ge(a_o, k.t + 1)
                nc.vector.reciprocal(prcp[:, k.p:k.p + 1], psum_row[:, k.p:k.p + 1]).then_inc(a_f1, 1)
                dve.wait_ge(a_f1, k.t + 1)
                stt(xs[:, k.t, :], bank(4 + k.p)[:, 0:D], prcp[:, k.p:k.p + 1], xs[:, k.t, :],
                    ALU.mult, ALU.add).then_inc(a_f2, 1)
                dve.wait_ge(a_f2, k.t + 1)
                nc.vector.bn_stats(stat[:, k.t, :], xs[:, k.t, :]).then_inc(a_fin, 1)

            steps(dve, T, [(0, a_mask), (3, a_norm), (1, a_keys), (0, a_finish)])
            rstds(1, a_fin, T)

            def b_norm(k):
                at_least(dve, b_tr, k.t - 1)
                normalise(xn[:, k.p, :], k).then_inc(b_xn, 1)

            def b_route(k):
                dve.wait_ge(b_r, k.t + 1)
                nc.vector.tensor_copy(rsc[:, k.t, :], bank(2 + k.p)[:, 0:E]).then_inc(b_rc, 1)

            def b_low(k):
                dve.wait_ge(b_f, k.t + 1)
                tt(xl[:, :, cols(k.t)], bank(k.p)[:, 0:D].rearrange("p (c s) -> p c s", c=DC),
                   xh[:, :, cols(k.t)], ALU.subtract).then_inc(b_lo, 1)

            steps(dve, T, [(1, b_norm), (0, b_low), (0, b_route)])

            def wide(v):
                return v.unsqueeze(2).to_broadcast([P, T, E])

            dve.wait_ge(b_rc, T)
            top1, top2, e21, d21 = rs[:, 0, :], rs[:, 1, :], rs[:, 2, :], rs[:, 3, :]
            pick, den, p1, p2 = rs[:, 4, :], rs[:, 5, :], rs[:, 6, :], rs[:, 7, :]
            hit, one1, one2, rest = rt[:, 0, :, :], rt[:, 1, :, :], rt[:, 2, :, :], rt[:, 3, :, :]

            def first_of(scores_ap, top, one):
                link(nc.vector.tensor_reduce(top, scores_ap, axis=AX.X, op=ALU.max))
                link(tt(hit, scores_ap, wide(top), ALU.is_equal))
                link(tt(hit, hit, key8[:, :, :], ALU.mult))
                link(nc.vector.tensor_reduce(pick, hit, axis=AX.X, op=ALU.max))
                link(tt(one, key8[:, :, :], wide(pick), ALU.is_equal))

            first_of(rsc[:, :, :], top1, one1)
            link(stt(rest, one1, NEG, rsc[:, :, :], ALU.mult, ALU.add))
            first_of(rest, top2, one2)
            tt(d21, top2, top1, ALU.subtract).then_inc(r_d, 1)
            dve.wait_ge(r_e, 1)
            link(ts(den, e21, 1.0, None, ALU.add))
            link(nc.vector.reciprocal(p1, den))
            link(tt(p2, p1, e21, ALU.mult))
            link(tt(one1, one1, wide(p1), ALU.mult))
            link(tt(one2, one2, wide(p2), ALU.mult))
            link(tt(hit, one1, one2, ALU.add))
            link(ts(pw[:, :, :], hit, 1.0 / WS, None, ALU.mult))

            with dve.Fori(0, E) as e:
                for g in range(6):
                    dve.wait_ge(w_hi, e * 6 + (g + 1))
                    src = bank(6 + g % 2)
                    if g < 4:
                        hi = w12h[:, g // 2, (g % 2) * 512:(g % 2 + 1) * 512]
                        lo = w12l[:, g // 2, (g % 2) * 512:(g % 2 + 1) * 512]
                    else:
                        src = src.rearrange("p (c d) -> p c d", d=D)
                        hi = w3h[:, 2 * (g - 4):2 * (g - 4) + 2, :]
                        lo = w3l[:, 2 * (g - 4):2 * (g - 4) + 2, :]
                    stt(lo, src, WS, hi, ALU.mult, ALU.subtract).then_inc(w_lo, 1)

                def hidden(k):
                    dve.wait_ge(m_s, e * T + k.t + 1)
                    stt(hid[:, k.p, :], bank(2 * k.p + 1), 1.0 / WS, sil[:, k.p, :], ALU.mult,
                        ALU.mult).then_inc(m_h, 1)

                def low(k):
                    dve.wait_ge(m_hh, e * T + k.t + 1)
                    tt(hl[:, k.p, :], hid[:, k.p, :], hh[:, k.p, :], ALU.subtract).then_inc(m_hl, 1)

                def accumulate(k):
                    dve.wait_ge(m_y, e * T + k.t + 1)
                    stt(xs[:, k.t, :], bank(4 + k.p)[:, 0:D],
                        pw[:, :, :].rearrange("p t e -> p (t e)")[:, cols1(k.t * E + e)],
                        xs[:, k.t, :], ALU.mult, ALU.add).then_inc(m_acc, 1)

                steps(dve, T, [(1, hidden), (1, low), (0, accumulate)])

            dve.wait_ge(m_acc, E * T)
            statistics(st2)
            rstds(2, st2, T)
            nc.vector.memset(rc1[:, :], 0.0).then_inc(st_done, 1)

            def c_norm(k):
                at_least(dve, c_tr, k.t)
                normalise(xn[:, 0, :], k).then_inc(c_xn, 1)

            def c_shift(s):
                def step(k):
                    b4 = bank(4 + s).rearrange("p (h s) -> p h s", h=4)
                    o4 = sc1[:, s % 2, :].rearrange("p (h s) -> p h s", h=4)
                    dve.wait_ge(c_s, k.t * 4 + (s + 1))
                    at_least(dve, c_e, k.t * 4 + (s - 1))
                    nc.vector.tensor_reduce(nm1[:, s % 2, :], b4, axis=AX.X, op=ALU.max,
                                            negate=True).then_inc(c_nm, 1)
                    dve.wait_ge(c_nm, k.t * 4 + (s + 1))
                    tt(o4, b4, nm1[:, s % 2, :].unsqueeze(2).to_broadcast([P, 4, P]),
                       ALU.add).then_inc(c_sm, 1)
                return step

            def c_finish(k):
                dve.wait_ge(c_v, k.t * 4 + 4)
                o = bank(0)[:, 0:NH * (DH + 1)].rearrange("p (h e) -> p h e", e=DH + 1)
                nc.vector.reciprocal(rc1[:, :], o[:, :, DH]).then_inc(c_f1, 1)
                dve.wait_ge(c_f1, k.t + 1)
                tt(o1[:, :, :], o[:, :, 0:DH], rc1[:, :].unsqueeze(2).to_broadcast([P, NH, DH]),
                   ALU.mult).then_inc(c_f2, 1)
                dve.wait_ge(c_f2, k.t + 1)
                tt(xs[:, k.t, :], xs[:, k.t, :], o1[:, :, :].rearrange("p h e -> p (h e)"),
                   ALU.add).then_inc(c_f3, 1)
                dve.wait_ge(c_f3, k.t + 1)
                nc.vector.bn_stats(stat[:, k.t, :], xs[:, k.t, :]).then_inc(c_fin, 1)

            stages = []
            for s in range(4):
                if s == 0:
                    stages.append((2, c_norm))
                stages.append(((s + 3) // 4, c_shift((s + 3) % 4)))
            stages.append((0, c_finish))
            steps(dve, T, stages)
            rstds(3, c_fin, T)

            z = hs[:, 0:2, :].rearrange("p c n -> p (c n)").rearrange("p (t d) -> p t d", d=D)
            with dve.Fori(0, T) as t:
                ts(z[:, t, :], xs[:, t, :], mean[:, cols1(t)], rstd[:, cols1(t)], ALU.subtract,
                   ALU.mult).then_inc(d_z, 1)
                dve.wait_ge(d_z, t + 1)
                nc.vector.tensor_reduce(zam[:, cols1(t)], z[:, t, :], axis=AX.X, op=ALU.max,
                                        apply_absolute_value=True).then_inc(d_lk, 1)
            dve.wait_ge(d_lk, T)
            nc.vector.tensor_reduce(am[:, 0:1], zam[:, :], axis=AX.X, op=ALU.max).then_inc(d_am, 1)
            dve.wait_ge(d_amr, 1)
            link(ts(am[:, 2:3], am[:, 1:2], sig[:, 2, 0:1], 1.0 / QMAX, ALU.mult, ALU.mult))
            link(nc.vector.reciprocal(am[:, 3:4], am[:, 2:3]))
            link(ts(gu[:, :, :].rearrange("p w c -> p (w c)"), wsc[:, 0:2 * IC], am[:, 2:3], None, ALU.mult))

            def z_quant(k):
                at_least(dve, d_qb, k.t - 1)
                ts(zqa[:, k.p, :], z[:, k.t, :], am[:, 3:4], MAGIC, ALU.mult, ALU.add).then_inc(d_sc, 1)
                dve.wait_ge(d_sc, k.t + 1)
                ts(zqa[:, k.p, :], zqa[:, k.p, :], MAGIC + QMAX, MAGIC - QMAX - 1.0, ALU.min,
                   ALU.max).then_inc(d_q, 1)

            steps(dve, T, [(1, z_quant)])
            with dve.Fori(0, NB) as b:
                for c in range(IC):
                    r = IROWS[c]
                    dve.wait_ge(g_s, b * IC + (c + 1))
                    stt(hs[0:r, c, bass.ts(b, BLK)], ps[0:r, 2 * (c % 3) + 1, :], gu[0:r, 1, c:c + 1],
                        sil[0:r, c % 2, :], ALU.mult, ALU.mult).then_inc(g_h, 1)
                    dve.wait_ge(g_h, b * IC + (c + 1))
                    nc.vector.tensor_reduce(ham[0:r, c, bass.ts(b, 1)], hs[0:r, c, bass.ts(b, BLK)],
                                            axis=AX.X, op=ALU.max,
                                            apply_absolute_value=True).then_inc(g_am, 1)
            dve.wait_ge(g_am, NB * IC)
            nc.vector.memset(am[:, 4:5], 0.0).then_inc(e_lk, 1)
            link(nc.vector.tensor_reduce(zam[:, 0:IC - 1], ham[:, 0:IC - 1, :], axis=AX.X, op=ALU.max))
            link(nc.vector.memset(zam[:, IC - 1:IC], 0.0))
            link(nc.vector.tensor_reduce(zam[0:IROWS[-1], IC - 1:IC], ham[0:IROWS[-1], IC - 1, :],
                                         axis=AX.X, op=ALU.max))
            dve.wait_ge(e_lk, 1)
            nc.vector.tensor_reduce(am[:, 4:5], zam[:, 0:IC], axis=AX.X, op=ALU.max).then_inc(e_am, 1)
            dve.wait_ge(e_amr, 1)
            link(ts(am[:, 6:7], am[:, 5:6], sig[:, 2, 1:2], 1.0 / QMAX, ALU.mult, ALU.mult))
            nc.vector.reciprocal(am[:, 7:8], am[:, 6:7]).then_inc(e_sc, 1)
            link(ts(cdrow[:, :], wdrow[:, :], am[:, 6:7], None, ALU.mult))

            def last_quant(b):
                for c in range(IC):
                    r = IROWS[c]
                    dve.wait_ge(e_a, b * IC + (c + 1))
                    if c == 0:
                        at_least(dve, e_y, b * 4)
                    ts(hqa[0:r, c % 2, :], hqa[0:r, c % 2, :], MAGIC + QMAX, MAGIC - QMAX - 1.0, ALU.min,
                       ALU.max).then_inc(e_c, 1)
                    dve.wait_ge(e_c, b * IC + (c + 1))
                    ts(hq[0:r, c, :], hqa[0:r, c % 2, :], -MAGIC, None, ALU.add).then_inc(e_q, 1)
                for j in range(BLK // P):
                    p = j % 2
                    dve.wait_ge(e_y, b * 4 + (j + 1))
                    at_least(dve, e_out[p], b * 32 + (16 if j >= 2 else 0))
                    tt(oo[:, p, :], bank(6 + p)[:, 0:D], cdrow[:, :], ALU.mult).then_inc(e_f, 1)
                    dve.wait_ge(e_f, b * 4 + (j + 1))
                    tt(oo[:, p, :], oo[:, p, :], xs[:, b * 4 + j, :], ALU.add).then_inc(e_o, 1)

            each(dve, NB, last_quant)


_INS = ['x', 'ctx_1024', 'L0_xattn_w_q', 'L0_xattn_w_k', 'L0_xattn_w_v', 'L0_ffn_w12', 'L0_ffn_w3',
        'L0_ffn_gate_w', 'L1_xattn_Wk', 'L1_xattn_Wq', 'L1_xattn_Wv', 'L1_ffn_clip_x',
        'L1_ffn_clip_down', 'L1_ffn_w_gate', 'L1_ffn_w_up', 'L1_ffn_w_down']


def kernel(**inputs):
    import numpy as _np
    import concourse.bacc as _bacc
    from concourse import mybir as _mybir
    from concourse.bass_utils import run_bass_kernel_spmd as _run

    nc = _bacc.Bacc("TRN2", target_bir_lowering=False, num_devices=1)
    arrays, args = {}, []
    for name in _INS:
        a = _np.ascontiguousarray(inputs[name])
        arrays[f"in_{name}"] = a
        args.append(nc.dram_tensor(f"in_{name}", a.shape, _mybir.dt.from_np(a.dtype), kind="ExternalInput").ap())
    shape = inputs['x'].shape
    res = nc.dram_tensor("out_x", shape, _mybir.dt.float32, kind="ExternalOutput").ap()
    block_program(nc, *args, res)
    r = _run(nc, [arrays], core_ids=[0])
    return r.results[0]["out_x"]
```

```python
import concourse.bass as bass
from concourse import mybir
from contextlib import ExitStack


class Tile:

    def __init__(self, t, parity, half):
        self.t, self.p, self.half = t, parity, half


def steps(eng, count, stages, peel=2):
    lead = max(a for a, _ in stages)
    end = (count - lead) // 2 * 2

    def straight(first, last):
        for t in range(first, last):
            for ahead, step in stages:
                if 0 <= t + ahead < count:
                    step(Tile(t + ahead, (t + ahead) % 2, (t + ahead) // 2))

    straight(-lead, peel)
    with eng.Fori(peel // 2, end // 2) as i:
        for p in range(2):
            for ahead, step in stages:
                n = p + ahead
                step(Tile(i * 2 + n, n % 2, i + n // 2))
    straight(end, count)


def each(eng, count, body):
    body(0)
    with eng.Fori(1, count) as i:
        body(i)


def at_least(eng, sem, value):
    if not isinstance(value, int) or value > 0:
        eng.wait_ge(sem, value)


def block_program(nc, x, ctxT, wq0T, wk0T, wv0, experts, gate_wT, wk1, wq1, wv1_blocks,
                  clip_x, clip_down, w_gate, w_up, w_down, out):
    f32, f16, bf16, i32 = mybir.dt.float32, mybir.dt.float16, mybir.dt.bfloat16, mybir.dt.int32
    ALU, ACT, AX = mybir.AluOpType, mybir.ActivationFunctionType, mybir.AxisListType

    REDUCE_MAX = bass.bass_isa.ReduceOp.max

    P = 128
    T, S, D = x.shape
    DC = D // P
    E = gate_wT.shape[1]
    HALF = experts.shape[2]
    H = 2 * HALF * P // (3 * D)
    H2 = 2 * H
    HC = H // P
    TOPK = 2
    YB = 8
    NT = TOPK * T * S // P + E - 1
    DH = wk1.shape[0]
    NH = D // DH
    I = w_gate.shape[0]
    IC = -(-I // P)
    IROWS = [min(P, I - c * P) for c in range(IC)]
    BLK = 512
    NB = T * S // BLK
    EPS = 1e-5
    NEG = -1e30
    QMAX = 127.0
    MAGIC = 1.5 * 2.0 ** 23
    WS = 64.0
    SCALE0 = float(D) ** -0.5
    SCALE1 = float(DH) ** -0.5
    BIASED = (1, 3)

    st = ExitStack()
    with st:
        def sb(name, shape, dt=f32):
            return st.enter_context(nc.sbuf_tensor(name, shape, dt))

        def sem(name):
            return st.enter_context(nc.semaphore(name))

        region_w = sb("region_w", [P, E * 2 * HALF])
        region_r = sb("region_r", [P, 6144])
        region_x = sb("region_x", [P, T * D])

        class Carve:

            def __init__(self, region, at=0):
                self.region, self.at = region, at

            def __call__(self, shape, dt=f32):
                n = 1
                for d in shape:
                    n *= d
                words = n if dt == f32 or dt == i32 else n // 2
                v = self.region[:, self.at:self.at + words]
                self.at += words
                assert self.at <= self.region.shape[1]
                v = v if dt == f32 else v.bitcast(dt)
                if len(shape) == 1:
                    return v
                names = "abcd"[:len(shape)]
                return v.rearrange("p (" + " ".join(names) + ") -> p " + " ".join(names),
                                   **dict(zip(names, shape)))

        xs = sb("xs", [P, T, D])
        stat = sb("stat", [P, T, 6])
        ln = sb("ln", [P, 8, T])
        mean, var_eps, root, rstd = ln[:, 0, :], ln[:, 1, :], ln[:, 2, :], ln[:, 3, :]
        ln_a, ln_b, ln_c = ln[:, 4, :], ln[:, 5, :], ln[:, 6, :]
        ident = sb("ident", [P, P])
        ident_b = sb("ident_b", [P, P], bf16)
        ident_h = sb("ident_h", [P, P], f16)
        ones = sb("ones", [P, P])
        causal = sb("causal", [P, P])
        below = sb("below", [P, P])
        key8 = sb("key8", [P, T, E])
        tile_no_i = sb("tile_no_i", [P, NT], i32)
        tile_no = sb("tile_no", [P, NT])
        zero_row = sb("zero_row", [P, 2 * D], f16)
        bdv = sb("bdv", [P, P])
        bdqs = sb("bdqs", [P, P])
        parity = sb("parity", [P, 2])
        blocks = sb("blocks", [P, P])
        wq1_s = sb("wq1_s", [DH, P])
        wk1_s = sb("wk1_s", [DH, P])
        gwT = sb("gwT", [P, DC, E])
        v1h = sb("v1h", [P, T, NH, DH + 1], f16)
        v1l = sb("v1l", [P, T, NH, DH + 1], f16)
        rs = sb("rs", [P, 8, T])
        xg_in = sb("xg_in", [P, 2, 2 * D], f16)
        slot_i = sb("slot_i", [P, T, TOPK], i32)
        tile_e = sb("tile_e", [P, NT], i32)
        take = Carve(region_r)
        wqT, wkT, wv, m0 = [take([DC, D]) for _ in range(4)]
        xn, xT, ctT = take([2, D]), take([2, D]), take([2, DC, P])
        gT, v0 = take([2, D]), take([2, D])
        sc, pr, prT = take([2, P]), take([2, P]), take([2, P])
        nmax = sb("nmax", [P, 2])
        psum_row = sb("psum_row", [P, 2])
        prcp = sb("prcp", [P, 2])
        take = Carve(region_x)
        raw = take([2, HALF])
        take = Carve(region_x)
        rows = take([T, 2 * D], f16)
        take = Carve(region_w)
        w_high, w_low = take([2 * E, HALF], f16), take([2 * E, HALF], f16)

        def w12_of(w, e, c):
            return w[:, e * 2 + c, 0:H2]

        def w3_of(w, e, c):
            return w[:, e * 2 + c // 2, H2 + c % 2 * D:H2 + (c % 2 + 1) * D]

        take = Carve(region_r)
        rsc = take([T, E])
        rt = take([8, T, E])
        routed = take([NT, E])
        take = Carve(region_r)
        sil = take([2, BLK])
        hid = take([2, BLK])
        xgT = take([2, 2 * D], f16)
        hTh, hTl = take([2, BLK], f16), take([2, BLK], f16)
        y_out = take([2, D])
        take = Carve(region_r)
        y_in = take([YB, TOPK, D])
        take = Carve(region_w)
        k1s = take([2, DC, P])
        qzh = [take([4, DC, P], f16) for _ in range(2)]
        qzl = [take([4, DC, P], f16) for _ in range(2)]
        kh, kl = take([2, DC, 2, P], f16), take([2, DC, 2, P], f16)
        khl = [take([2, DC, P], f16) for _ in range(2)]
        vch, vcl = take([2, NH, DH + 1], f16), take([2, NH, DH + 1], f16)
        sc1, pr1 = take([2, 4 * P]), take([2, 4 * P])
        pTh, pTl = take([2, 4 * P], f16), take([2, 4 * P], f16)
        o1 = take([2, NH, DH])
        nm1 = sb("nm1", [P, 4, 4])
        rc1 = sb("rc1", [P, NH])
        take = Carve(region_r, 1536)
        wraw, wqb = take([2, IC, D]), take([2, IC, D], bf16)
        wdraw = sb("wdraw", [P, DC, I])
        wdqb = sb("wdqb", [P, DC, I], bf16)
        diag = sb("diag", [P, DC, P])
        take = Carve(region_w)
        hs = take([IC, T * S])
        zqT = take([DC, T * S], bf16)
        hq = take([IC, BLK], bf16)
        hqa = take([2, BLK])
        sil_g = take([2, BLK])
        zqa, zqb, oo = take([2, D]), take([2, D], bf16), take([2, D])
        wmax = sb("wmax", [P, 2 * IC + DC])
        wsc = sb("wsc", [P, 2 * IC + DC])
        wrc = sb("wrc", [P, 2 * IC + DC])
        wguT = sb("wguT", [P, 2, DC, IC * P], bf16)
        wdT = sb("wdT", [P, IC, D], bf16)
        wdrow = sb("wdrow", [P, D])
        cdrow = sb("cdrow", [P, D])
        clips = sb("clips", [P, 2])
        sig = sb("sig", [P, 4, 2])
        zam = sb("zam", [P, T])
        am = sb("am", [P, 8])
        gu = sb("gu", [P, 2, IC])
        ham = sb("ham", [P, IC, NB])

        rows_sent = nc.dram_tensor("rows_sent", [NT * P, 2 * D], f16).ap()
        rows_back = nc.dram_tensor("rows_back", [NT * P, D], f32).ap()

        ps = st.enter_context(nc.psum_tensor("ps", [P, 8, 512], f32))

        def bank(n):
            return ps[:, n, :]

        x_loaded = sem("x_loaded")
        w_loaded = sem("w_loaded")
        bd_loaded = sem("bd_loaded")
        l1w_loaded = sem("l1w_loaded")
        ctx_loaded = [sem("ctx_loaded0"), sem("ctx_loaded1")]
        const_ready = sem("const_ready")
        pool_step = sem("pool_step")
        bd_zero = sem("bd_zero")
        dchain = sem("dchain")
        setup_done = sem("setup_done")
        sig_exp = sem("sig_exp")
        sig_one = sem("sig_one")
        l1q_ready = sem("l1q_ready")
        l1t_done = sem("l1t_done")
        l1t_copied = sem("l1t_copied")
        ln_ve = sem("ln_ve")
        ln_root = sem("ln_root")
        a_xn, a_tr, a_trc, a_qk, a_qkc, a_v, a_vc, a_vl = [
            sem(n) for n in ("a_xn", "a_tr", "a_trc", "a_qk", "a_qkc", "a_v", "a_vc", "a_vl")]
        folded, folded_c = sem("folded"), sem("folded_c")
        a_s, a_sm, a_e, a_pt, a_ptc, a_o, a_fin, a_lk = [
            sem(n) for n in ("a_s", "a_sm", "a_e", "a_pt", "a_ptc", "a_o", "a_fin", "a_lk")]
        b_xn, b_tr, b_hi, b_f, b_lo, b_r, b_rc = [
            sem(n) for n in ("b_xn", "b_tr", "b_hi", "b_f", "b_lo", "b_r", "b_rc")]
        r_d, r_e, r_one, r_rank, r_slot = [sem(n) for n in ("r_d", "r_e", "r_one", "r_rank", "r_slot")]
        w_in = [sem("w_in0"), sem("w_in1")]
        w_hi, w_lo = sem("w_hi"), sem("w_lo")
        zero_ready = sem("zero_ready")
        zeroed, sent = sem("zeroed"), sem("sent")
        m_in = [sem("m_in0"), sem("m_in1")]
        m_back = [sem("m_back0"), sem("m_back1")]
        m_tr, m_trc, m_u, m_s, m_h, m_ht, m_hh, m_hl, m_y, m_yc = [
            sem(n) for n in ("m_tr", "m_trc", "m_u", "m_s", "m_h", "m_ht", "m_hh", "m_hl", "m_y", "m_yc")]
        g_in = [sem(f"g_in{n}") for n in range(YB)]
        c_kin = [sem("c_kin0"), sem("c_kin1")]
        g_one, g_two, g_fin = sem("g_one"), sem("g_two"), sem("g_fin")
        st_done = sem("st_done")
        c_zero = sem("c_zero")
        c_xn, c_tr, c_trc, c_q, c_qc, c_ql, c_kh, c_kl, c_k, c_vv = [
            sem(n) for n in ("c_xn", "c_tr", "c_trc", "c_q", "c_qc", "c_ql", "c_kh", "c_kl", "c_k", "c_vv")]
        c_s, c_nm, c_sm, c_e, c_t, c_tc, c_tl, c_v, c_fin, c_lk = [
            sem(n) for n in ("c_s", "c_nm", "c_sm", "c_e", "c_t", "c_tc", "c_tl", "c_v", "c_fin", "c_lk")]
        d_z, d_am, d_amr, d_sc, d_lk, d_q, d_qb, d_tr, d_trc = [
            sem(n) for n in ("d_z", "d_am", "d_amr", "d_sc", "d_lk", "d_q", "d_qb", "d_tr", "d_trc")]
        g_p, g_s, g_h, g_am = [sem(n) for n in ("g_p", "g_s", "g_h", "g_am")]
        e_am, e_amr, e_sc, e_a, e_c, e_q, e_y, e_o, e_lk, e_out0, e_out1 = [
            sem(n) for n in ("e_am", "e_amr", "e_sc", "e_a", "e_c", "e_q", "e_y", "e_o", "e_lk",
                             "e_out0", "e_out1")]
        e_out = [e_out0, e_out1]
        st0, st2, a_f1, a_f2, c_f1, c_f2, c_f3, e_f = [
            sem(n) for n in ("st0", "st2", "a_f1", "a_f2", "c_f1", "c_f2", "c_f3", "e_f")]

        NBD = P // DH
        NW = 2 * IC + DC

        def cols(t):
            return bass.ts(t, P)

        block = st.enter_context(nc.Block())

        @block.sync
        def _(sp):
            x_v = x.rearrange("b s d -> s b d")
            sp.dma_start(xs[:, 0:T // 2, :], x_v[:, 0:T // 2, :]).then_inc(x_loaded, 16)
            sp.dma_start(xs[:, T // 2:T, :], x_v[:, T // 2:T, :]).then_inc(x_loaded, 16)
            for dst, src in ((wqT, wq0T), (wkT, wk0T), (wv, wv0)):
                sp.dma_start(dst, src.rearrange("(c p) h -> p c h", p=P)).then_inc(w_loaded, 16)

            def load_tile(k):
                at_least(sp, a_s, k.t - 1)
                sp.dma_start(ctT[:, k.p, :, :],
                             ctxT[k.t, :, :].rearrange("(c p) s -> p c s", p=P)).then_inc(ctx_loaded[k.p], 16)
                at_least(sp, w_lo, k.t - 1)
                sp.dma_start(raw[:, k.p, :], experts[k.t, :, :]).then_inc(w_in[k.p], 16)

            steps(sp, T, [(2, load_tile)])

            sp.wait_ge(b_rc, T)
            full = I // P
            for n, src in enumerate((w_gate, w_up)):
                sp.dma_start(wraw[:, n, 0:full, :],
                             src[0:full * P, :].rearrange("(c p) d -> p c d", p=P)).then_inc(l1w_loaded, 16)
                sp.dma_start(wraw[0:I - full * P, n, full, :], src[full * P:I, :]).then_inc(l1w_loaded, 16)
            sp.dma_start(wdraw[:, :, :], w_down.rearrange("(c p) i -> p c i", p=P)).then_inc(l1w_loaded, 16)

            def rows_in(k):
                at_least(sp, m_tr, k.t - 1)
                sp.dma_start(xg_in[:, k.p, :], rows_sent[bass.ts(k.t, P), :]).then_inc(m_in[k.p], 16)

            def rows_out(k):
                sp.wait_ge(m_yc, k.t + 1)
                sp.dma_start(rows_back[bass.ts(k.t, P), :], y_out[:, k.p, :]).then_inc(m_back[k.p], 16)

            sp.wait_ge(sent, TOPK * T * 16)
            steps(sp, NT, [(3, rows_in), (0, rows_out)])

            def load_keys(k):
                if isinstance(k.t, int) and k.t == 0:
                    sp.wait_ge(m_y, NT)
                at_least(sp, c_k, k.t - 1)
                sp.dma_start(k1s[:, k.p, :, :],
                             ctxT[k.t, :, :].rearrange("(c p) s -> p c s", p=P)).then_inc(c_kin[k.p], 16)

            steps(sp, T, [(2, load_keys)])

            def store(k):
                sp.wait_ge(e_o, k.t + 1)
                sp.dma_start(out[k.t, :, :], oo[:, k.p, :]).then_inc(e_out[k.p], 16)

            steps(sp, T, [(0, store)])
            for p in range(2):
                sp.wait_ge(e_out[p], 16 * (T // 2))

        @block.gpsimd
        def _(pool):
            nc.gpsimd.memset(ident[:, :], 0.0).then_inc(pool_step, 1)
            nc.gpsimd.memset(causal[:, :], 0.0).then_inc(pool_step, 1)
            nc.gpsimd.memset(v1h[:, :, :, DH:DH + 1], 1.0)
            nc.gpsimd.memset(v1l[:, :, :, DH:DH + 1], 0.0)
            nc.gpsimd.memset(zero_row[:, :], 0.0).then_inc(zero_ready, 1)
            nc.gpsimd.memset(ones[:, :], 1.0).then_inc(pool_step, 1)
            for j in range(E):
                nc.gpsimd.memset(key8[:, :, j:j + 1], float(E - j))
            nc.gpsimd.iota(tile_no_i[:, :], [[1, NT]], base=0, channel_multiplier=0).then_inc(pool_step, 1)
            pool.wait_ge(pool_step, 4)
            nc.gpsimd.affine_select(out=ident[:, :], in_=ident[:, :], compare_op=ALU.not_equal, fill=1.0,
                                    base=0, pattern=[[-1, P]], channel_multiplier=1).then_inc(pool_step, 1)
            nc.gpsimd.affine_select(out=causal[:, :], in_=causal[:, :], compare_op=ALU.is_ge, fill=NEG,
                                    base=0, pattern=[[-1, P]], channel_multiplier=1).then_inc(pool_step, 1)
            nc.gpsimd.affine_select(out=below[:, :], in_=ones[:, :], compare_op=ALU.is_gt, fill=0.0,
                                    base=0, pattern=[[1, P]], channel_multiplier=-1).then_inc(pool_step, 1)
            nc.gpsimd.affine_select(out=blocks[:, :], in_=ones[:, :], compare_op=ALU.is_ge, fill=0.0,
                                    base=0, pattern=[[-DH, P // DH], [0, DH]],
                                    channel_multiplier=1).then_inc(pool_step, 1)
            pool.wait_ge(pool_step, 8)
            nc.gpsimd.affine_select(out=blocks[:, :], in_=blocks[:, :], compare_op=ALU.is_ge, fill=0.0,
                                    base=DH - 1, pattern=[[DH, P // DH], [0, DH]],
                                    channel_multiplier=-1)
            nc.gpsimd.tensor_copy(tile_no[:, :], tile_no_i[:, :])
            nc.gpsimd.tensor_copy(ident_h[:, :], ident[:, :])
            nc.gpsimd.tensor_copy(ident_b[:, :], ident[:, :]).then_inc(const_ready, 1)

            pool.wait_ge(r_slot, 1)
            pool.wait_ge(zeroed, 16)
            for t in range(T):
                for j in range(TOPK):
                    pool.indirect_dma_start(
                        out=rows_sent[:, :], in_=rows[:, t, :], in_offset=None,
                        out_offset=bass.IndirectOffsetOnAxis(ap=slot_i[:, t, j:j + 1], axis=0)
                    ).then_inc(sent, 16)
            for p in range(2):
                pool.wait_ge(m_back[p], 16 * ((NT + 1 - p) // 2))
            for t in range(T):
                if t >= YB:
                    pool.wait_ge(g_two, t - YB + 1)
                for j in range(TOPK):
                    pool.indirect_dma_start(
                        out=y_in[:, t % YB, j, :], in_=rows_back[:, :], out_offset=None,
                        in_offset=bass.IndirectOffsetOnAxis(ap=slot_i[:, t, j:j + 1], axis=0)
                    ).then_inc(g_in[t % YB], 16)

            def keys(k):
                pool.wait_ge(c_kin[k.p], (k.half + 1) * 16)
                if isinstance(k.t, int) and k.t < 2:
                    pool.wait_ge(m_y, NT)
                else:
                    pool.wait_ge(c_s, (k.t - 1) * 4)
                nc.gpsimd.tensor_tensor(khl[k.p][:, 0, :, :], k1s[:, k.p, :, :],
                                        ones[:, :].unsqueeze(1).to_broadcast([P, DC, P]),
                                        ALU.mult).then_inc(c_kh, 1)
                pool.wait_ge(c_kh, k.t + 1)
                nc.gpsimd.tensor_tensor(khl[k.p][:, 1, :, :], k1s[:, k.p, :, :], khl[k.p][:, 0, :, :],
                                        ALU.subtract).then_inc(c_kl, 1)
                pool.wait_ge(c_kl, k.t + 1)
                for n, to in enumerate((kh, kl)):
                    for par in range(2):
                        ins = nc.gpsimd.tensor_tensor(
                            to[:, k.p, :, par, :], khl[k.p][:, n, :, :],
                            parity[:, par:par + 1].unsqueeze(2).to_broadcast([P, DC, P]), ALU.mult)
                ins.then_inc(c_k, 1)

            def values(k):
                if isinstance(k.t, int) and k.t < 2:
                    pool.wait_ge(m_y, NT)
                else:
                    pool.wait_ge(c_v, (k.t - 1) * 4)
                nc.gpsimd.tensor_copy(vch[:, k.p, :, :], v1h[:, k.t, :, :])
                nc.gpsimd.tensor_copy(vcl[:, k.p, :, :], v1l[:, k.t, :, :]).then_inc(c_vv, 1)

            def add(k):
                pool.wait_ge(c_f2, k.t + 1)
                nc.gpsimd.tensor_tensor(xs[:, k.t, :], xs[:, k.t, :],
                                        o1[:, k.p, :, :].rearrange("p h e -> p (h e)"),
                                        ALU.add).then_inc(c_f3, 1)

            pool.wait_ge(st_done, 1)
            steps(pool, T, [(2, values), (0, add), (3, keys)])

            pool.wait_ge(d_am, 1)
            nc.gpsimd.partition_all_reduce(am[:, 1:2], am[:, 0:1], P, REDUCE_MAX).then_inc(d_amr, 1)
            pool.wait_ge(e_am, 1)
            nc.gpsimd.partition_all_reduce(am[:, 5:6], am[:, 4:5], P, REDUCE_MAX).then_inc(e_amr, 1)

        @block.tensor
        def _(pe):
            mm = nc.tensor.matmul
            pe.wait_ge(const_ready, 1)
            pe.wait_ge(w_loaded, 48)
            pe.wait_ge(bd_loaded, 16 * 6)
            for m in range(DC):
                for c in range(DC):
                    mm(bank(0)[:, m * D:(m + 1) * D], wqT[:, c, m * P:(m + 1) * P], wkT[:, c, :],
                       start=(c == 0), stop=(c == DC - 1))
            mm(bank(1)[:, 0:P], wq1_s[:, :], wk1_s[:, :], start=True, stop=True).then_inc(folded, 1)
            pe.wait_ge(folded_c, 1)

            def transposes(k):
                pe.wait_ge(a_xn, k.t + 1)
                for c in range(DC):
                    last = nc.tensor.transpose(bank(0)[:, c * P:(c + 1) * P],
                                               xn[:, k.p, c * P:(c + 1) * P], ident[:, :])
                last.then_inc(a_tr, 1)

            def projections(k):
                pe.wait_ge(a_trc, k.t + 1)
                for m in range(DC):
                    for c in range(DC):
                        last = mm(bank(2 + k.p)[:, m * P:(m + 1) * P], m0[:, c, m * P:(m + 1) * P],
                                  xT[:, k.p, c * P:(c + 1) * P], start=(c == 0), stop=(c == DC - 1))
                last.then_inc(a_qk, 1)
                pe.wait_ge(ctx_loaded[k.p], (k.half + 1) * 16)
                at_least(pe, a_fin, k.t - 1)
                for c in range(DC):
                    mm(bank(4 + k.p)[:, 0:D], ctT[:, k.p, c, :], wv[:, c, :],
                       start=(c == 0), stop=(c == DC - 1))
                for c in range(DC):
                    last = mm(bank(4 + k.p)[:, D + c * P:D + (c + 1) * P], ctT[:, k.p, c, :], bdv[:, :],
                              start=True, stop=True)
                last.then_inc(a_v, 1)

            def scores(k):
                pe.wait_ge(a_qkc, k.t + 1)
                for c in range(DC):
                    last = mm(bank(6 + k.p)[:, D:D + P], gT[:, k.p, c * P:(c + 1) * P],
                              ctT[:, k.p, c, :], start=(c == 0), stop=(c == DC - 1))
                last.then_inc(a_s, 1)

            def prob_transpose(k):
                pe.wait_ge(a_e, k.t + 1)
                nc.tensor.transpose(bank(6 + k.p)[:, D + P:D + 2 * P], pr[:, k.p, :],
                                    ident[:, :]).then_inc(a_pt, 1)

            def attend(k):
                pe.wait_ge(a_ptc, k.t + 1)
                pe.wait_ge(a_vl, k.t + 1)
                mm(bank(4 + k.p)[:, 0:D], prT[:, k.p, :], v0[:, k.p, :], start=True,
                   stop=True).then_inc(a_o, 1)

            steps(pe, T, [(0, scores), (1, projections), (0, prob_transpose), (2, transposes), (0, attend)])

            pe.wait_ge(a_fin, T)

            def b_transposes(k):
                pe.wait_ge(b_xn, k.t + 1)
                for c in range(DC):
                    last = nc.tensor.transpose(bank(k.p)[:, c * P:(c + 1) * P],
                                               xn[:, k.p, c * P:(c + 1) * P], ident[:, :])
                last.then_inc(b_tr, 1)

            def router(k):
                pe.wait_ge(b_f, k.t + 1)
                at_least(pe, b_rc, k.t - 1)
                for c in range(DC):
                    last = mm(bank(2 + k.p)[:, 0:E], xT[:, k.p, c * P:(c + 1) * P], gwT[:, c, :],
                              start=(c == 0), stop=(c == DC - 1))
                last.then_inc(b_r, 1)

            steps(pe, T, [(1, b_transposes), (0, router)])

            pe.wait_ge(r_one, 1)
            chosen = rt[:, 4, :, :].rearrange("p t e -> p (t e)")
            mm(bank(4)[:, 0:T * E], below[:, :], chosen, start=True, stop=True)
            mm(bank(4)[:, T * E:2 * T * E], ones[:, :], chosen, start=True, stop=True).then_inc(r_rank, 1)

            n = 0
            for w in range(2):
                for dk in range(DC):
                    if n == 0:
                        pe.wait_ge(l1q_ready, 1)
                    if n >= 2:
                        pe.wait_ge(l1t_copied, n - 1)
                    bk = bank(n % 2).bitcast(bf16)
                    for c in range(IC):
                        last = nc.tensor.transpose(bk[:, c * P:c * P + IROWS[c]],
                                                   wqb[0:IROWS[c], w, c, dk * P:(dk + 1) * P],
                                                   ident_b[0:IROWS[c], 0:IROWS[c]])
                    last.then_inc(l1t_done, 1)
                    n += 1
            for half in range(2):
                pe.wait_ge(l1t_copied, n - 1)
                bk = bank(n % 2).bitcast(bf16)
                for c in range(half * IC // 2, (half + 1) * IC // 2):
                    for dk in range(DC):
                        o = (c - half * IC // 2) * D + dk * P
                        last = nc.tensor.transpose(bk[0:IROWS[c], o:o + P],
                                                   wdqb[:, dk, c * P:c * P + IROWS[c]], ident_b[:, :])
                last.then_inc(l1t_done, 1)
                n += 1
            pe.wait_ge(l1t_copied, n)
            for dk in range(DC):
                last = mm(bank(0)[:, dk * P:(dk + 1) * P], ones[:, :], diag[:, dk, :], start=True, stop=True)
            last.then_inc(l1t_done, 1)
            pe.wait_ge(l1t_copied, n + 1)

            def m_transposes(k):
                pe.wait_ge(m_in[k.p], (k.half + 1) * 16)
                bk = bank(0).bitcast(f16)
                for c in range(2 * DC):
                    last = nc.tensor.transpose(bk[:, c * P:(c + 1) * P],
                                               xg_in[:, k.p, c * P:(c + 1) * P], ident_h[:, :])
                last.then_inc(m_tr, 1)

            def up(k):
                e = pe.value_load(tile_e[0:1, bass.ts(k.t, 1)], min_val=0, max_val=E - 1)
                pe.wait_ge(m_trc, k.t + 1)
                terms = [(a, w, c) for c in range(DC) for a, w in ((0, w_high), (0, w_low), (DC, w_high))]
                for n in range(2):
                    for m, (a, w, c) in enumerate(terms):
                        last = mm(bank(1 + 2 * k.p + n), xgT[:, k.p, (a + c) * P:(a + c + 1) * P],
                                  w12_of(w, e, c)[:, n * H:(n + 1) * H],
                                  start=(m == 0), stop=(m == len(terms) - 1))
                last.then_inc(m_u, 1)

            def h_transposes(k):
                pe.wait_ge(m_h, k.t + 1)
                for c in range(HC):
                    last = nc.tensor.transpose(bank(5)[:, c * P:(c + 1) * P],
                                               hid[:, k.p, c * P:(c + 1) * P], ident[:, :])
                last.then_inc(m_ht, 1)

            def down(k):
                e = pe.value_load(tile_e[0:1, bass.ts(k.t, 1)], min_val=0, max_val=E - 1)
                pe.wait_ge(m_hl, k.t + 1)
                terms = [(a, w, c) for c in range(HC) for a, w in ((hTh, w_high), (hTh, w_low), (hTl, w_high))]
                for m, (a, w, c) in enumerate(terms):
                    last = mm(bank(6 + k.p)[:, 0:D], a[:, k.p, c * P:(c + 1) * P], w3_of(w, e, c),
                              start=(m == 0), stop=(m == len(terms) - 1))
                last.then_inc(m_y, 1)

            pe.wait_ge(r_slot, 1)
            steps(pe, NT, [(1, up), (2, m_transposes), (0, down), (1, h_transposes)])

            def c_transposes(k):
                pe.wait_ge(c_xn, k.t + 1)
                at_least(pe, c_f2, k.t - 2)
                for c in range(DC):
                    last = nc.tensor.transpose(bank(1 - k.p)[:, c * P:(c + 1) * P],
                                               xn[:, 0, c * P:(c + 1) * P], ident[:, :])
                last.then_inc(c_tr, 1)

            def c_project(k):
                pe.wait_ge(c_trc, k.t + 1)
                mm(bank(1 - k.p)[:, 0:D], bdqs[:, :], xT[:, 0, 0:D], start=True,
                   stop=True).then_inc(c_q, 1)

            def c_scores(s):
                def step(k):
                    if s == 0:
                        pe.wait_ge(c_ql, k.t + 1)
                        pe.wait_ge(c_k, k.t + 1)
                    for c in range(DC):
                        terms = ((qzh, kh), (qzh, kl), (qzl, kh))
                        for m, (a, b) in enumerate(terms):
                            last = mm(bank(4 + s)[:, 2 * c * P:(2 * c + 2) * P], a[k.p][:, s, c, :],
                                      b[:, k.p, c, :, :].rearrange("p a s -> p (a s)"),
                                      start=(m == 0), stop=(m == len(terms) - 1))
                    last.then_inc(c_s, 1)
                return step

            def c_ptrans(s):
                def step(k):
                    pe.wait_ge(c_e, k.t * 4 + (s + 1))
                    for j in range(4):
                        last = nc.tensor.transpose(bank(2 + s % 2)[:, j * P:(j + 1) * P],
                                                   pr1[:, s % 2, j * P:(j + 1) * P], ident[:, :])
                    last.then_inc(c_t, 1)
                return step

            def c_values(s):
                def step(k):
                    pe.wait_ge(c_tl, k.t * 4 + (s + 1))
                    if s == 0:
                        pe.wait_ge(c_ql, min(T, k.t + 2) if isinstance(k.t, int) else k.t + 2)
                        pe.wait_ge(c_vv, k.t + 1)
                    for c in range(DC):
                        for par in range(2):
                            h = c * NBD + 2 * s + par
                            at = (2 * c + par) * P
                            terms = ((pTh, vch), (pTh, vcl), (pTl, vch))
                            for m, (a, v) in enumerate(terms):
                                last = mm(bank(k.p)[:, h * (DH + 1):(h + 1) * (DH + 1)],
                                          a[:, s % 2, at:at + P], v[:, k.p, h, :],
                                          start=(m == 0), stop=(m == len(terms) - 1))
                    last.then_inc(c_v, 1)
                return step

            pe.wait_ge(st_done, 1)
            stages = []
            for s in range(4):
                stages.append(((s + 3) // 4, c_scores((s + 3) % 4)))
                stages.append(((s + 1) // 4, c_ptrans((s + 1) % 4)))
                if s == 1:
                    stages.append((2, c_transposes))
                if s == 2:
                    stages.append((2, c_project))
                stages.append((0, c_values(s)))
            steps(pe, T, stages)

            def d_transposes(k):
                pe.wait_ge(d_qb, k.t + 1)
                at_least(pe, d_trc, k.t - 1)
                bk = bank(k.p).bitcast(bf16)
                for c in range(DC):
                    last = nc.tensor.transpose(bk[:, c * P:(c + 1) * P], zqb[:, k.p, c * P:(c + 1) * P],
                                               ident_b[:, :])
                last.then_inc(d_tr, 1)

            pe.wait_ge(c_fin, T)
            steps(pe, T, [(0, d_transposes)])
            pe.wait_ge(d_trc, T)
            def gate_up(b):
                for c in range(IC):
                    r = IROWS[c]
                    if c < IC - 1:
                        back = c - 1 if c == IC - 2 else c - 2
                        at_least(pe, g_h, b * IC + back if back > 0 else b * IC)
                    for w in range(2):
                        for dk in range(DC):
                            last = mm(ps[0:r, 2 * (c % 3) + w, :], wguT[:, w, dk, c * P:c * P + r],
                                      zqT[:, dk, bass.ts(b, BLK)], start=(dk == 0), stop=(dk == DC - 1))
                    last.then_inc(g_p, 1)
            each(pe, NB, gate_up)
            pe.wait_ge(g_am, NB * IC)

            def last_down(b):
                pe.wait_ge(e_q, (b + 1) * IC)
                for j in range(BLK // P):
                    at_least(pe, e_f, b * 4 + (j - 1))
                    for c in range(IC):
                        r = IROWS[c]
                        last = mm(bank(6 + j % 2)[:, 0:D], hq[0:r, c, j * P:(j + 1) * P], wdT[0:r, c, :],
                                  start=(c == 0), stop=(c == IC - 1))
                    last.then_inc(e_y, 1)

            each(pe, NB, last_down)

        @block.scalar
        def _(act):
            for dst, src in ((wq1_s[:, :], wq1), (wk1_s[:, :], wk1), (bdv[:, :], wv1_blocks),
                             (gwT[:, :, :], gate_wT.rearrange("(c p) e -> p c e", p=P))):
                act.dma_start(dst, src).then_inc(bd_loaded, 16)
            for n, src in enumerate((clip_x, clip_down)):
                act.dma_start(clips[:, n:n + 1], src.rearrange("(a n) -> a n", a=1).to_broadcast([P, 1])
                              ).then_inc(bd_loaded, 16)
            act.wait_ge(zero_ready, 1)
            act.dma_start(rows_sent.rearrange("(n p) d -> p n d", p=P),
                          zero_row[:, :].unsqueeze(1).to_broadcast([P, NT, 2 * D])).then_inc(zeroed, 16)
            act.wait_ge(bd_loaded, 16 * 6)
            act.activation(sig[:, 0, :], clips[:, :], ACT.Exp, scale=-1.0).then_inc(sig_exp, 1)
            act.wait_ge(folded, 1)
            act.copy(m0, bank(0).rearrange("p (c d) -> p c d", d=D)).then_inc(folded_c, 1)

            def roots(n):
                act.wait_ge(ln_ve, n + 1)
                act.activation(root, var_eps, ACT.Sqrt).then_inc(ln_root, 1)

            roots(0)

            def transposed(k):
                act.wait_ge(a_tr, k.t + 1)
                at_least(act, a_qk, k.t - 1)
                act.copy(xT[:, k.p, :], bank(0)[:, 0:D]).then_inc(a_trc, 1)

            def qk_copy(k):
                act.wait_ge(a_qk, k.t + 1)
                act.copy(gT[:, k.p, :], bank(2 + k.p)[:, 0:D]).then_inc(a_qkc, 1)

            def v_copy(k):
                act.wait_ge(a_v, k.t + 1)
                act.copy(v0[:, k.p, :], bank(4 + k.p)[:, 0:D])
                act.copy(v1h[:, k.t, :, 0:DH],
                         bank(4 + k.p)[:, D:2 * D].rearrange("p (h e) -> p h e", e=DH)).then_inc(a_vc, 1)

            def exps(k):
                act.wait_ge(a_sm, k.t + 1)
                act.activation(pr[:, k.p, :], sc[:, k.p, :], ACT.Exp, bias=nmax[:, k.p:k.p + 1],
                               accum_out=psum_row[:, k.p:k.p + 1]).then_inc(a_e, 1)

            def pt_copy(k):
                act.wait_ge(a_pt, k.t + 1)
                act.copy(prT[:, k.p, :], bank(6 + k.p)[:, D + P:D + 2 * P]).then_inc(a_ptc, 1)

            act.wait_ge(const_ready, 1)
            nc.scalar.preload_act_table(ACT.Exp)
            def weights_high(k):
                act.wait_ge(w_in[k.p], (k.half + 1) * 16)
                act.mul(w_high[:, k.t, :], raw[:, k.p, :], WS).then_inc(w_hi, 1)

            steps(act, T, [(0, exps), (1, qk_copy), (0, pt_copy), (2, transposed), (1, v_copy),
                           (0, weights_high)])

            roots(1)

            nc.scalar.preload_act_table(ACT.Exp)

            def b_high(k):
                act.wait_ge(b_xn, k.t + 1)
                act.copy(rows[:, k.t, 0:D], xn[:, k.p, :]).then_inc(b_hi, 1)
                act.wait_ge(b_tr, k.t + 1)
                at_least(act, b_r, k.t - 1)
                act.copy(xT[:, k.p, 0:D], bank(k.p)[:, 0:D]).then_inc(b_f, 1)

            steps(act, T, [(0, b_high)])
            act.wait_ge(r_d, 1)
            act.activation(rs[:, 2, :], rs[:, 3, :], ACT.Exp).then_inc(r_e, 1)

            n = 0
            for w in range(2):
                for dk in range(DC):
                    act.wait_ge(l1t_done, n + 1)
                    act.copy(wguT[:, w, dk, 0:(IC - 1) * P],
                             bank(n % 2).bitcast(bf16)[:, 0:(IC - 1) * P])
                    act.copy(wguT[:, w, dk, (IC - 1) * P:I],
                             bank(n % 2).bitcast(bf16)[:, (IC - 1) * P:I]).then_inc(l1t_copied, 1)
                    n += 1
            for half in range(2):
                act.wait_ge(l1t_done, n + 1)
                bk = bank(n % 2).bitcast(bf16)
                for c in range(half * IC // 2, (half + 1) * IC // 2):
                    o = (c - half * IC // 2) * D
                    last = act.copy(wdT[0:IROWS[c], c, :], bk[0:IROWS[c], o:o + D])
                last.then_inc(l1t_copied, 1)
                n += 1
            act.wait_ge(l1t_done, n + 1)
            act.copy(wdrow[:, :], bank(0)[:, 0:D]).then_inc(l1t_copied, 1)

            nc.scalar.preload_act_table(ACT.Silu)

            def m_tcopy(k):
                act.wait_ge(m_tr, k.t + 1)
                act.copy(xgT[:, k.p, :], bank(0).bitcast(f16)[:, 0:2 * D]).then_inc(m_trc, 1)

            def silu(k):
                act.wait_ge(m_u, k.t + 1)
                act.activation(sil[:, k.p, :], bank(1 + 2 * k.p), ACT.Silu, scale=1.0 / WS).then_inc(m_s, 1)

            def high(k):
                act.wait_ge(m_ht, k.t + 1)
                act.copy(hTh[:, k.p, :], bank(5)).then_inc(m_hh, 1)

            steps(act, NT, [(1, silu), (2, m_tcopy), (1, high)])

            roots(2)

            nc.scalar.preload_act_table(ACT.Exp)

            def c_xcopy(k):
                act.wait_ge(c_tr, k.t + 1)
                act.copy(xT[:, 0, 0:D], bank(1 - k.p)[:, 0:D]).then_inc(c_trc, 1)

            def c_qcopy(k):
                act.wait_ge(c_q, k.t + 1)
                for s in range(4):
                    strip = slice(32 * s, 32 * s + 32)
                    last = act.copy(qzh[k.p][strip, s, :, :],
                                    bank(1 - k.p)[strip, 0:D].rearrange("p (c s) -> p c s", c=DC))
                last.then_inc(c_qc, 1)

            def c_exp(s):
                def step(k):
                    act.wait_ge(c_sm, k.t * 4 + (s + 1))
                    at_least(act, c_t, k.t * 4 + (s - 1))
                    if s in BIASED:
                        for j in range(4):
                            last = act.activation(pr1[:, s % 2, j * P:(j + 1) * P],
                                                  bank(4 + s)[:, j * P:(j + 1) * P], ACT.Exp,
                                                  bias=nm1[:, s, j:j + 1])
                    else:
                        last = act.activation(pr1[:, s % 2, :], sc1[:, s % 2, :], ACT.Exp)
                    last.then_inc(c_e, 1)
                return step

            def c_ptcopy(s):
                def step(k):
                    act.wait_ge(c_t, k.t * 4 + (s + 1))
                    act.copy(pTh[:, s % 2, :], bank(2 + s % 2)).then_inc(c_tc, 1)
                return step

            stages = []
            for s in range(4):
                stages.append(((s + 2) // 4, c_exp((s + 2) % 4)))
                stages.append(((s + 1) // 4, c_ptcopy((s + 1) % 4)))
                if s == 1:
                    stages.append((2, c_xcopy))
                if s == 2:
                    stages.append((2, c_qcopy))
            steps(act, T, stages)

            roots(3)

            nc.scalar.preload_act_table(ACT.Silu)

            def z_int(k):
                act.wait_ge(d_q, k.t + 1)
                at_least(act, d_tr, k.t - 1)
                act.activation(zqb[:, k.p, :], zqa[:, k.p, :], ACT.Copy, bias=-MAGIC).then_inc(d_qb, 1)

            def z_tcopy(k):
                act.wait_ge(d_tr, k.t + 1)
                act.copy(zqT[:, :, cols(k.t)],
                         bank(k.p).bitcast(bf16)[:, 0:D].rearrange("p (c s) -> p c s", c=DC)).then_inc(d_trc, 1)

            steps(act, T, [(1, z_int), (0, z_tcopy)])
            def gate_silu(b):
                for c in range(IC):
                    r = IROWS[c]
                    act.wait_ge(g_p, b * IC + (c + 1))
                    at_least(act, g_h, b * IC + (c - 1))
                    act.activation(sil_g[0:r, c % 2, :], ps[0:r, 2 * (c % 3), :], ACT.Silu,
                                   scale=gu[0:r, 0, c:c + 1]).then_inc(g_s, 1)
            each(act, NB, gate_silu)
            act.wait_ge(e_sc, 1)

            def hidden_scale(b):
                for c in range(IC):
                    r = IROWS[c]
                    at_least(act, e_q, b * IC + (c - 1))
                    act.activation(hqa[0:r, c % 2, :], hs[0:r, c, bass.ts(b, BLK)], ACT.Copy,
                                   bias=MAGIC, scale=am[0:r, 7:8]).then_inc(e_a, 1)

            each(act, NB, hidden_scale)

        @block.vector
        def _(dve):
            chain = [0]

            def link(ins):
                chain[0] += 1
                ins.then_inc(dchain, 1)
                dve.wait_ge(dchain, chain[0])

            ts, tt, stt = nc.vector.tensor_scalar, nc.vector.tensor_tensor, nc.vector.scalar_tensor_tensor

            def statistics(sem_name):
                with dve.Fori(0, T // 4) as q:
                    for i in range(4):
                        t = q * 4 + i
                        nc.vector.bn_stats(stat[:, t, :], xs[:, t, :]).then_inc(sem_name, 1)

            def rstds(n, sem_name, count):
                dve.wait_ge(sem_name, count)
                me, mo, ve, vo = stat[:, :, 1], stat[:, :, 4], stat[:, :, 2], stat[:, :, 5]
                link(tt(ln_a, me, mo, ALU.add))
                link(ts(mean, ln_a, 0.5, None, ALU.mult))
                link(tt(ln_b, me, mo, ALU.subtract))
                link(tt(ln_c, ln_b, ln_b, ALU.mult))
                link(tt(ln_a, ve, vo, ALU.add))
                link(ts(ln_b, ln_a, 1.0 / D, EPS, ALU.mult, ALU.add))
                stt(var_eps, ln_c, 0.25, ln_b, ALU.mult, ALU.add).then_inc(ln_ve, 1)
                dve.wait_ge(ln_root, n + 1)
                link(nc.vector.reciprocal(rstd, root))
                link(tt(ln_a, rstd, rstd, ALU.mult))
                link(tt(ln_b, ln_a, var_eps, ALU.mult))
                link(ts(ln_c, ln_b, -0.5, 1.5, ALU.mult, ALU.add))
                link(tt(rstd, rstd, ln_c, ALU.mult))

            def normalise(dst, k):
                return ts(dst, xs[:, k.t, :], mean[:, cols1(k.t)], rstd[:, cols1(k.t)],
                          ALU.subtract, ALU.mult)

            def cols1(t):
                return bass.ts(t, 1)

            dve.wait_ge(x_loaded, 32)
            statistics(st0)
            dve.wait_ge(const_ready, 1)
            dve.wait_ge(folded, 1)
            stt(bdqs[:, :], bank(1)[:, 0:P], SCALE1, blocks[:, :], ALU.mult, ALU.mult)
            nc.vector.tensor_reduce(parity[:, :],
                                    blocks[:, :].rearrange("p (g a e) -> p a g e", a=2, e=DH)[:, :, :, 0],
                                    axis=AX.X, op=ALU.max)
            dve.wait_ge(sig_exp, 1)
            link(ts(sig[:, 1, :], sig[:, 0, :], 1.0, None, ALU.add))
            link(nc.vector.reciprocal(sig[:, 2, :], sig[:, 1, :]))

            rstds(0, st0, T)

            def a_norm(k):
                at_least(dve, a_tr, k.t - 1)
                normalise(xn[:, k.p, :], k).then_inc(a_xn, 1)

            def a_mask(k):
                dve.wait_ge(a_s, k.t + 1)
                stt(sc[:, k.p, :], bank(6 + k.p)[:, D:D + P], SCALE0, causal[:, :], ALU.mult,
                    ALU.add).then_inc(a_lk, 1)
                dve.wait_ge(a_lk, k.t + 1)
                nc.vector.tensor_reduce(nmax[:, k.p:k.p + 1], sc[:, k.p, :], axis=AX.X, op=ALU.max,
                                        negate=True).then_inc(a_sm, 1)

            def a_v_low(k):
                dve.wait_ge(a_vc, k.t + 1)
                tt(v1l[:, k.t, :, 0:DH], bank(4 + k.p)[:, D:2 * D].rearrange("p (h e) -> p h e", e=DH),
                   v1h[:, k.t, :, 0:DH], ALU.subtract).then_inc(a_vl, 1)

            def a_finish(k):
                dve.wait_ge(a_o, k.t + 1)
                nc.vector.reciprocal(prcp[:, k.p:k.p + 1], psum_row[:, k.p:k.p + 1]).then_inc(a_f1, 1)
                dve.wait_ge(a_f1, k.t + 1)
                stt(xs[:, k.t, :], bank(4 + k.p)[:, 0:D], prcp[:, k.p:k.p + 1], xs[:, k.t, :],
                    ALU.mult, ALU.add).then_inc(a_f2, 1)
                dve.wait_ge(a_f2, k.t + 1)
                nc.vector.bn_stats(stat[:, k.t, :], xs[:, k.t, :]).then_inc(a_fin, 1)

            def weights_low(k):
                dve.wait_ge(w_hi, k.t + 1)
                stt(w_low[:, k.t, :], raw[:, k.p, :], WS, w_high[:, k.t, :], ALU.mult,
                    ALU.subtract).then_inc(w_lo, 1)

            steps(dve, T, [(0, a_mask), (3, a_norm), (1, a_v_low), (0, a_finish), (0, weights_low)])
            rstds(1, a_fin, T)

            def b_norm(k):
                at_least(dve, b_tr, k.t - 1)
                at_least(dve, b_lo, k.t - 1)
                normalise(xn[:, k.p, :], k).then_inc(b_xn, 1)

            def b_route(k):
                dve.wait_ge(b_r, k.t + 1)
                nc.vector.tensor_copy(rsc[:, k.t, :], bank(2 + k.p)[:, 0:E]).then_inc(b_rc, 1)

            def b_low(k):
                dve.wait_ge(b_hi, k.t + 1)
                tt(rows[:, k.t, D:2 * D], xn[:, k.p, :], rows[:, k.t, 0:D], ALU.subtract).then_inc(b_lo, 1)

            steps(dve, T, [(1, b_norm), (0, b_low), (0, b_route)])

            def wide(v):
                return v.unsqueeze(2).to_broadcast([P, T, E])

            dve.wait_ge(b_rc, T)
            top1, top2, e21, d21 = rs[:, 0, :], rs[:, 1, :], rs[:, 2, :], rs[:, 3, :]
            pick, den, p1, p2 = rs[:, 4, :], rs[:, 5, :], rs[:, 6, :], rs[:, 7, :]
            hit, one1, one2, rest = rt[:, 0, :, :], rt[:, 1, :, :], rt[:, 2, :, :], rt[:, 3, :, :]

            def first_of(scores_ap, top, one):
                link(nc.vector.tensor_reduce(top, scores_ap, axis=AX.X, op=ALU.max))
                link(tt(hit, scores_ap, wide(top), ALU.is_equal))
                link(tt(hit, hit, key8[:, :, :], ALU.mult))
                link(nc.vector.tensor_reduce(pick, hit, axis=AX.X, op=ALU.max))
                link(tt(one, key8[:, :, :], wide(pick), ALU.is_equal))

            first_of(rsc[:, :, :], top1, one1)
            link(stt(rest, one1, NEG, rsc[:, :, :], ALU.mult, ALU.add))
            first_of(rest, top2, one2)
            tt(d21, top2, top1, ALU.subtract).then_inc(r_d, 1)
            chosen = rt[:, 4, :, :]
            tt(chosen, one1, one2, ALU.add).then_inc(r_one, 1)
            dve.wait_ge(r_e, 1)
            link(ts(den, e21, 1.0, None, ALU.add))
            link(nc.vector.reciprocal(p1, den))
            link(tt(p2, p1, e21, ALU.mult))

            def running(a, b, width, axis_slice):
                shift = 1
                while shift < width:
                    nc.vector.tensor_copy(axis_slice(b, 0, shift), axis_slice(a, 0, shift))
                    link(tt(axis_slice(b, shift, width), axis_slice(a, shift, width),
                            axis_slice(a, 0, width - shift), ALU.add))
                    a, b = b, a
                    shift *= 2
                return a, b

            dve.wait_ge(r_rank, 1)
            rank = bank(4)[:, 0:T * E].rearrange("p (t e) -> p t e", e=E)
            count = bank(4)[:, T * E:2 * T * E].rearrange("p (t e) -> p t e", e=E)
            place = rt[:, 7, :, :]
            link(nc.vector.tensor_copy(rt[:, 5, :, :], count))
            upto, _ = running(rt[:, 5, :, :], rt[:, 6, :, :], T, lambda v, a, b: v[:, a:b, :])
            link(tt(place, upto, count, ALU.subtract))
            link(tt(place, place, rank, ALU.add))
            need, ends = routed[:, 0, :], routed[:, 1, :]
            link(ts(need, upto[:, T - 1, :], 1.0 / P, 0.5 - 0.5 / P, ALU.mult, ALU.add))
            link(ts(need, need, MAGIC, None, ALU.add))
            link(ts(need, need, -MAGIC, None, ALU.add))
            link(nc.vector.tensor_copy(ends, need))
            ends, spare = running(ends, routed[:, 2, :], E, lambda v, a, b: v[:, a:b])
            link(tt(spare, ends, need, ALU.subtract))
            first = routed[:, 3, :]
            link(ts(first, spare, float(P), None, ALU.mult))
            link(tt(place, place, first.unsqueeze(1).to_broadcast([P, T, E]), ALU.add))
            slot_f = rt[:, 5, :, :].rearrange("p t e -> p (t e)")[:, 0:T * TOPK].rearrange(
                "p (t j) -> p t j", j=TOPK)
            for j, one in enumerate((one1, one2)):
                link(tt(hit, place, one, ALU.mult))
                link(nc.vector.tensor_reduce(slot_f[:, :, j], hit, axis=AX.X, op=ALU.add))
            link(nc.vector.tensor_copy(slot_i[:, :, :], slot_f))
            past = rt[:, 5:8, :, :].rearrange("p a t e -> p (a t e)")[:, 0:NT * E].rearrange(
                "p (n e) -> p n e", e=E)
            link(tt(past, tile_no[:, :].unsqueeze(2).to_broadcast([P, NT, E]),
                    ends.unsqueeze(1).to_broadcast([P, NT, E]), ALU.is_ge))
            owner = rt[:, 4, :, :].rearrange("p t e -> p (t e)")[:, 0:NT]
            link(nc.vector.tensor_reduce(owner, past, axis=AX.X, op=ALU.add))
            ts(tile_e[:, :], owner, float(E - 1), None, ALU.min).then_inc(r_slot, 1)

            dve.wait_ge(l1w_loaded, 16 * 5)
            parts = []
            for w in range(2):
                for c in range(IC):
                    parts.append((wraw[0:IROWS[c], w, c, :], wqb[0:IROWS[c], w, c, :], IROWS[c], w * IC + c))
            for c in range(DC):
                parts.append((wdraw[:, c, :], wdqb[:, c, :], P, 2 * IC + c))
            link(nc.vector.memset(wmax[:, :], 1.0))
            for src, _, r, n in parts:
                last = nc.vector.tensor_reduce(wmax[0:r, n:n + 1], src, axis=AX.X, op=ALU.max,
                                               apply_absolute_value=True)
            link(last)
            link(ts(wsc[:, :], wmax[:, :], 1.0 / QMAX, None, ALU.mult))
            link(nc.vector.reciprocal(wrc[:, :], wsc[:, :]))
            for src, _, r, n in parts:
                last = ts(src, src, wrc[0:r, n:n + 1], MAGIC, ALU.mult, ALU.add)
            link(last)
            for src, _, r, n in parts:
                last = ts(src, src, MAGIC + QMAX, MAGIC - QMAX - 1.0, ALU.min, ALU.max)
            link(last)
            for src, dst, r, n in parts:
                nc.vector.tensor_scalar(dst, src, -MAGIC, None, ALU.add)
            for c in range(DC):
                last = ts(diag[:, c, :], ident[:, :], wsc[:, 2 * IC + c:2 * IC + c + 1], None, ALU.mult)
            last.then_inc(l1q_ready, 1)

            def hidden(k):
                dve.wait_ge(m_s, k.t + 1)
                stt(hid[:, k.p, :], bank(2 + 2 * k.p), 1.0 / WS, sil[:, k.p, :], ALU.mult,
                    ALU.mult).then_inc(m_h, 1)

            def low(k):
                dve.wait_ge(m_hh, k.t + 1)
                tt(hTl[:, k.p, :], bank(5), hTh[:, k.p, :], ALU.subtract).then_inc(m_hl, 1)

            def back(k):
                dve.wait_ge(m_y, k.t + 1)
                at_least(dve, m_back[k.p], k.half * 16)
                ts(y_out[:, k.p, :], bank(6 + k.p)[:, 0:D], 1.0 / WS, None, ALU.mult).then_inc(m_yc, 1)

            steps(dve, NT, [(1, hidden), (0, back), (1, low)])

            for t in range(T):
                p = t % YB
                dve.wait_ge(g_in[p], 32 * (t // YB + 1))
                stt(xs[:, t, :], y_in[:, p, 0, :], rs[:, 6, t:t + 1], xs[:, t, :], ALU.mult,
                    ALU.add).then_inc(g_one, 1)
                dve.wait_ge(g_one, t + 1)
                stt(xs[:, t, :], y_in[:, p, 1, :], rs[:, 7, t:t + 1], xs[:, t, :], ALU.mult,
                    ALU.add).then_inc(g_two, 1)
            dve.wait_ge(g_two, T)
            statistics(st2)
            rstds(2, st2, T)
            nc.vector.memset(rc1[:, :], 0.0).then_inc(st_done, 1)

            for q in qzh + qzl:
                last = nc.vector.memset(q.rearrange("p a c s -> p (a c s)"), 0.0)
            last.then_inc(c_zero, 1)
            dve.wait_ge(c_zero, 1)

            def c_norm(k):
                at_least(dve, c_tr, k.t)
                normalise(xn[:, 0, :], k).then_inc(c_xn, 1)

            def c_shift(s):
                def step(k):
                    b4 = bank(4 + s).rearrange("p (h s) -> p h s", h=4)
                    o4 = sc1[:, s % 2, :].rearrange("p (h s) -> p h s", h=4)
                    dve.wait_ge(c_s, k.t * 4 + (s + 1))
                    if s in BIASED:
                        at_least(dve, c_e, k.t * 4 + (s - 3))
                        nc.vector.tensor_reduce(nm1[:, s, :], b4, axis=AX.X, op=ALU.max,
                                                negate=True).then_inc(c_sm, 1)
                        return
                    at_least(dve, c_e, k.t * 4 + (s - 1))
                    nc.vector.tensor_reduce(nm1[:, s, :], b4, axis=AX.X, op=ALU.max,
                                            negate=True).then_inc(c_nm, 1)
                    shifted = [g for g in range(4) if g not in BIASED]
                    dve.wait_ge(c_nm, k.t * len(shifted) + (shifted.index(s) + 1))
                    tt(o4, b4, nm1[:, s, :].unsqueeze(2).to_broadcast([P, 4, P]),
                       ALU.add).then_inc(c_sm, 1)
                return step

            def c_low(s):
                def step(k):
                    dve.wait_ge(c_tc, k.t * 4 + (s + 1))
                    tt(pTl[:, s % 2, :], bank(2 + s % 2), pTh[:, s % 2, :], ALU.subtract).then_inc(c_tl, 1)
                return step

            def c_qlow(k):
                dve.wait_ge(c_qc, k.t + 1)
                for s in range(4):
                    strip = slice(32 * s, 32 * s + 32)
                    last = tt(qzl[k.p][strip, s, :, :],
                              bank(1 - k.p)[strip, 0:D].rearrange("p (c s) -> p c s", c=DC),
                              qzh[k.p][strip, s, :, :], ALU.subtract)
                last.then_inc(c_ql, 1)

            def c_output(k):
                dve.wait_ge(c_v, k.t * 4 + 4)
                o = bank(k.p)[:, 0:NH * (DH + 1)].rearrange("p (h e) -> p h e", e=DH + 1)
                nc.vector.reciprocal(rc1[:, :], o[:, :, DH]).then_inc(c_f1, 1)
                dve.wait_ge(c_f1, k.t + 1)
                at_least(dve, c_f3, k.t - 1)
                tt(o1[:, k.p, :, :], o[:, :, 0:DH], rc1[:, :].unsqueeze(2).to_broadcast([P, NH, DH]),
                   ALU.mult).then_inc(c_f2, 1)

            def c_stats(k):
                dve.wait_ge(c_f3, k.t + 1)
                nc.vector.bn_stats(stat[:, k.t, :], xs[:, k.t, :]).then_inc(c_fin, 1)

            stages = []
            for s in range(4):
                stages.append((1, c_low(s)))
                if s == 0:
                    stages.append((0, c_output))
                stages.append((1 + (s + 3) // 4, c_shift((s + 3) % 4)))
                if s == 1:
                    stages.append((0, c_stats))
                if s == 2:
                    stages.append((4, c_norm))
                if s == 3:
                    stages.append((3, c_qlow))
            steps(dve, T, stages)
            rstds(3, c_fin, T)

            z = region_w[:, 0:T * D].rearrange("p (t d) -> p t d", d=D)
            with dve.Fori(0, T) as t:
                ts(z[:, t, :], xs[:, t, :], mean[:, cols1(t)], rstd[:, cols1(t)], ALU.subtract,
                   ALU.mult).then_inc(d_z, 1)
                dve.wait_ge(d_z, t + 1)
                nc.vector.tensor_reduce(zam[:, cols1(t)], z[:, t, :], axis=AX.X, op=ALU.max,
                                        apply_absolute_value=True).then_inc(d_lk, 1)
            dve.wait_ge(d_lk, T)
            nc.vector.tensor_reduce(am[:, 0:1], zam[:, :], axis=AX.X, op=ALU.max).then_inc(d_am, 1)
            dve.wait_ge(d_amr, 1)
            link(ts(am[:, 2:3], am[:, 1:2], sig[:, 2, 0:1], 1.0 / QMAX, ALU.mult, ALU.mult))
            link(nc.vector.reciprocal(am[:, 3:4], am[:, 2:3]))
            link(ts(gu[:, :, :].rearrange("p w c -> p (w c)"), wsc[:, 0:2 * IC], am[:, 2:3], None, ALU.mult))

            def z_quant(k):
                at_least(dve, d_qb, k.t - 1)
                ts(zqa[:, k.p, :], z[:, k.t, :], am[:, 3:4], MAGIC, ALU.mult, ALU.add).then_inc(d_sc, 1)
                dve.wait_ge(d_sc, k.t + 1)
                ts(zqa[:, k.p, :], zqa[:, k.p, :], MAGIC + QMAX, MAGIC - QMAX - 1.0, ALU.min,
                   ALU.max).then_inc(d_q, 1)

            steps(dve, T, [(1, z_quant)])
            with dve.Fori(0, NB) as b:
                for c in range(IC):
                    r = IROWS[c]
                    dve.wait_ge(g_s, b * IC + (c + 1))
                    stt(hs[0:r, c, bass.ts(b, BLK)], ps[0:r, 2 * (c % 3) + 1, :], gu[0:r, 1, c:c + 1],
                        sil_g[0:r, c % 2, :], ALU.mult, ALU.mult).then_inc(g_h, 1)
                    dve.wait_ge(g_h, b * IC + (c + 1))
                    nc.vector.tensor_reduce(ham[0:r, c, bass.ts(b, 1)], hs[0:r, c, bass.ts(b, BLK)],
                                            axis=AX.X, op=ALU.max,
                                            apply_absolute_value=True).then_inc(g_am, 1)
            dve.wait_ge(g_am, NB * IC)
            nc.vector.memset(am[:, 4:5], 0.0).then_inc(e_lk, 1)
            link(nc.vector.tensor_reduce(zam[:, 0:IC - 1], ham[:, 0:IC - 1, :], axis=AX.X, op=ALU.max))
            link(nc.vector.memset(zam[:, IC - 1:IC], 0.0))
            link(nc.vector.tensor_reduce(zam[0:IROWS[-1], IC - 1:IC], ham[0:IROWS[-1], IC - 1, :],
                                         axis=AX.X, op=ALU.max))
            dve.wait_ge(e_lk, 1)
            nc.vector.tensor_reduce(am[:, 4:5], zam[:, 0:IC], axis=AX.X, op=ALU.max).then_inc(e_am, 1)
            dve.wait_ge(e_amr, 1)
            link(ts(am[:, 6:7], am[:, 5:6], sig[:, 2, 1:2], 1.0 / QMAX, ALU.mult, ALU.mult))
            nc.vector.reciprocal(am[:, 7:8], am[:, 6:7]).then_inc(e_sc, 1)
            link(ts(cdrow[:, :], wdrow[:, :], am[:, 6:7], None, ALU.mult))

            def last_quant(b):
                for c in range(IC):
                    r = IROWS[c]
                    dve.wait_ge(e_a, b * IC + (c + 1))
                    if c == 0:
                        at_least(dve, e_y, b * 4)
                    ts(hqa[0:r, c % 2, :], hqa[0:r, c % 2, :], MAGIC + QMAX, MAGIC - QMAX - 1.0, ALU.min,
                       ALU.max).then_inc(e_c, 1)
                    dve.wait_ge(e_c, b * IC + (c + 1))
                    ts(hq[0:r, c, :], hqa[0:r, c % 2, :], -MAGIC, None, ALU.add).then_inc(e_q, 1)
                for j in range(BLK // P):
                    p = j % 2
                    dve.wait_ge(e_y, b * 4 + (j + 1))
                    at_least(dve, e_out[p], b * 32 + (16 if j >= 2 else 0))
                    tt(oo[:, p, :], bank(6 + p)[:, 0:D], cdrow[:, :], ALU.mult).then_inc(e_f, 1)
                    dve.wait_ge(e_f, b * 4 + (j + 1))
                    tt(oo[:, p, :], oo[:, p, :], xs[:, b * 4 + j, :], ALU.add).then_inc(e_o, 1)

            each(dve, NB, last_quant)


def kernel(**inputs):
    import numpy as _np
    import concourse.bacc as _bacc
    from concourse import mybir as _mybir
    from concourse.bass_utils import run_bass_kernel_spmd as _run

    def blocks(w, n):
        d = w.shape[0]
        out = _np.zeros((n * d, n * d), w.dtype)
        for i in range(n):
            out[i * d:(i + 1) * d, i * d:(i + 1) * d] = w.T
        return out

    P = 128
    w12, w3 = _np.asarray(inputs['L0_ffn_w12']), _np.asarray(inputs['L0_ffn_w3'])
    E, H2, D = w12.shape
    up = w12.transpose(0, 2, 1).reshape(E, 2, P, H2)
    down = w3.transpose(0, 2, 1).reshape(E, 2, 2, P, D).transpose(0, 1, 3, 2, 4).reshape(E, 2, P, 2 * D)
    experts = _np.concatenate([up, down], axis=3).reshape(2 * E, P, H2 + 2 * D)
    heads = P // inputs['L1_xattn_Wk'].shape[0]
    laid = {
        'x': inputs['x'],
        'ctxT': _np.transpose(inputs['ctx_1024'], (0, 2, 1)),
        'wq0T': _np.transpose(inputs['L0_xattn_w_q']),
        'wk0T': _np.transpose(inputs['L0_xattn_w_k']),
        'wv0': inputs['L0_xattn_w_v'],
        'experts': experts,
        'gate_wT': _np.transpose(inputs['L0_ffn_gate_w']),
        'wk1': _np.tile(inputs['L1_xattn_Wk'], (1, heads)),
        'wq1': _np.tile(inputs['L1_xattn_Wq'], (1, heads)),
        'wv1_blocks': blocks(_np.asarray(inputs['L1_xattn_Wv']), heads),
        'clip_x': inputs['L1_ffn_clip_x'],
        'clip_down': inputs['L1_ffn_clip_down'],
        'w_gate': inputs['L1_ffn_w_gate'],
        'w_up': inputs['L1_ffn_w_up'],
        'w_down': inputs['L1_ffn_w_down'],
    }

    nc = _bacc.Bacc("TRN2", target_bir_lowering=False, num_devices=1)
    arrays, args = {}, []
    for name, value in laid.items():
        a = _np.ascontiguousarray(value)
        arrays[f"in_{name}"] = a
        args.append(nc.dram_tensor(f"in_{name}", a.shape, _mybir.dt.from_np(a.dtype), kind="ExternalInput").ap())
    shape = inputs['x'].shape
    res = nc.dram_tensor("out_x", shape, _mybir.dt.float32, kind="ExternalOutput").ap()
    block_program(nc, *args, res)
    r = _run(nc, [arrays], core_ids=[0])
    return r.results[0]["out_x"]
```

```python
import concourse.bass as bass
from concourse import mybir
from contextlib import ExitStack


class Tile:

    def __init__(self, t, parity, half):
        self.t, self.p, self.half = t, parity, half


def steps(eng, count, stages, peel=2):
    lead = max(a for a, _ in stages)
    end = (count - lead) // 2 * 2

    def straight(first, last):
        for t in range(first, last):
            for ahead, step in stages:
                if 0 <= t + ahead < count:
                    step(Tile(t + ahead, (t + ahead) % 2, (t + ahead) // 2))

    if end <= peel:
        straight(-lead, count)
        return
    straight(-lead, peel)
    with eng.Fori(peel // 2, end // 2) as i:
        for p in range(2):
            for ahead, step in stages:
                n = p + ahead
                step(Tile(i * 2 + n, n % 2, i + n // 2))
    straight(end, count)


def each(eng, count, body):
    body(0)
    with eng.Fori(1, count) as i:
        body(i)


def at_least(eng, sem, value):
    if not isinstance(value, int) or value > 0:
        eng.wait_ge(sem, value)


def block_program(nc, x, ctxT, wq0T, wk0T, wv0, experts, gate_wT, wk1, wq1, wv1_blocks,
                  clip_x, clip_down, w_gate, w_up, w_down, out):
    f32, f16, bf16, i32 = mybir.dt.float32, mybir.dt.float16, mybir.dt.bfloat16, mybir.dt.int32
    ALU, ACT, AX = mybir.AluOpType, mybir.ActivationFunctionType, mybir.AxisListType

    REDUCE_MAX = bass.bass_isa.ReduceOp.max

    P = 128
    T, S, D = x.shape
    DC = D // P
    E = gate_wT.shape[1]
    HALF = experts.shape[2]
    H = 2 * HALF * P // (3 * D)
    H2 = 2 * H
    HC = H // P
    TOPK = 2
    YB = 8
    NT = TOPK * T * S // P + E - 1
    DH = wk1.shape[0]
    NH = D // DH
    I = w_gate.shape[0]
    IC = -(-I // P)
    IROWS = [min(P, I - c * P) for c in range(IC)]
    BLK = 512
    NB = T * S // BLK
    QT = BLK // P
    EPS = 1e-5
    NEG = -1e30
    QMAX = 127.0
    MAGIC = 1.5 * 2.0 ** 23
    WS = 64.0
    SCALE0 = float(D) ** -0.5
    SCALE1 = float(DH) ** -0.5

    st = ExitStack()
    with st:
        def sb(name, shape, dt=f32):
            return st.enter_context(nc.sbuf_tensor(name, shape, dt))

        def sem(name):
            return st.enter_context(nc.semaphore(name))

        region_w = sb("region_w", [P, E * 2 * HALF])
        region_r = sb("region_r", [P, 6144])
        region_x = sb("region_x", [P, T * D])

        class Carve:

            def __init__(self, region, at=0):
                self.region, self.at = region, at

            def __call__(self, shape, dt=f32):
                n = 1
                for d in shape:
                    n *= d
                words = n if dt == f32 or dt == i32 else n // 2
                v = self.region[:, self.at:self.at + words]
                self.at += words
                assert self.at <= self.region.shape[1]
                v = v if dt == f32 else v.bitcast(dt)
                if len(shape) == 1:
                    return v
                names = "abcd"[:len(shape)]
                return v.rearrange("p (" + " ".join(names) + ") -> p " + " ".join(names),
                                   **dict(zip(names, shape)))

        xs = sb("xs", [P, T, D])
        stat = sb("stat", [P, T, 6])
        ln = sb("ln", [P, 8, T])
        mean, var_eps, root, rstd = ln[:, 0, :], ln[:, 1, :], ln[:, 2, :], ln[:, 3, :]
        ln_a, ln_b, ln_c = ln[:, 4, :], ln[:, 5, :], ln[:, 6, :]
        neg_mr = ln[:, 7, :]
        ident = sb("ident", [P, P])
        ident_b = sb("ident_b", [P, P], bf16)
        ident_h = sb("ident_h", [P, P], f16)
        ones = sb("ones", [P, P])
        causal = sb("causal", [P, P])
        below = sb("below", [P, P])
        key8 = sb("key8", [P, T, E])
        place_i = sb("place_i", [P, P], i32)
        tile_no_i = sb("tile_no_i", [P, NT], i32)
        tile_no = sb("tile_no", [P, NT])
        place_no = sb("place_no", [P, P], f16)
        token_i = sb("token_i", [P, T], i32)
        token = sb("token", [P, T])
        bdv = sb("bdv", [P, P])
        bdqs = sb("bdqs", [P, P])
        parity = sb("parity", [P, 2])
        blocks = sb("blocks", [P, P])
        wq1_s = sb("wq1_s", [DH, P])
        wk1_s = sb("wk1_s", [DH, P])
        gwT = sb("gwT", [P, DC, E])
        v1h = sb("v1h", [P, T, NH, DH + 1], f16)
        v1l = sb("v1l", [P, T, NH, DH + 1], f16)
        rs = sb("rs", [P, 8, T])
        xg_in = sb("xg_in", [P, 2, 2 * D], f16)
        slot_i = sb("slot_i", [P, T, TOPK], i32)
        tile_e = sb("tile_e", [P, NT], i32)
        source_i = sb("source_i", [P, NT], i32)
        take = Carve(region_r)
        wqT, wkT, wv, m0 = [take([DC, D]) for _ in range(4)]
        xn, xT, ctT = take([2, D]), take([2, D]), take([2, DC, P])
        gT, v0 = take([2, D]), take([2, D])
        sc, pr, prT = take([2, P]), take([2, P]), take([2, P])
        nmax = sb("nmax", [P, 2])
        psum_row = sb("psum_row", [P, 2])
        prcp = sb("prcp", [P, 2])
        take = Carve(region_x)
        raw = take([2, HALF])
        take = Carve(region_x)
        rows = take([T, 2 * D], f16)
        take = Carve(region_w)
        w_high, w_low = take([2 * E, HALF], f16), take([2 * E, HALF], f16)

        def w12_of(w, e):
            return w[:, bass.ts(e, 2), 0:H2]

        def w3_of(w, e):
            return w[:, bass.ts(e, 2), H2:HALF]

        take = Carve(region_r)
        rsc = take([T, E])
        rt = take([8, T, E])
        routed = take([NT, E])
        place_hot, tile_hot = take([T * TOPK, P], f16), take([T * TOPK, NT], f16)
        at_place_h = take([T * TOPK], f16)
        take = Carve(region_r)
        sil = take([2, BLK])
        hid = take([2, BLK])
        xgT = take([2, 2 * D], f16)
        hTh, hTl = take([2, BLK], f16), take([2, BLK], f16)
        y_out = take([2, D])
        w3_now = [[take([2, 2 * D], f16) for _ in range(2)] for _ in range(2)]
        take = Carve(region_x)
        w12_now = [[take([DC, H2], f16) for _ in range(2)] for _ in range(2)]
        take = Carve(region_r)
        y_in = take([YB, TOPK, D])
        take = Carve(region_w)
        k1s = take([2, DC, P])
        qzh = [take([4, DC, P], f16) for _ in range(2)]
        qzl = [take([4, DC, P], f16) for _ in range(2)]
        kh, kl = take([2, DC, 2, P], f16), take([2, DC, 2, P], f16)
        khl = [take([2, DC, P], f16) for _ in range(2)]
        vch, vcl = take([2, NH, DH + 1], f16), take([2, NH, DH + 1], f16)
        pr1 = take([2, 4 * P])
        pTh, pTl = take([2, 4 * P], f16), take([2, 4 * P], f16)
        o1 = take([2, NH, DH])
        nm1 = sb("nm1", [P, 4, 4])
        rc1 = sb("rc1", [P, NH])
        take = Carve(region_w, 8192)
        wraw, wqb = take([2, IC, D]), take([2, IC, D], bf16)
        wdraw, wdqb = take([DC, I]), take([DC, I], bf16)
        diag = take([DC, P])
        take = Carve(region_w)
        hs = take([IC, T * S])
        zqT = take([DC, T * S], bf16)
        hq = [take([IC, BLK], bf16) for _ in range(2)]
        hqi = take([2, BLK], bf16)
        hqa = take([IC, BLK])
        sil_g = take([2, BLK])
        take = Carve(region_r)
        zqa = take([2, QT * D])
        zqi, zqb = take([2, QT * D], bf16), take([2, QT, D], bf16)
        oo = take([QT, D])
        take = Carve(region_x)
        z = take([T, D])
        wmax = sb("wmax", [P, 2 * IC + DC])
        wsc = sb("wsc", [P, 2 * IC + DC])
        wrc = sb("wrc", [P, 2 * IC + DC])
        wguT = sb("wguT", [P, 2, DC, IC * P], bf16)
        wdT = sb("wdT", [P, IC, D], bf16)
        wdrow = sb("wdrow", [P, D])
        cdrow = sb("cdrow", [P, D])
        clips = sb("clips", [P, 2])
        sig = sb("sig", [P, 4, 2])
        zam = sb("zam", [P, T])
        am = sb("am", [P, 8])
        gu = sb("gu", [P, 2, IC])
        ham = sb("ham", [P, IC, NB])

        rows_kept = nc.dram_tensor("rows_kept", [T * P, 2 * D], f16).ap()
        rows_back = nc.dram_tensor("rows_back", [NT * P, D], f32).ap()

        ps = st.enter_context(nc.psum_tensor("ps", [P, 8, 512], f32))

        def bank(n):
            return ps[:, n, :]

        x_loaded = [sem(f"x_loaded{n}") for n in range(4)]
        fold_loaded = sem("fold_loaded")
        w_loaded = sem("w_loaded")
        bd_loaded = sem("bd_loaded")
        l1w_in = [sem(f"l1w_in{n}") for n in range(3)]
        ctx_loaded = [sem("ctx_loaded0"), sem("ctx_loaded1")]
        const_ready = sem("const_ready")
        pool_step = sem("pool_step")
        dchain = sem("dchain")
        sig_exp = sem("sig_exp")
        l1_scales, l1_scaled, l1_clamped = sem("l1_scales"), sem("l1_scaled"), sem("l1_clamped")
        l1q_ready = sem("l1q_ready")
        l1_diag = sem("l1_diag")
        l1t_done = sem("l1t_done")
        l1t_copied = sem("l1t_copied")
        ln_ve = sem("ln_ve")
        ln_root = sem("ln_root")
        a_xn, a_tr, a_trc, a_qk, a_qkc, a_v, a_vc, a_vl = [
            sem(n) for n in ("a_xn", "a_tr", "a_trc", "a_qk", "a_qkc", "a_v", "a_vc", "a_vl")]
        folded, folded_c = sem("folded"), sem("folded_c")
        a_s, a_sm, a_e, a_pt, a_ptc, a_o, a_fin, a_lk = [
            sem(n) for n in ("a_s", "a_sm", "a_e", "a_pt", "a_ptc", "a_o", "a_fin", "a_lk")]
        b_xn, b_tr, b_hi, b_f, b_lo, b_r, b_rc = [
            sem(n) for n in ("b_xn", "b_tr", "b_hi", "b_f", "b_lo", "b_r", "b_rc")]
        r_d, r_e, r_one, r_rank, r_slot, r_hot, r_at, r_source = [
            sem(n) for n in ("r_d", "r_e", "r_one", "r_rank", "r_slot", "r_hot", "r_at", "r_source")]
        w_in = [sem("w_in0"), sem("w_in1")]
        w_hi, w_lo = sem("w_hi"), sem("w_lo")
        kept = sem("kept")
        m_in = [sem("m_in0"), sem("m_in1")]
        m_back = [sem("m_back0"), sem("m_back1")]
        m_w12, m_w3, m_tr, m_trc, m_u, m_s, m_h, m_hh, m_hl, m_y, m_yc = [
            sem(n) for n in ("m_w12", "m_w3", "m_tr", "m_trc", "m_u", "m_s", "m_h", "m_hh", "m_hl", "m_y", "m_yc")]
        g_in = [sem(f"g_in{n}") for n in range(YB)]
        c_kin = [sem("c_kin0"), sem("c_kin1")]
        g_one, g_two = sem("g_one"), sem("g_two")
        st_done = sem("st_done")
        c_zero = sem("c_zero")
        c_xn, c_tr, c_trc, c_q, c_qc, c_ql, c_kh, c_kl, c_k, c_vv = [
            sem(n) for n in ("c_xn", "c_tr", "c_trc", "c_q", "c_qc", "c_ql", "c_kh", "c_kl", "c_k", "c_vv")]
        c_s, c_sm, c_e, c_t, c_tc, c_tl, c_v, c_fin = [
            sem(n) for n in ("c_s", "c_sm", "c_e", "c_t", "c_tc", "c_tl", "c_v", "c_fin")]
        d_rs, d_z, d_za, d_am, d_amr, d_sc, d_lk, d_q, d_qb, d_tr, d_trc = [
            sem(n) for n in ("d_rs", "d_z", "d_za", "d_am", "d_amr", "d_sc", "d_lk", "d_q", "d_qb", "d_tr",
                             "d_trc")]
        g_p, g_s, g_h, g_am = [sem(n) for n in ("g_p", "g_s", "g_h", "g_am")]
        e_am, e_amr, e_sc, e_a, e_c, e_q, e_y, e_o = [
            sem(n) for n in ("e_am", "e_amr", "e_sc", "e_a", "e_c", "e_q", "e_y", "e_o")]
        e_out = [sem(f"e_out{n}") for n in range(QT)]
        st0, st2, a_f1, a_f2, c_f1, c_f2, c_f3, e_f = [
            sem(n) for n in ("st0", "st2", "a_f1", "a_f2", "c_f1", "c_f2", "c_f3", "e_f")]

        NBD = P // DH
        EARLY = 2
        LAST = Tile(NB - 1, (NB - 1) % 2, (NB - 1) // 2)

        def cols(t):
            return bass.ts(t, P)

        pieces = [[(wraw[0:IROWS[c], w, c, :], wqb[0:IROWS[c], w, c, :], IROWS[c], w * IC + c)
                   for c in range(IC)] for w in range(2)]
        pieces.append([(wdraw[:, c, :], wdqb[:, c, :], P, 2 * IC + c) for c in range(DC)])

        block = st.enter_context(nc.Block())

        @block.sync
        def _(sp):
            x_v = x.rearrange("b s d -> s b d")
            for dst, src in ((wqT, wq0T), (wkT, wk0T), (wv, wv0)):
                sp.dma_start(dst, src.rearrange("(c p) h -> p c h", p=P)).then_inc(w_loaded, 16)
            for n in range(4):
                some = slice(n * T // 4, (n + 1) * T // 4)
                sp.dma_start(xs[:, some, :], x_v[:, some, :]).then_inc(x_loaded[n], 16)

            def load_weights(k):
                at_least(sp, w_lo, k.t - 1)
                sp.dma_start(raw[:, k.p, :], experts[k.t, :, :]).then_inc(w_in[k.p], 16)

            steps(sp, T, [(2, load_weights)])

            def keep(k):
                sp.wait_ge(b_lo, k.t + 1)
                sp.dma_start(rows_kept[bass.ts(k.t, P), :], rows[:, k.t, :]).then_inc(kept, 16)

            steps(sp, T, [(0, keep)])

            def rows_out(k):
                sp.wait_ge(m_yc, k.t + 1)
                sp.dma_start(rows_back[bass.ts(k.t, P), :], y_out[:, k.p, :]).then_inc(m_back[k.p], 16)

            steps(sp, NT, [(0, rows_out)])

            sp.wait_ge(m_w3, NT)
            full = I // P
            for n, src in enumerate((w_gate, w_up)):
                sp.dma_start(wraw[:, n, 0:full, :],
                             src[0:full * P, :].rearrange("(c p) d -> p c d", p=P)).then_inc(l1w_in[n], 16)
                sp.dma_start(wraw[0:I - full * P, n, full, :], src[full * P:I, :]).then_inc(l1w_in[n], 16)
            sp.dma_start(wdraw[:, :, :], w_down.rearrange("(c p) i -> p c i", p=P)).then_inc(l1w_in[2], 16)

            def load_keys(k):
                if isinstance(k.t, int) and k.t == 0:
                    sp.wait_ge(m_w3, NT)
                at_least(sp, c_k, k.t - 1)
                sp.dma_start(k1s[:, k.p, :, :],
                             ctxT[k.t, :, :].rearrange("(c p) s -> p c s", p=P)).then_inc(c_kin[k.p], 16)

            steps(sp, T, [(2, load_keys)])

            def store(b):
                for j in range(QT):
                    sp.wait_ge(e_o, b * QT + (j + 1))
                    sp.dma_start(out[b * QT + j, :, :], oo[:, j, :]).then_inc(e_out[j], 16)

            each(sp, NB, store)
            for j in range(QT):
                sp.wait_ge(e_out[j], 16 * NB)

        @block.gpsimd
        def _(pool):
            nc.gpsimd.memset(ident[:, :], 0.0).then_inc(pool_step, 1)
            nc.gpsimd.memset(causal[:, :], 0.0).then_inc(pool_step, 1)
            nc.gpsimd.memset(v1h[:, :, :, DH:DH + 1], 1.0)
            nc.gpsimd.memset(v1l[:, :, :, DH:DH + 1], 0.0)
            nc.gpsimd.memset(ones[:, :], 1.0).then_inc(pool_step, 1)
            for j in range(E):
                nc.gpsimd.memset(key8[:, :, j:j + 1], float(E - j))
            nc.gpsimd.iota(tile_no_i[:, :], [[1, NT]], base=0, channel_multiplier=0).then_inc(pool_step, 1)
            nc.gpsimd.iota(token_i[:, :], [[P, T]], base=0, channel_multiplier=1).then_inc(pool_step, 1)
            nc.gpsimd.iota(place_i[:, :], [[1, P]], base=0, channel_multiplier=0).then_inc(pool_step, 1)
            pool.wait_ge(pool_step, 6)
            nc.gpsimd.affine_select(out=ident[:, :], in_=ident[:, :], compare_op=ALU.not_equal, fill=1.0,
                                    base=0, pattern=[[-1, P]], channel_multiplier=1).then_inc(pool_step, 1)
            nc.gpsimd.affine_select(out=causal[:, :], in_=causal[:, :], compare_op=ALU.is_ge, fill=NEG,
                                    base=0, pattern=[[-1, P]], channel_multiplier=1).then_inc(pool_step, 1)
            nc.gpsimd.affine_select(out=below[:, :], in_=ones[:, :], compare_op=ALU.is_gt, fill=0.0,
                                    base=0, pattern=[[1, P]], channel_multiplier=-1).then_inc(pool_step, 1)
            nc.gpsimd.affine_select(out=blocks[:, :], in_=ones[:, :], compare_op=ALU.is_ge, fill=0.0,
                                    base=0, pattern=[[-DH, P // DH], [0, DH]],
                                    channel_multiplier=1).then_inc(pool_step, 1)
            pool.wait_ge(pool_step, 10)
            nc.gpsimd.affine_select(out=blocks[:, :], in_=blocks[:, :], compare_op=ALU.is_ge, fill=0.0,
                                    base=DH - 1, pattern=[[DH, P // DH], [0, DH]],
                                    channel_multiplier=-1)
            nc.gpsimd.tensor_copy(tile_no[:, :], tile_no_i[:, :])
            nc.gpsimd.tensor_copy(token[:, :], token_i[:, :])
            nc.gpsimd.tensor_copy(place_no[:, :], place_i[:, :])
            nc.gpsimd.tensor_copy(ident_h[:, :], ident[:, :])
            nc.gpsimd.tensor_copy(ident_b[:, :], ident[:, :]).then_inc(const_ready, 1)

            def load_context(k):
                at_least(pool, a_s, k.t - 1)
                pool.dma_start(ctT[:, k.p, :, :],
                             ctxT[k.t, :, :].rearrange("(c p) s -> p c s", p=P)).then_inc(ctx_loaded[k.p], 16)

            steps(pool, T, [(2, load_context)])

            pool.wait_ge(r_source, 1)
            pool.wait_ge(kept, 16 * T)
            for n in range(NT):
                if n >= 2:
                    pool.wait_ge(m_tr, n - 1)
                pool.indirect_dma_start(
                    out=xg_in[:, n % 2, :], in_=rows_kept[:, :], out_offset=None,
                    in_offset=bass.IndirectOffsetOnAxis(ap=source_i[:, n:n + 1], axis=0)
                ).then_inc(m_in[n % 2], 16)
            for p in range(2):
                pool.wait_ge(m_back[p], 16 * ((NT + 1 - p) // 2))
            for t in range(T):
                if t >= YB:
                    pool.wait_ge(g_two, t - YB + 1)
                for j in range(TOPK):
                    pool.indirect_dma_start(
                        out=y_in[:, t % YB, j, :], in_=rows_back[:, :], out_offset=None,
                        in_offset=bass.IndirectOffsetOnAxis(ap=slot_i[:, t, j:j + 1], axis=0)
                    ).then_inc(g_in[t % YB], 16)

            def keys(k):
                pool.wait_ge(c_kin[k.p], (k.half + 1) * 16)
                if isinstance(k.t, int) and k.t < 2:
                    pool.wait_ge(m_w3, NT)
                else:
                    pool.wait_ge(c_s, (k.t - 1) * 4)
                nc.gpsimd.tensor_tensor(khl[k.p][:, 0, :, :], k1s[:, k.p, :, :],
                                        ones[:, :].unsqueeze(1).to_broadcast([P, DC, P]),
                                        ALU.mult).then_inc(c_kh, 1)
                pool.wait_ge(c_kh, k.t + 1)
                nc.gpsimd.tensor_tensor(khl[k.p][:, 1, :, :], k1s[:, k.p, :, :], khl[k.p][:, 0, :, :],
                                        ALU.subtract).then_inc(c_kl, 1)
                pool.wait_ge(c_kl, k.t + 1)
                for n, to in enumerate((kh, kl)):
                    for par in range(2):
                        ins = nc.gpsimd.tensor_tensor(
                            to[:, k.p, :, par, :], khl[k.p][:, n, :, :],
                            parity[:, par:par + 1].unsqueeze(2).to_broadcast([P, DC, P]), ALU.mult)
                ins.then_inc(c_k, 1)

            def values(k):
                if isinstance(k.t, int) and k.t < 2:
                    pool.wait_ge(m_w3, NT)
                else:
                    pool.wait_ge(c_v, (k.t - 1) * 4)
                nc.gpsimd.tensor_copy(vch[:, k.p, :, :], v1h[:, k.t, :, :])
                nc.gpsimd.tensor_copy(vcl[:, k.p, :, :], v1l[:, k.t, :, :]).then_inc(c_vv, 1)

            def add(k):
                pool.wait_ge(c_f2, k.t + 1)
                nc.gpsimd.tensor_tensor(xs[:, k.t, :], xs[:, k.t, :],
                                        o1[:, k.p, :, :].rearrange("p h e -> p (h e)"),
                                        ALU.add).then_inc(c_f3, 1)

            steps(pool, T, [(2, values), (0, add), (3, keys)])

            pool.wait_ge(d_am, 1)
            nc.gpsimd.partition_all_reduce(am[:, 1:2], am[:, 0:1], P, REDUCE_MAX).then_inc(d_amr, 1)

            pool.wait_ge(e_am, 1)
            nc.gpsimd.partition_all_reduce(am[:, 5:6], am[:, 4:5], P, REDUCE_MAX).then_inc(e_amr, 1)

            def residual(b):
                for j in range(QT):
                    pool.wait_ge(e_f, b * QT + (j + 1))
                    nc.gpsimd.tensor_tensor(oo[:, j, :], oo[:, j, :], xs[:, b * QT + j, :],
                                            ALU.add).then_inc(e_o, 1)

            each(pool, NB, residual)

        @block.tensor
        def _(pe):
            mm = nc.tensor.matmul
            pe.wait_ge(const_ready, 1)
            pe.wait_ge(w_loaded, 48)
            pe.wait_ge(fold_loaded, 32)
            for m in range(DC):
                for c in range(DC):
                    mm(bank(0)[:, m * D:(m + 1) * D], wqT[:, c, m * P:(m + 1) * P], wkT[:, c, :],
                       start=(c == 0), stop=(c == DC - 1))
            mm(bank(1)[:, 0:P], wq1_s[:, :], wk1_s[:, :], start=True, stop=True).then_inc(folded, 1)
            pe.wait_ge(folded_c, 1)
            pe.wait_ge(bd_loaded, 16 * 4)

            def transposes(k):
                pe.wait_ge(a_xn, k.t + 1)
                for c in range(DC):
                    last = nc.tensor.transpose(bank(0)[:, c * P:(c + 1) * P],
                                               xn[:, k.p, c * P:(c + 1) * P], ident[:, :])
                last.then_inc(a_tr, 1)

            def projections(k):
                pe.wait_ge(a_trc, k.t + 1)
                for m in range(DC):
                    for c in range(DC):
                        last = mm(bank(2 + k.p)[:, m * P:(m + 1) * P], m0[:, c, m * P:(m + 1) * P],
                                  xT[:, k.p, c * P:(c + 1) * P], start=(c == 0), stop=(c == DC - 1))
                last.then_inc(a_qk, 1)
                pe.wait_ge(ctx_loaded[k.p], (k.half + 1) * 16)
                for c in range(DC):
                    mm(bank(4 + k.p)[:, 0:D], ctT[:, k.p, c, :], wv[:, c, :],
                       start=(c == 0), stop=(c == DC - 1))
                for c in range(DC):
                    last = mm(bank(4 + k.p)[:, D + c * P:D + (c + 1) * P], ctT[:, k.p, c, :], bdv[:, :],
                              start=True, stop=True)
                last.then_inc(a_v, 1)

            def scores(k):
                pe.wait_ge(a_qkc, k.t + 1)
                for c in range(DC):
                    last = mm(bank(6 + k.p)[:, D:D + P], gT[:, k.p, c * P:(c + 1) * P],
                              ctT[:, k.p, c, :], start=(c == 0), stop=(c == DC - 1))
                last.then_inc(a_s, 1)

            def prob_transpose(k):
                pe.wait_ge(a_e, k.t + 1)
                nc.tensor.transpose(bank(6 + k.p)[:, D + P:D + 2 * P], pr[:, k.p, :],
                                    ident[:, :]).then_inc(a_pt, 1)

            def attend(k):
                pe.wait_ge(a_ptc, k.t + 1)
                pe.wait_ge(a_vl, k.t + 1)
                at_least(pe, a_fin, k.t)
                mm(bank(1)[:, 0:D], prT[:, k.p, :], v0[:, k.p, :], start=True,
                   stop=True).then_inc(a_o, 1)

            steps(pe, T, [(0, attend), (2, projections), (1, prob_transpose), (3, transposes), (2, scores)])

            pe.wait_ge(a_fin, T)

            def b_transposes(k):
                pe.wait_ge(b_xn, k.t + 1)
                for c in range(DC):
                    last = nc.tensor.transpose(bank(k.p)[:, c * P:(c + 1) * P],
                                               xn[:, k.p, c * P:(c + 1) * P], ident[:, :])
                last.then_inc(b_tr, 1)

            def router(k):
                pe.wait_ge(b_f, k.t + 1)
                at_least(pe, b_rc, k.t - 1)
                for c in range(DC):
                    last = mm(bank(2 + k.p)[:, 0:E], xT[:, k.p, c * P:(c + 1) * P], gwT[:, c, :],
                              start=(c == 0), stop=(c == DC - 1))
                last.then_inc(b_r, 1)

            steps(pe, T, [(1, b_transposes), (0, router)])

            pe.wait_ge(r_one, 1)
            chosen = rt[:, 4, :, :].rearrange("p t e -> p (t e)")
            mm(bank(4)[:, 0:T * E], below[:, :], chosen, start=True, stop=True)
            mm(bank(4)[:, T * E:2 * T * E], ones[:, :], chosen, start=True, stop=True).then_inc(r_rank, 1)

            for n in range(T * TOPK):
                if n % (4 * TOPK) == 0:
                    pe.wait_ge(r_hot, n // (4 * TOPK) + 1)
                last = mm(bank(5)[:, 0:NT], place_hot[:, n, :], tile_hot[:, n, :],
                          start=(n == 0), stop=(n == T * TOPK - 1))
            last.then_inc(r_at, 1)

            def m_transposes(k):
                pe.wait_ge(m_in[k.p], (k.half + 1) * 16)
                bk = bank(0).bitcast(f16)
                for c in range(2 * DC):
                    last = nc.tensor.transpose(bk[:, c * P:(c + 1) * P],
                                               xg_in[:, k.p, c * P:(c + 1) * P], ident_h[:, :])
                last.then_inc(m_tr, 1)

            def up(k):
                pe.wait_ge(m_trc, k.t + 1)
                pe.wait_ge(m_w12, k.t + 1)
                high, low = w12_now[k.p]
                terms = [(a, w, c) for c in range(DC) for a, w in ((0, high), (0, low), (DC, high))]
                for n in range(2 * HC):
                    for m, (a, w, c) in enumerate(terms):
                        last = mm(bank(1 + 2 * k.p + n // HC)[:, n % HC * P:(n % HC + 1) * P],
                                  w[:, c, n * P:(n + 1) * P], xgT[:, k.p, (a + c) * P:(a + c + 1) * P],
                                  start=(m == 0), stop=(m == len(terms) - 1))
                last.then_inc(m_u, 1)

            def down(k):
                pe.wait_ge(m_w3, k.t + 1)
                pe.wait_ge(m_hl, k.t + 1)
                high, low = w3_now[k.p]
                terms = [(a, w, c) for c in range(HC) for a, w in ((hTh, high), (hTh, low), (hTl, high))]
                for m, (a, w, c) in enumerate(terms):
                    last = mm(bank(6 + k.p)[:, 0:D], a[:, k.p, c * P:(c + 1) * P],
                              w[:, c // 2, c % 2 * D:(c % 2 + 1) * D],
                              start=(m == 0), stop=(m == len(terms) - 1))
                last.then_inc(m_y, 1)

            steps(pe, NT, [(1, up), (2, m_transposes), (0, down)])

            n = 0
            for w in range(2):
                for dk in range(DC):
                    if dk == 0:
                        pe.wait_ge(l1q_ready, w + 1)
                    if n >= 2:
                        pe.wait_ge(l1t_copied, n - 1)
                    bk = bank(n % 2).bitcast(bf16)
                    for c in range(IC):
                        last = nc.tensor.transpose(bk[:, c * P:c * P + IROWS[c]],
                                                   wqb[0:IROWS[c], w, c, dk * P:(dk + 1) * P],
                                                   ident_b[0:IROWS[c], 0:IROWS[c]])
                    last.then_inc(l1t_done, 1)
                    n += 1
            pe.wait_ge(l1q_ready, 3)
            for half in range(2):
                pe.wait_ge(l1t_copied, n - 1)
                bk = bank(n % 2).bitcast(bf16)
                for c in range(half * IC // 2, (half + 1) * IC // 2):
                    for dk in range(DC):
                        o = (c - half * IC // 2) * D + dk * P
                        last = nc.tensor.transpose(bk[0:IROWS[c], o:o + P],
                                                   wdqb[:, dk, c * P:c * P + IROWS[c]], ident_b[:, :])
                last.then_inc(l1t_done, 1)
                n += 1
            pe.wait_ge(l1t_copied, n)
            pe.wait_ge(l1_diag, 1)
            for dk in range(DC):
                last = mm(bank(0)[:, dk * P:(dk + 1) * P], ones[:, :], diag[:, dk, :], start=True, stop=True)
            last.then_inc(l1t_done, 1)
            pe.wait_ge(l1t_copied, n + 1)

            def c_transposes(k):
                pe.wait_ge(c_xn, k.t + 1)
                at_least(pe, c_f2, k.t - 2)
                for c in range(DC):
                    last = nc.tensor.transpose(bank(1 - k.p)[:, c * P:(c + 1) * P],
                                               xn[:, 0, c * P:(c + 1) * P], ident[:, :])
                last.then_inc(c_tr, 1)

            def c_project(k):
                pe.wait_ge(c_trc, k.t + 1)
                mm(bank(1 - k.p)[:, 0:D], bdqs[:, :], xT[:, 0, 0:D], start=True,
                   stop=True).then_inc(c_q, 1)

            def c_scores(s):
                def step(k):
                    if s == 0:
                        pe.wait_ge(c_ql, k.t + 1)
                        pe.wait_ge(c_k, k.t + 1)
                    for c in range(DC):
                        terms = ((qzh, kh), (qzh, kl), (qzl, kh))
                        for m, (a, b) in enumerate(terms):
                            last = mm(bank(4 + s)[:, 2 * c * P:(2 * c + 2) * P], a[k.p][:, s, c, :],
                                      b[:, k.p, c, :, :].rearrange("p a s -> p (a s)"),
                                      start=(m == 0), stop=(m == len(terms) - 1))
                    last.then_inc(c_s, 1)
                return step

            def c_ptrans(s):
                def step(k):
                    pe.wait_ge(c_e, k.t * 4 + (s + 1))
                    for j in range(4):
                        last = nc.tensor.transpose(bank(2 + s % 2)[:, j * P:(j + 1) * P],
                                                   pr1[:, s % 2, j * P:(j + 1) * P], ident[:, :])
                    last.then_inc(c_t, 1)
                return step

            def c_values(s):
                def step(k):
                    pe.wait_ge(c_tl, k.t * 4 + (s + 1))
                    if s == 0:
                        pe.wait_ge(c_ql, min(T, k.t + 2) if isinstance(k.t, int) else k.t + 2)
                        pe.wait_ge(c_vv, k.t + 1)
                    for c in range(DC):
                        for par in range(2):
                            h = c * NBD + 2 * s + par
                            at = (2 * c + par) * P
                            terms = ((pTh, vch), (pTh, vcl), (pTl, vch))
                            for m, (a, v) in enumerate(terms):
                                last = mm(bank(k.p)[:, h * (DH + 1):(h + 1) * (DH + 1)],
                                          a[:, s % 2, at:at + P], v[:, k.p, h, :],
                                          start=(m == 0), stop=(m == len(terms) - 1))
                    last.then_inc(c_v, 1)
                return step

            pe.wait_ge(st_done, 1)
            stages = []
            for s in range(4):
                stages.append(((s + 3) // 4, c_scores((s + 3) % 4)))
                stages.append(((s + 1) // 4, c_ptrans((s + 1) % 4)))
                if s == 1:
                    stages.append((2, c_transposes))
                if s == 2:
                    stages.append((2, c_project))
                stages.append((0, c_values(s)))
            steps(pe, T, stages)

            def d_transposes(k):
                pe.wait_ge(d_qb, k.t + 1)
                at_least(pe, d_trc, k.t - 1)
                bk = bank(6 + k.p).bitcast(bf16)
                for c in range(DC):
                    for i in range(QT):
                        last = nc.tensor.transpose(bk[:, (c * QT + i) * P:(c * QT + i + 1) * P],
                                                   zqb[:, k.p, i, c * P:(c + 1) * P], ident_b[:, :])
                last.then_inc(d_tr, 1)

            pe.wait_ge(c_fin, T)
            steps(pe, NB - 1, [(0, d_transposes)])

            def gate_up(b, chunks=range(IC)):
                pe.wait_ge(d_trc, b + 1)
                for c in chunks:
                    r = IROWS[c]
                    if c < IC - 1:
                        back = c - 1 if c == IC - 2 else c - 2
                        at_least(pe, g_h, b * IC + back)
                    for w in range(2):
                        for dk in range(DC):
                            last = mm(ps[0:r, 2 * (c % 3) + w, :], wguT[:, w, dk, c * P:c * P + r],
                                      zqT[:, dk, bass.ts(b, BLK)], start=(dk == 0), stop=(dk == DC - 1))
                    last.then_inc(g_p, 1)

            gate_up(0, range(EARLY))
            d_transposes(LAST)
            gate_up(0, range(EARLY, IC))
            with pe.Fori(1, NB) as b:
                gate_up(b)
            pe.wait_ge(g_h, NB * IC)

            def last_down(k):
                b, hq_at = k.t, hq[k.p]
                pe.wait_ge(e_q, (b + 1) * IC)
                for j in range(QT):
                    at_least(pe, e_f, b * QT + (j - QT + 1))
                    for c in range(IC):
                        r = IROWS[c]
                        last = mm(bank(4 + j)[:, 0:D], hq_at[0:r, c, j * P:(j + 1) * P], wdT[0:r, c, :],
                                  start=(c == 0), stop=(c == IC - 1))
                    last.then_inc(e_y, 1)

            steps(pe, NB, [(0, last_down)])

        @block.scalar
        def _(act):
            for dst, src in ((wq1_s[:, :], wq1), (wk1_s[:, :], wk1)):
                act.dma_start(dst, src).then_inc(fold_loaded, 16)
            for dst, src in ((bdv[:, :], wv1_blocks),
                             (gwT[:, :, :], gate_wT.rearrange("(c p) e -> p c e", p=P))):
                act.dma_start(dst, src).then_inc(bd_loaded, 16)
            for n, src in enumerate((clip_x, clip_down)):
                act.dma_start(clips[:, n:n + 1], src.rearrange("(a n) -> a n", a=1).to_broadcast([P, 1])
                              ).then_inc(bd_loaded, 16)
            act.wait_ge(folded, 1)
            act.copy(m0, bank(0).rearrange("p (c d) -> p c d", d=D)).then_inc(folded_c, 1)

            def roots(n):
                act.wait_ge(ln_ve, n + 1)
                act.activation(root, var_eps, ACT.Sqrt).then_inc(ln_root, 1)

            roots(0)

            def transposed(k):
                act.wait_ge(a_tr, k.t + 1)
                at_least(act, a_qk, k.t - 1)
                act.copy(xT[:, k.p, :], bank(0)[:, 0:D]).then_inc(a_trc, 1)

            def qk_copy(k):
                act.wait_ge(a_qk, k.t + 1)
                act.copy(gT[:, k.p, :], bank(2 + k.p)[:, 0:D]).then_inc(a_qkc, 1)

            def v_copy(k):
                act.wait_ge(a_v, k.t + 1)
                act.copy(v0[:, k.p, :], bank(4 + k.p)[:, 0:D])
                act.copy(v1h[:, k.t, :, 0:DH],
                         bank(4 + k.p)[:, D:2 * D].rearrange("p (h e) -> p h e", e=DH)).then_inc(a_vc, 1)

            def exps(k):
                act.wait_ge(a_sm, k.t + 1)
                at_least(act, a_f1, k.t - 1)
                act.activation(pr[:, k.p, :], sc[:, k.p, :], ACT.Exp, bias=nmax[:, k.p:k.p + 1],
                               accum_out=psum_row[:, k.p:k.p + 1]).then_inc(a_e, 1)

            def pt_copy(k):
                act.wait_ge(a_pt, k.t + 1)
                act.copy(prT[:, k.p, :], bank(6 + k.p)[:, D + P:D + 2 * P]).then_inc(a_ptc, 1)

            act.wait_ge(const_ready, 1)
            nc.scalar.preload_act_table(ACT.Exp)
            act.wait_ge(bd_loaded, 16 * 4)
            act.activation(sig[:, 0, :], clips[:, :], ACT.Exp, scale=-1.0).then_inc(sig_exp, 1)

            def weights_high(k):
                act.wait_ge(w_in[k.p], (k.half + 1) * 16)
                act.mul(w_high[:, k.t, :], raw[:, k.p, :], WS).then_inc(w_hi, 1)

            steps(act, T, [(1, exps), (2, qk_copy), (2, v_copy), (1, pt_copy), (3, transposed),
                           (2, weights_high)])

            roots(1)

            nc.scalar.preload_act_table(ACT.Exp)

            def b_high(k):
                act.wait_ge(b_xn, k.t + 1)
                act.copy(rows[:, k.t, 0:D], xn[:, k.p, :]).then_inc(b_hi, 1)
                act.wait_ge(b_tr, k.t + 1)
                at_least(act, b_r, k.t - 1)
                act.copy(xT[:, k.p, 0:D], bank(k.p)[:, 0:D]).then_inc(b_f, 1)

            steps(act, T, [(0, b_high)])
            act.wait_ge(r_d, 1)
            act.activation(rs[:, 2, :], rs[:, 3, :], ACT.Exp).then_inc(r_e, 1)

            nc.scalar.preload_act_table(ACT.Silu)

            def m_tcopy(k):
                act.wait_ge(m_tr, k.t + 1)
                act.copy(xgT[:, k.p, :], bank(0).bitcast(f16)[:, 0:2 * D]).then_inc(m_trc, 1)

            def silu(k):
                act.wait_ge(m_u, k.t + 1)
                act.activation(sil[:, k.p, :], bank(1 + 2 * k.p), ACT.Silu, scale=1.0 / WS).then_inc(m_s, 1)

            def high(k):
                act.wait_ge(m_h, k.t + 1)
                act.copy(hTh[:, k.p, :], hid[:, k.p, :]).then_inc(m_hh, 1)

            steps(act, NT, [(1, silu), (2, m_tcopy), (1, high)])

            def scale_piece(n):
                act.wait_ge(l1_scales, n + 1)
                for src, _, r, c in pieces[n]:
                    last = act.activation(src, src, ACT.Copy, bias=MAGIC, scale=wrc[0:r, c:c + 1])
                last.then_inc(l1_scaled, 1)

            def whole_piece(n):
                act.wait_ge(l1_clamped, n + 1)
                for src, dst, _, _ in pieces[n]:
                    last = act.activation(dst, src, ACT.Copy, bias=-MAGIC, scale=1.0)
                last.then_inc(l1q_ready, 1)

            def copy_gate_up(w):
                for dk in range(DC):
                    n = w * DC + dk
                    act.wait_ge(l1t_done, n + 1)
                    act.copy(wguT[:, w, dk, 0:I], bank(n % 2).bitcast(bf16)[:, 0:I]).then_inc(l1t_copied, 1)

            def copy_down():
                for half in range(2):
                    n = 2 * DC + half
                    act.wait_ge(l1t_done, n + 1)
                    bk = bank(n % 2).bitcast(bf16)
                    for c in range(half * IC // 2, (half + 1) * IC // 2):
                        o = (c - half * IC // 2) * D
                        last = act.copy(wdT[0:IROWS[c], c, :], bk[0:IROWS[c], o:o + D])
                    last.then_inc(l1t_copied, 1)

            scale_piece(0)
            scale_piece(1)
            whole_piece(0)
            copy_gate_up(0)
            scale_piece(2)
            whole_piece(1)
            copy_gate_up(1)
            whole_piece(2)
            copy_down()
            act.wait_ge(l1t_done, 2 * DC + 3)
            act.copy(wdrow[:, :], bank(0)[:, 0:D]).then_inc(l1t_copied, 1)

            roots(2)

            nc.scalar.preload_act_table(ACT.Exp)

            def c_xcopy(k):
                act.wait_ge(c_tr, k.t + 1)
                act.copy(xT[:, 0, 0:D], bank(1 - k.p)[:, 0:D]).then_inc(c_trc, 1)

            def c_qcopy(k):
                act.wait_ge(c_q, k.t + 1)
                for s in range(4):
                    strip = slice(32 * s, 32 * s + 32)
                    last = act.copy(qzh[k.p][strip, s, :, :],
                                    bank(1 - k.p)[strip, 0:D].rearrange("p (c s) -> p c s", c=DC))
                last.then_inc(c_qc, 1)

            def c_exp(s):
                def step(k):
                    act.wait_ge(c_sm, k.t * 4 + (s + 1))
                    at_least(act, c_t, k.t * 4 + (s - 1))
                    for j in range(4):
                        last = act.activation(pr1[:, s % 2, j * P:(j + 1) * P],
                                              bank(4 + s)[:, j * P:(j + 1) * P], ACT.Exp,
                                              bias=nm1[:, s, j:j + 1])
                    last.then_inc(c_e, 1)
                return step

            def c_ptcopy(s):
                def step(k):
                    act.wait_ge(c_t, k.t * 4 + (s + 1))
                    act.copy(pTh[:, s % 2, :], bank(2 + s % 2)).then_inc(c_tc, 1)
                return step

            stages = []
            for s in range(4):
                stages.append(((s + 2) // 4, c_exp((s + 2) % 4)))
                stages.append(((s + 1) // 4, c_ptcopy((s + 1) % 4)))
                if s == 1:
                    stages.append((2, c_xcopy))
                if s == 2:
                    stages.append((2, c_qcopy))
            steps(act, T, stages)

            roots(3)

            nc.scalar.preload_act_table(ACT.Silu)

            act.wait_ge(d_rs, 1)

            def z_norm(b):
                for i in range(QT // 2, QT):
                    t = b * QT + i
                    last = act.activation(z[:, t, :], xs[:, t, :], ACT.Identity,
                                          bias=neg_mr[:, bass.ts(t, 1)], scale=rstd[:, bass.ts(t, 1)])
                last.then_inc(d_za, 1)

            each(act, NB, z_norm)

            def z_tcopy(k):
                act.wait_ge(d_tr, k.t + 1)
                act.copy(zqT[:, :, bass.ts(k.t, BLK)],
                         bank(6 + k.p).bitcast(bf16).rearrange("p (c s) -> p c s", c=DC)).then_inc(d_trc, 1)

            steps(act, NB - 1, [(0, z_tcopy)])

            def gate_silu(b, chunks=range(IC)):
                for c in chunks:
                    r = IROWS[c]
                    act.wait_ge(g_p, b * IC + (c + 1))
                    at_least(act, g_h, b * IC + (c - 1))
                    act.activation(sil_g[0:r, c % 2, :], ps[0:r, 2 * (c % 3), :], ACT.Silu,
                                   scale=gu[0:r, 0, c:c + 1]).then_inc(g_s, 1)

            gate_silu(0, range(EARLY))
            z_tcopy(LAST)
            gate_silu(0, range(EARLY, IC))
            with act.Fori(1, NB) as b:
                gate_silu(b)
            act.wait_ge(e_sc, 1)

            def hidden_scale(b):
                for c in range(IC):
                    r = IROWS[c]
                    at_least(act, e_c, b * IC + (c - IC + 1))
                    act.activation(hqa[0:r, c, :], hs[0:r, c, bass.ts(b, BLK)], ACT.Copy,
                                   bias=MAGIC, scale=am[0:r, 7:8]).then_inc(e_a, 1)

            each(act, NB, hidden_scale)

        @block.vector
        def _(dve):
            chain = [0]

            def link(ins):
                chain[0] += 1
                ins.then_inc(dchain, 1)
                dve.wait_ge(dchain, chain[0])

            ts, tt, stt = nc.vector.tensor_scalar, nc.vector.tensor_tensor, nc.vector.scalar_tensor_tensor

            def rstds(n, sem_name, count):
                dve.wait_ge(sem_name, count)
                me, mo, ve, vo = stat[:, :, 1], stat[:, :, 4], stat[:, :, 2], stat[:, :, 5]
                tt(ln_a, me, mo, ALU.add)
                tt(ln_b, me, mo, ALU.subtract)
                link(tt(ln_c, ve, vo, ALU.add))
                ts(mean, ln_a, 0.5, None, ALU.mult)
                link(tt(root, ln_b, ln_b, ALU.mult))
                link(ts(ln_b, ln_c, 1.0 / D, EPS, ALU.mult, ALU.add))
                stt(var_eps, root, 0.25, ln_b, ALU.mult, ALU.add).then_inc(ln_ve, 1)
                dve.wait_ge(ln_root, n + 1)
                link(nc.vector.reciprocal(rstd, root))
                link(tt(ln_a, rstd, rstd, ALU.mult))
                link(tt(ln_b, ln_a, var_eps, ALU.mult))
                link(ts(ln_c, ln_b, -0.5, 1.5, ALU.mult, ALU.add))
                link(tt(rstd, rstd, ln_c, ALU.mult))

            def normalise(dst, k):
                return ts(dst, xs[:, k.t, :], mean[:, cols1(k.t)], rstd[:, cols1(k.t)],
                          ALU.subtract, ALU.mult)

            def cols1(t):
                return bass.ts(t, 1)

            for t in range(T):
                if t % (T // 4) == 0:
                    dve.wait_ge(x_loaded[t // (T // 4)], 16)
                nc.vector.bn_stats(stat[:, t, :], xs[:, t, :]).then_inc(st0, 1)
            dve.wait_ge(const_ready, 1)
            dve.wait_ge(folded, 1)
            stt(bdqs[:, :], bank(1)[:, 0:P], SCALE1, blocks[:, :], ALU.mult, ALU.mult)
            nc.vector.tensor_reduce(parity[:, :],
                                    blocks[:, :].rearrange("p (g a e) -> p a g e", a=2, e=DH)[:, :, :, 0],
                                    axis=AX.X, op=ALU.max)
            rstds(0, st0, T)

            def a_norm(k):
                at_least(dve, a_tr, k.t - 1)
                normalise(xn[:, k.p, :], k).then_inc(a_xn, 1)

            def a_mask(k):
                dve.wait_ge(a_s, k.t + 1)
                stt(sc[:, k.p, :], bank(6 + k.p)[:, D:D + P], SCALE0, causal[:, :], ALU.mult,
                    ALU.add).then_inc(a_lk, 1)
                dve.wait_ge(a_lk, k.t + 1)
                nc.vector.tensor_reduce(nmax[:, k.p:k.p + 1], sc[:, k.p, :], axis=AX.X, op=ALU.max,
                                        negate=True).then_inc(a_sm, 1)

            def a_v_low(k):
                dve.wait_ge(a_vc, k.t + 1)
                tt(v1l[:, k.t, :, 0:DH], bank(4 + k.p)[:, D:2 * D].rearrange("p (h e) -> p h e", e=DH),
                   v1h[:, k.t, :, 0:DH], ALU.subtract).then_inc(a_vl, 1)

            def a_finish(k):
                dve.wait_ge(a_o, k.t + 1)
                nc.vector.reciprocal(prcp[:, k.p:k.p + 1], psum_row[:, k.p:k.p + 1]).then_inc(a_f1, 1)
                dve.wait_ge(a_f1, k.t + 1)
                stt(xs[:, k.t, :], bank(1)[:, 0:D], prcp[:, k.p:k.p + 1], xs[:, k.t, :],
                    ALU.mult, ALU.add).then_inc(a_f2, 1)
                dve.wait_ge(a_f2, k.t + 1)
                nc.vector.bn_stats(stat[:, k.t, :], xs[:, k.t, :]).then_inc(a_fin, 1)

            def weights_low(k):
                dve.wait_ge(w_hi, k.t + 1)
                stt(w_low[:, k.t, :], raw[:, k.p, :], WS, w_high[:, k.t, :], ALU.mult,
                    ALU.subtract).then_inc(w_lo, 1)

            steps(dve, T, [(4, a_norm), (0, a_finish), (2, a_v_low), (2, a_mask), (2, weights_low)])
            rstds(1, a_fin, T)

            def b_norm(k):
                at_least(dve, b_tr, k.t - 1)
                at_least(dve, b_lo, k.t - 1)
                normalise(xn[:, k.p, :], k).then_inc(b_xn, 1)

            def b_route(k):
                dve.wait_ge(b_r, k.t + 1)
                nc.vector.tensor_copy(rsc[:, k.t, :], bank(2 + k.p)[:, 0:E]).then_inc(b_rc, 1)

            def b_low(k):
                dve.wait_ge(b_hi, k.t + 1)
                tt(rows[:, k.t, D:2 * D], xn[:, k.p, :], rows[:, k.t, 0:D], ALU.subtract).then_inc(b_lo, 1)

            steps(dve, T, [(3, b_norm), (2, b_low), (0, b_route)])

            def wide(v):
                return v.unsqueeze(2).to_broadcast([P, T, E])

            dve.wait_ge(b_rc, T)
            top1, top2, e21, d21 = rs[:, 0, :], rs[:, 1, :], rs[:, 2, :], rs[:, 3, :]
            pick, den, p1, p2 = rs[:, 4, :], rs[:, 5, :], rs[:, 6, :], rs[:, 7, :]
            hit, one1, one2, rest = rt[:, 0, :, :], rt[:, 1, :, :], rt[:, 2, :, :], rt[:, 3, :, :]

            def first_of(scores_ap, top, one):
                link(nc.vector.tensor_reduce(top, scores_ap, axis=AX.X, op=ALU.max))
                link(tt(hit, scores_ap, wide(top), ALU.is_equal))
                link(tt(hit, hit, key8[:, :, :], ALU.mult))
                link(nc.vector.tensor_reduce(pick, hit, axis=AX.X, op=ALU.max))
                link(tt(one, key8[:, :, :], wide(pick), ALU.is_equal))

            first_of(rsc[:, :, :], top1, one1)
            link(stt(rest, one1, NEG, rsc[:, :, :], ALU.mult, ALU.add))
            first_of(rest, top2, one2)
            tt(d21, top2, top1, ALU.subtract).then_inc(r_d, 1)
            chosen = rt[:, 4, :, :]
            tt(chosen, one1, one2, ALU.add).then_inc(r_one, 1)
            dve.wait_ge(r_e, 1)
            link(ts(den, e21, 1.0, None, ALU.add))
            link(nc.vector.reciprocal(p1, den))
            link(tt(p2, p1, e21, ALU.mult))

            def running(a, b, width, axis_slice):
                shift = 1
                while shift < width:
                    nc.vector.tensor_copy(axis_slice(b, 0, shift), axis_slice(a, 0, shift))
                    link(tt(axis_slice(b, shift, width), axis_slice(a, shift, width),
                            axis_slice(a, 0, width - shift), ALU.add))
                    a, b = b, a
                    shift *= 2
                return a, b

            dve.wait_ge(r_rank, 1)
            rank = bank(4)[:, 0:T * E].rearrange("p (t e) -> p t e", e=E)
            count = bank(4)[:, T * E:2 * T * E].rearrange("p (t e) -> p t e", e=E)
            place = rt[:, 7, :, :]
            link(nc.vector.tensor_copy(rt[:, 5, :, :], count))
            upto, _ = running(rt[:, 5, :, :], rt[:, 6, :, :], T, lambda v, a, b: v[:, a:b, :])
            link(tt(place, upto, count, ALU.subtract))
            link(tt(place, place, rank, ALU.add))
            need, ends = routed[:, 0, :], routed[:, 1, :]
            link(ts(need, upto[:, T - 1, :], 1.0 / P, 0.5 - 0.5 / P, ALU.mult, ALU.add))
            link(ts(need, need, MAGIC, None, ALU.add))
            link(ts(need, need, -MAGIC, None, ALU.add))
            link(nc.vector.tensor_copy(ends, need))
            ends, spare = running(ends, routed[:, 2, :], E, lambda v, a, b: v[:, a:b])
            link(tt(spare, ends, need, ALU.subtract))
            first = routed[:, 3, :]
            link(ts(first, spare, float(P), None, ALU.mult))
            link(tt(place, place, first.unsqueeze(1).to_broadcast([P, T, E]), ALU.add))
            slot_f = rt[:, 5, :, :].rearrange("p t e -> p (t e)")[:, 0:T * TOPK].rearrange(
                "p (t j) -> p t j", j=TOPK)
            for j, one in enumerate((one1, one2)):
                link(tt(hit, place, one, ALU.mult))
                link(nc.vector.tensor_reduce(slot_f[:, :, j], hit, axis=AX.X, op=ALU.add))
            link(nc.vector.tensor_copy(slot_i[:, :, :], slot_f))
            at_tile = rt[:, 0, :, :].rearrange("p t e -> p (t e)")[:, 0:T * TOPK]
            at_place = rt[:, 1, :, :].rearrange("p t e -> p (t e)")[:, 0:T * TOPK]
            slots = slot_f.rearrange("p t j -> p (t j)")
            link(ts(at_tile, slots, 1.0 / P, 0.5 / P - 0.5, ALU.mult, ALU.add))
            link(ts(at_tile, at_tile, MAGIC, None, ALU.add))
            link(ts(at_tile, at_tile, -MAGIC, None, ALU.add))
            link(stt(at_place, at_tile, -float(P), slots, ALU.mult, ALU.add))
            past = rt[:, 5:8, :, :].rearrange("p a t e -> p (a t e)")[:, 0:NT * E].rearrange(
                "p (n e) -> p n e", e=E)
            link(tt(past, tile_no[:, :].unsqueeze(2).to_broadcast([P, NT, E]),
                    ends.unsqueeze(1).to_broadcast([P, NT, E]), ALU.is_ge))
            owner = rt[:, 4, :, :].rearrange("p t e -> p (t e)")[:, 0:NT]
            link(nc.vector.tensor_reduce(owner, past, axis=AX.X, op=ALU.add))
            ts(tile_e[:, :], owner, float(E - 1), None, ALU.min).then_inc(r_slot, 1)
            link(nc.vector.tensor_copy(at_place_h, at_place))
            group = 4 * TOPK
            for g in range(T * TOPK // group):
                some = slice(g * group, (g + 1) * group)
                link(tt(tile_hot[:, some, :], tile_no[:, :].unsqueeze(1).to_broadcast([P, group, NT]),
                        at_tile[:, some].unsqueeze(2).to_broadcast([P, group, NT]), ALU.is_equal))
                tt(place_hot[:, some, :], place_no[:, :].unsqueeze(1).to_broadcast([P, group, P]),
                   at_place_h[:, some].unsqueeze(2).to_broadcast([P, group, P]), ALU.is_equal)
                hot = tile_hot[:, some, :].rearrange("p (t j) n -> p t (j n)", j=TOPK)
                tt(hot, hot, token[:, g * 4:(g + 1) * 4].unsqueeze(2).to_broadcast([P, 4, TOPK * NT]),
                   ALU.mult).then_inc(r_hot, 1)
            dve.wait_ge(r_at, 1)
            nc.vector.tensor_copy(source_i[:, :], bank(5)[:, 0:NT]).then_inc(r_source, 1)
            dve.wait_ge(r_source, 1)
            dve.wait_ge(kept, 16 * T)

            def hidden(k):
                dve.wait_ge(m_s, k.t + 1)
                stt(hid[:, k.p, :], bank(2 + 2 * k.p), 1.0 / WS, sil[:, k.p, :], ALU.mult,
                    ALU.mult).then_inc(m_h, 1)

            def low(k):
                dve.wait_ge(m_hh, k.t + 1)
                tt(hTl[:, k.p, :], hid[:, k.p, :], hTh[:, k.p, :], ALU.subtract).then_inc(m_hl, 1)

            def back(k):
                dve.wait_ge(m_y, k.t + 1)
                at_least(dve, m_back[k.p], k.half * 16)
                ts(y_out[:, k.p, :], bank(6 + k.p)[:, 0:D], 1.0 / WS, None, ALU.mult).then_inc(m_yc, 1)

            def fetch_up(k):
                e = dve.value_load(tile_e[0:1, bass.ts(k.t, 1)], min_val=0, max_val=E - 1)
                at_least(dve, m_u, k.t - 1)
                nc.vector.tensor_copy(w12_now[k.p][0], w12_of(w_high, e))
                nc.vector.tensor_copy(w12_now[k.p][1], w12_of(w_low, e)).then_inc(m_w12, 1)

            def fetch_down(k):
                e = dve.value_load(tile_e[0:1, bass.ts(k.t, 1)], min_val=0, max_val=E - 1)
                at_least(dve, m_y, k.t - 1)
                nc.vector.tensor_copy(w3_now[k.p][0], w3_of(w_high, e))
                nc.vector.tensor_copy(w3_now[k.p][1], w3_of(w_low, e)).then_inc(m_w3, 1)

            steps(dve, NT, [(2, fetch_up), (1, hidden), (1, fetch_down), (1, low), (0, back)])

            def scales_piece(n):
                dve.wait_ge(l1w_in[n], 16 * (2 if n < 2 else 1))
                for src, _, r, c in pieces[n]:
                    last = nc.vector.tensor_reduce(wmax[0:r, c:c + 1], src, axis=AX.X, op=ALU.max,
                                                   apply_absolute_value=True)
                link(last)
                some = slice(pieces[n][0][3], pieces[n][-1][3] + 1)
                link(ts(wsc[:, some], wmax[:, some], 1.0 / QMAX, None, ALU.mult))
                nc.vector.reciprocal(wrc[:, some], wsc[:, some]).then_inc(l1_scales, 1)
                if n == 2:
                    for c in range(DC):
                        last = ts(diag[:, c, :], ident[:, :], wsc[:, 2 * IC + c:2 * IC + c + 1], None,
                                  ALU.mult)
                    last.then_inc(l1_diag, 1)

            def clamp_piece(n):
                dve.wait_ge(l1_scaled, n + 1)
                for src, _, _, _ in pieces[n]:
                    last = ts(src, src, MAGIC + QMAX, MAGIC - QMAX - 1.0, ALU.min, ALU.max)
                last.then_inc(l1_clamped, 1)

            beside = {0: (scales_piece, 0), 1: (scales_piece, 1), 3: (clamp_piece, 0), 4: (scales_piece, 2),
                      6: (clamp_piece, 1), 8: (clamp_piece, 2)}
            dve.wait_ge(m_w3, NT)
            for q in qzh + qzl:
                last = nc.vector.memset(q.rearrange("p a c s -> p (a c s)"), 0.0)
            last.then_inc(c_zero, 1)
            link(nc.vector.memset(wmax[:, :], 1.0))
            for t in range(T):
                if t in beside:
                    part, n = beside[t]
                    part(n)
                p = t % YB
                dve.wait_ge(g_in[p], 32 * (t // YB + 1))
                stt(xs[:, t, :], y_in[:, p, 0, :], rs[:, 6, t:t + 1], xs[:, t, :], ALU.mult,
                    ALU.add).then_inc(g_one, 1)
                dve.wait_ge(g_one, t + 1)
                stt(xs[:, t, :], y_in[:, p, 1, :], rs[:, 7, t:t + 1], xs[:, t, :], ALU.mult,
                    ALU.add).then_inc(g_two, 1)
                dve.wait_ge(g_two, t + 1)
                nc.vector.bn_stats(stat[:, t, :], xs[:, t, :]).then_inc(st2, 1)
            rstds(2, st2, T)
            nc.vector.memset(rc1[:, :], 0.0).then_inc(st_done, 1)

            dve.wait_ge(c_zero, 1)

            def c_norm(k):
                at_least(dve, c_tr, k.t)
                normalise(xn[:, 0, :], k).then_inc(c_xn, 1)

            def c_maxima(s):
                def step(k):
                    b4 = bank(4 + s).rearrange("p (h s) -> p h s", h=4)
                    dve.wait_ge(c_s, k.t * 4 + (s + 1))
                    at_least(dve, c_e, k.t * 4 + (s - 3))
                    nc.vector.tensor_reduce(nm1[:, s, :], b4, axis=AX.X, op=ALU.max,
                                            negate=True).then_inc(c_sm, 1)
                return step

            def c_low(s):
                def step(k):
                    dve.wait_ge(c_tc, k.t * 4 + (s + 1))
                    tt(pTl[:, s % 2, :], bank(2 + s % 2), pTh[:, s % 2, :], ALU.subtract).then_inc(c_tl, 1)
                return step

            def c_qlow(k):
                dve.wait_ge(c_qc, k.t + 1)
                for s in range(4):
                    strip = slice(32 * s, 32 * s + 32)
                    last = tt(qzl[k.p][strip, s, :, :],
                              bank(1 - k.p)[strip, 0:D].rearrange("p (c s) -> p c s", c=DC),
                              qzh[k.p][strip, s, :, :], ALU.subtract)
                last.then_inc(c_ql, 1)

            def c_output(k):
                dve.wait_ge(c_v, k.t * 4 + 4)
                o = bank(k.p)[:, 0:NH * (DH + 1)].rearrange("p (h e) -> p h e", e=DH + 1)
                nc.vector.reciprocal(rc1[:, :], o[:, :, DH]).then_inc(c_f1, 1)
                dve.wait_ge(c_f1, k.t + 1)
                at_least(dve, c_f3, k.t - 1)
                tt(o1[:, k.p, :, :], o[:, :, 0:DH], rc1[:, :].unsqueeze(2).to_broadcast([P, NH, DH]),
                   ALU.mult).then_inc(c_f2, 1)

            def c_stats(k):
                dve.wait_ge(c_f3, k.t + 1)
                nc.vector.bn_stats(stat[:, k.t, :], xs[:, k.t, :]).then_inc(c_fin, 1)

            stages = []
            for s in range(4):
                stages.append((1, c_low(s)))
                if s == 0:
                    stages.append((0, c_output))
                stages.append((1 + (s + 3) // 4, c_maxima((s + 3) % 4)))
                if s == 1:
                    stages.append((0, c_stats))
                if s == 2:
                    stages.append((4, c_norm))
                if s == 3:
                    stages.append((3, c_qlow))
            steps(dve, T, stages)
            rstds(3, c_fin, T)

            dve.wait_ge(sig_exp, 1)
            link(ts(sig[:, 1, :], sig[:, 0, :], 1.0, None, ALU.add))
            link(nc.vector.reciprocal(sig[:, 2, :], sig[:, 1, :]))

            stt(neg_mr, mean, -1.0, rstd, ALU.mult, ALU.mult).then_inc(d_rs, 1)

            def z_norm(b):
                for i in range(QT // 2):
                    t = b * QT + i
                    last = ts(z[:, t, :], xs[:, t, :], mean[:, cols1(t)], rstd[:, cols1(t)], ALU.subtract,
                              ALU.mult)
                last.then_inc(d_z, 1)

            def z_maxima(b):
                dve.wait_ge(d_z, b + 1)
                dve.wait_ge(d_za, b + 1)
                nc.vector.tensor_reduce(zam[:, bass.ts(b, QT)], z[:, bass.ts(b, QT), :], axis=AX.X, op=ALU.max,
                                        apply_absolute_value=True).then_inc(d_lk, 1)

            z_norm(0)
            with dve.Fori(0, NB - 1) as b:
                z_norm(b + 1)
                z_maxima(b)
            z_maxima(NB - 1)
            dve.wait_ge(d_lk, NB)
            nc.vector.tensor_reduce(am[:, 0:1], zam[:, :], axis=AX.X, op=ALU.max).then_inc(d_am, 1)
            dve.wait_ge(d_amr, 1)
            link(ts(am[:, 2:3], am[:, 1:2], sig[:, 2, 0:1], 1.0 / QMAX, ALU.mult, ALU.mult))
            link(nc.vector.reciprocal(am[:, 3:4], am[:, 2:3]))
            link(ts(gu[:, :, :].rearrange("p w c -> p (w c)"), wsc[:, 0:2 * IC], am[:, 2:3], None, ALU.mult))

            def z_quant(k):
                zk = z[:, bass.ts(k.t, QT), :].rearrange("p t d -> p (t d)")
                at_least(dve, d_q, k.t - 1)
                ts(zqa[:, k.p, :], zk, am[:, 3:4], MAGIC, ALU.mult, ALU.add).then_inc(d_sc, 1)
                dve.wait_ge(d_sc, k.t + 1)
                at_least(dve, d_qb, k.t - 1)
                ts(zqi[:, k.p, :], zqa[:, k.p, :], MAGIC + QMAX, MAGIC, ALU.min, ALU.subtract).then_inc(d_q, 1)
                dve.wait_ge(d_q, k.t + 1)
                at_least(dve, d_tr, k.t - 1)
                ts(zqb[:, k.p, :, :].rearrange("p t d -> p (t d)"), zqi[:, k.p, :], -QMAX - 1.0, None,
                   ALU.max).then_inc(d_qb, 1)

            steps(dve, NB, [(0, z_quant)])

            def g_maxima(b, c):
                r = IROWS[c]
                dve.wait_ge(g_h, b * IC + (c + 1))
                nc.vector.tensor_reduce(ham[0:r, c, bass.ts(b, 1)], hs[0:r, c, bass.ts(b, BLK)],
                                        axis=AX.X, op=ALU.max, apply_absolute_value=True).then_inc(g_am, 1)

            with dve.Fori(0, NB) as b:
                for c in range(IC):
                    r = IROWS[c]
                    dve.wait_ge(g_s, b * IC + (c + 1))
                    stt(hs[0:r, c, bass.ts(b, BLK)], ps[0:r, 2 * (c % 3) + 1, :], gu[0:r, 1, c:c + 1],
                        sil_g[0:r, c % 2, :], ALU.mult, ALU.mult).then_inc(g_h, 1)
                    if c > 0:
                        g_maxima(b, c - 1)
                g_maxima(b, IC - 1)
            dve.wait_ge(g_am, NB * IC)
            link(nc.vector.memset(zam[:, IC - 1:IC], 0.0))
            nc.vector.tensor_reduce(zam[:, 0:IC - 1], ham[:, 0:IC - 1, :], axis=AX.X, op=ALU.max)
            link(nc.vector.tensor_reduce(zam[0:IROWS[-1], IC - 1:IC], ham[0:IROWS[-1], IC - 1, :],
                                         axis=AX.X, op=ALU.max))
            nc.vector.tensor_reduce(am[:, 4:5], zam[:, 0:IC], axis=AX.X, op=ALU.max).then_inc(e_am, 1)
            dve.wait_ge(e_amr, 1)
            link(ts(am[:, 6:7], am[:, 5:6], sig[:, 2, 1:2], 1.0 / QMAX, ALU.mult, ALU.mult))
            nc.vector.reciprocal(am[:, 7:8], am[:, 6:7]).then_inc(e_sc, 1)
            link(ts(cdrow[:, :], wdrow[:, :], am[:, 6:7], None, ALU.mult))

            def last_quant(k):
                for c in range(IC + 1):
                    if c < IC:
                        r, n = IROWS[c], k.t * IC + c
                        dve.wait_ge(e_a, n + 1)
                        at_least(dve, e_q, n - 1)
                        ts(hqi[0:r, c % 2, :], hqa[0:r, c, :], MAGIC + QMAX, MAGIC, ALU.min,
                           ALU.subtract).then_inc(e_c, 1)
                    if c > 0:
                        r, n = IROWS[c - 1], k.t * IC + (c - 1)
                        dve.wait_ge(e_c, n + 1)
                        if c == 1:
                            at_least(dve, e_y, (k.t - 1) * QT)
                        ts(hq[k.p][0:r, c - 1, :], hqi[0:r, (c - 1) % 2, :], -QMAX - 1.0, None,
                           ALU.max).then_inc(e_q, 1)

            def scaled(k):
                for j in range(QT):
                    dve.wait_ge(e_y, k.t * QT + (j + 1))
                    at_least(dve, e_out[j], k.t * 16)
                    tt(oo[:, j, :], bank(4 + j)[:, 0:D], cdrow[:, :], ALU.mult).then_inc(e_f, 1)

            steps(dve, NB, [(1, last_quant), (0, scaled)])


def kernel(**inputs):
    import numpy as _np
    import concourse.bacc as _bacc
    from concourse import mybir as _mybir
    from concourse.bass_utils import run_bass_kernel_spmd as _run

    def blocks(w, n):
        d = w.shape[0]
        out = _np.zeros((n * d, n * d), w.dtype)
        for i in range(n):
            out[i * d:(i + 1) * d, i * d:(i + 1) * d] = w.T
        return out

    P = 128
    w12, w3 = _np.asarray(inputs['L0_ffn_w12']), _np.asarray(inputs['L0_ffn_w3'])
    E, H2, D = w12.shape
    up = w12.transpose(0, 2, 1).reshape(E, 2, P, H2)
    down = w3.transpose(0, 2, 1).reshape(E, 2, 2, P, D).transpose(0, 1, 3, 2, 4).reshape(E, 2, P, 2 * D)
    experts = _np.concatenate([up, down], axis=3).reshape(2 * E, P, H2 + 2 * D)
    heads = P // inputs['L1_xattn_Wk'].shape[0]
    laid = {
        'x': inputs['x'],
        'ctxT': _np.transpose(inputs['ctx_1024'], (0, 2, 1)),
        'wq0T': _np.transpose(inputs['L0_xattn_w_q']),
        'wk0T': _np.transpose(inputs['L0_xattn_w_k']),
        'wv0': inputs['L0_xattn_w_v'],
        'experts': experts,
        'gate_wT': _np.transpose(inputs['L0_ffn_gate_w']),
        'wk1': _np.tile(inputs['L1_xattn_Wk'], (1, heads)),
        'wq1': _np.tile(inputs['L1_xattn_Wq'], (1, heads)),
        'wv1_blocks': blocks(_np.asarray(inputs['L1_xattn_Wv']), heads),
        'clip_x': inputs['L1_ffn_clip_x'],
        'clip_down': inputs['L1_ffn_clip_down'],
        'w_gate': inputs['L1_ffn_w_gate'],
        'w_up': inputs['L1_ffn_w_up'],
        'w_down': inputs['L1_ffn_w_down'],
    }

    nc = _bacc.Bacc("TRN2", target_bir_lowering=False, num_devices=1)
    arrays, args = {}, []
    for name, value in laid.items():
        a = _np.ascontiguousarray(value)
        arrays[f"in_{name}"] = a
        args.append(nc.dram_tensor(f"in_{name}", a.shape, _mybir.dt.from_np(a.dtype), kind="ExternalInput").ap())
    shape = inputs['x'].shape
    res = nc.dram_tensor("out_x", shape, _mybir.dt.float32, kind="ExternalOutput").ap()
    block_program(nc, *args, res)
    r = _run(nc, [arrays], core_ids=[0])
    return r.results[0]["out_x"]
```
